# Optimizing a Trainium2 kernel written in Bass

```python
import numpy as np
import jax
import jax.numpy as jnp

def _softmax(x, axis=-1):
    return jax.nn.softmax(x, axis=axis)

def _gelu(x):
    return jax.nn.gelu(x, approximate=True)

def _silu(x):
    return jax.nn.silu(x)

def _sigmoid(x):
    return jax.nn.sigmoid(x)

def _layernorm(x, axis=-1, eps=1e-05):
    m = jnp.mean(x, axis=axis, keepdims=True)
    v = jnp.var(x, axis=axis, keepdims=True)
    return (x - m) / jnp.sqrt(v + eps)

def _scatter_add(tgt, idx, src, axis=0):
    return tgt.at[idx].add(src)

def _segment_sum(src, seg, n):
    return jax.ops.segment_sum(src, seg, n)
kernel_name = 'mk_gps_d1_gnn_r8_e36039'

def setup_inputs(seed: int=0):
    np.random.seed(seed)
    _w = jnp.asarray

    def _rec_inputs():
        import jax
        import jax.numpy as jnp
        _gk = jax.random.key(seed)
        x = -0.0003713 + 1 * jax.random.normal(jax.random.fold_in(_gk, 1), (6250, 256), jnp.float32)
        src = jax.random.randint(jax.random.fold_in(_gk, 2), (100000,), 0, 6250, jnp.int32)
        dst = jnp.minimum((6250 * jax.random.uniform(jax.random.fold_in(_gk, 3), (100000,)) ** 2.0).astype(jnp.int32), 49999)
        _o = jnp.argsort(dst, stable=True)
        src = src[_o]
        dst = dst[_o]
        edge_attr_128 = 9.41057e-06 + 1 * jax.random.normal(jax.random.fold_in(_gk, 11), (100000, 128), jnp.float32)
        node_vec1 = jax.random.uniform(jax.random.fold_in(_gk, 13), (6250, 1), jnp.float32, 0.0, 0.999973)
        node_vec1_n2 = jax.random.uniform(jax.random.fold_in(_gk, 14), (6250, 1), jnp.float32, 0.0, 0.999973)
        return (x, src, dst, edge_attr_128, node_vec1, node_vec1_n2)
    x, src, dst, edge_attr_128, node_vec1, node_vec1_n2 = _rec_inputs()

    def _L0_gnn_setup():
        import jax, jax.numpy as jnp
        import numpy as np
        NUM_NODES = 6250
        NUM_EDGES = 200000
        NODE_DIM = 256
        EDGE_DIM = 128
        MAX_IN_DEGREE = 512
        MAX_OUT_DEGREE = 512
        key = jax.random.key(seed)
        ks = jax.random.split(key, 12)
        x = jax.random.normal(ks[0], (NUM_NODES, NODE_DIM), dtype=jnp.float32)
        edge_index = jax.random.randint(ks[1], (2, NUM_EDGES), 0, NUM_NODES, dtype=jnp.int64 if jax.config.read('jax_enable_x64') else jnp.int32)
        edge_attr = jax.random.normal(ks[2], (NUM_EDGES, EDGE_DIM), dtype=jnp.float32)
        voronoi_values = jax.random.uniform(ks[3], (NUM_NODES, 1), dtype=jnp.float32)
        centralities = jax.random.uniform(ks[4], (NUM_NODES, 1), dtype=jnp.float32)
        z_in = jax.random.normal(ks[5], (MAX_IN_DEGREE, NODE_DIM), dtype=jnp.float32)
        z_out = jax.random.normal(ks[6], (MAX_OUT_DEGREE, NODE_DIM), dtype=jnp.float32)
        W_cent = jax.random.normal(ks[7], (1, NODE_DIM), dtype=jnp.float32) * 0.5
        b_cent = jnp.zeros((NODE_DIM,), dtype=jnp.float32)
        W_vor = jax.random.normal(ks[8], (1, NODE_DIM), dtype=jnp.float32) * 0.5
        b_vor = jnp.zeros((NODE_DIM,), dtype=jnp.float32)
        W_sum = jax.random.normal(ks[9], (EDGE_DIM, NODE_DIM), dtype=jnp.float32) * (1.0 / np.sqrt(EDGE_DIM))
        b_sum = jnp.zeros((NODE_DIM,), dtype=jnp.float32)
        return {'x': x, 'edge_index': edge_index, 'edge_attr': edge_attr, 'voronoi_values': voronoi_values, 'centralities': centralities, 'z_in': z_in, 'z_out': z_out, 'W_cent': W_cent, 'b_cent': b_cent, 'W_vor': W_vor, 'b_vor': b_vor, 'W_sum': W_sum, 'b_sum': b_sum}
    _L0_gnn_all = _L0_gnn_setup()
    _L0_gnn_in = {k: v for k, v in _L0_gnn_all.items() if k in ('z_in', 'z_out', 'W_cent', 'b_cent', 'W_vor', 'b_vor', 'W_sum', 'b_sum')}
    del _L0_gnn_all

    def _L0_mix_setup():
        import jax, jax.numpy as jnp
        import numpy as np
        HEADS = 8
        DIM_HEAD = 64
        EPS = 1e-05

        def _inst_norm(t):
            mu = jnp.mean(t, axis=-1, keepdims=True)
            var = jnp.var(t, axis=-1, keepdims=True)
            return (t - mu) / jnp.sqrt(var + EPS)
        key = jax.random.key(seed)
        k1, k2, k3, k4 = jax.random.split(key, 4)
        b, n, dim = (4, 1024, 256)
        inner = HEADS * DIM_HEAD
        x = jax.random.normal(k1, (b, n, dim), dtype=jnp.float32)
        w_qkv = jax.random.normal(k2, (dim, 3 * inner), dtype=jnp.float32) * (1.0 / DIM_HEAD)
        w_out = jax.random.normal(k3, (inner, dim), dtype=jnp.float32) * dim ** (-0.5)
        b_out = jax.random.normal(k4, (dim,), dtype=jnp.float32) * 0.01
        return {'x': x, 'w_qkv': w_qkv, 'w_out': w_out, 'b_out': b_out}
    _L0_mix_all = _L0_mix_setup()
    _L0_mix_in = {k: v for k, v in _L0_mix_all.items() if k in ('w_qkv', 'w_out', 'b_out')}
    del _L0_mix_all

    def _L0_ffn_setup():
        import jax, jax.numpy as jnp
        import numpy as np
        TOP_K = 2
        LN_EPS = 1e-05
        key = jax.random.key(seed)
        ks = jax.random.split(key, 8)
        B, S, D, E, H = (16, 1024, 256, 8, 1024)
        x = jax.random.normal(ks[0], (B, S, D), dtype=jnp.float32)
        Wr = jax.random.normal(ks[1], (D, E), dtype=jnp.float32) * 0.1
        br = jnp.zeros((E,), dtype=jnp.float32)
        ln_g = jnp.ones((E, D), dtype=jnp.float32)
        ln_b = jnp.zeros((E, D), dtype=jnp.float32)
        W1 = jax.random.normal(ks[2], (E, D, H), dtype=jnp.float32) * (1.0 / np.sqrt(D))
        b1 = jnp.zeros((E, H), dtype=jnp.float32)
        W2 = jax.random.normal(ks[3], (E, H, D), dtype=jnp.float32) * (1.0 / np.sqrt(H))
        b2 = jnp.zeros((E, D), dtype=jnp.float32)
        return {'x': x, 'Wr': Wr, 'br': br, 'ln_g': ln_g, 'ln_b': ln_b, 'W1': W1, 'b1': b1, 'W2': W2, 'b2': b2}
    _L0_ffn_all = _L0_ffn_setup()
    _L0_ffn_in = {k: v for k, v in _L0_ffn_all.items() if k in ('Wr', 'br', 'ln_g', 'ln_b', 'W1', 'b1', 'W2', 'b2')}
    del _L0_ffn_all
    return {'x': x, 'src': src, 'dst': dst, 'edge_attr_128': edge_attr_128, 'node_vec1': node_vec1, 'node_vec1_n2': node_vec1_n2, 'L0_gnn_z_in': _L0_gnn_in['z_in'], 'L0_gnn_z_out': _L0_gnn_in['z_out'], 'L0_gnn_W_cent': _L0_gnn_in['W_cent'], 'L0_gnn_b_cent': _L0_gnn_in['b_cent'], 'L0_gnn_W_vor': _L0_gnn_in['W_vor'], 'L0_gnn_b_vor': _L0_gnn_in['b_vor'], 'L0_gnn_W_sum': _L0_gnn_in['W_sum'], 'L0_gnn_b_sum': _L0_gnn_in['b_sum'], 'L0_mix_w_qkv': _L0_mix_in['w_qkv'], 'L0_mix_w_out': _L0_mix_in['w_out'], 'L0_mix_b_out': _L0_mix_in['b_out'], 'L0_ffn_Wr': _L0_ffn_in['Wr'], 'L0_ffn_br': _L0_ffn_in['br'], 'L0_ffn_ln_g': _L0_ffn_in['ln_g'], 'L0_ffn_ln_b': _L0_ffn_in['ln_b'], 'L0_ffn_W1': _L0_ffn_in['W1'], 'L0_ffn_b1': _L0_ffn_in['b1'], 'L0_ffn_W2': _L0_ffn_in['W2'], 'L0_ffn_b2': _L0_ffn_in['b2']}

def reference(x, src, dst, edge_attr_128, node_vec1, node_vec1_n2, L0_gnn_z_in, L0_gnn_z_out, L0_gnn_W_cent, L0_gnn_b_cent, L0_gnn_W_vor, L0_gnn_b_vor, L0_gnn_W_sum, L0_gnn_b_sum, L0_mix_w_qkv, L0_mix_w_out, L0_mix_b_out, L0_ffn_Wr, L0_ffn_br, L0_ffn_ln_g, L0_ffn_ln_b, L0_ffn_W1, L0_ffn_b1, L0_ffn_W2, L0_ffn_b2):
    import jax
    import jax.numpy as jnp

    def _L0_gnn_ref(x, edge_index, edge_attr, voronoi_values, centralities, z_in, z_out, W_cent, b_cent, W_vor, b_vor, W_sum, b_sum):
        import jax, jax.numpy as jnp
        import numpy as np
        NUM_NODES = 6250
        NUM_EDGES = 200000
        NODE_DIM = 256
        EDGE_DIM = 128
        MAX_IN_DEGREE = 512
        MAX_OUT_DEGREE = 512
        num_nodes = x.shape[0]
        src = edge_index[0]
        dst = edge_index[1]
        ones = jnp.ones_like(src, dtype=jnp.int32)
        in_deg = jnp.minimum(jax.ops.segment_sum(ones, dst, num_segments=num_nodes), MAX_IN_DEGREE - 1)
        out_deg = jnp.minimum(jax.ops.segment_sum(ones, src, num_segments=num_nodes), MAX_OUT_DEGREE - 1)
        edge_proj = edge_attr @ W_sum + b_sum
        sum3d = jax.ops.segment_sum(edge_proj, src, num_segments=num_nodes)
        cent_term = jax.nn.sigmoid(centralities @ W_cent + b_cent)
        vor_term = jax.nn.sigmoid(voronoi_values @ W_vor + b_vor)
        return x + z_in[in_deg] + z_out[out_deg] + cent_term + vor_term + sum3d

    def _L0_mix_ref(x, w_qkv, w_out, b_out):
        import jax, jax.numpy as jnp
        import numpy as np
        HEADS = 8
        DIM_HEAD = 64
        EPS = 1e-05

        def _inst_norm(t):
            mu = jnp.mean(t, axis=-1, keepdims=True)
            var = jnp.var(t, axis=-1, keepdims=True)
            return (t - mu) / jnp.sqrt(var + EPS)
        b, n, dim = x.shape
        qkv = x @ w_qkv
        q, k, v = jnp.split(qkv, 3, axis=-1)
        to_heads = lambda t: t.reshape(b, n, HEADS, DIM_HEAD).transpose(0, 2, 1, 3)
        q, k, v = (to_heads(q), to_heads(k), to_heads(v))
        k = _inst_norm(k)
        v = _inst_norm(v)
        dots = jnp.einsum('bhnd,bhne->bhde', k, v)
        out = jnp.einsum('bhnd,bhde->bhne', q, dots) * (1.0 / n)
        out = out.transpose(0, 2, 1, 3).reshape(b, n, HEADS * DIM_HEAD)
        return out @ w_out + b_out

    def _L0_ffn_ref(x, Wr, br, ln_g, ln_b, W1, b1, W2, b2):
        import jax, jax.numpy as jnp
        import numpy as np
        TOP_K = 2
        LN_EPS = 1e-05
        B, S, D = x.shape
        N = B * S
        xt = x.reshape(N, D)
        logits = xt @ Wr + br
        probs = jax.nn.softmax(logits, axis=-1)
        top_p, top_idx = jax.lax.top_k(probs, TOP_K)
        weights = top_p / top_p.sum(axis=-1, keepdims=True)
        mu = xt.mean(axis=-1, keepdims=True)
        var = ((xt - mu) ** 2).mean(axis=-1, keepdims=True)
        xn = (xt - mu) * jax.lax.rsqrt(var + LN_EPS)
        xe = xn[None, :, :] * ln_g[:, None, :] + ln_b[:, None, :]
        h = jax.nn.gelu(jnp.einsum('end,edh->enh', xe, W1) + b1[:, None, :], approximate=False)
        y = jnp.einsum('enh,ehd->end', h, W2) + b2[:, None, :]
        y_tok = jnp.transpose(y, (1, 0, 2))
        sel = jnp.take_along_axis(y_tok, top_idx[:, :, None], axis=1)
        out = (weights[:, :, None] * sel).sum(axis=1)
        return out.reshape(B, S, D)
    edge_index = jnp.stack([src, dst])
    xn = _layernorm(x, axis=-1)
    x = x + _L0_gnn_ref(xn, edge_index, edge_attr_128, node_vec1, node_vec1_n2, L0_gnn_z_in, L0_gnn_z_out, L0_gnn_W_cent, L0_gnn_b_cent, L0_gnn_W_vor, L0_gnn_b_vor, L0_gnn_W_sum, L0_gnn_b_sum) + _L0_mix_ref(xn[None], L0_mix_w_qkv, L0_mix_w_out, L0_mix_b_out)[0]
    x = x + _L0_ffn_ref(_layernorm(x, axis=-1)[None], L0_ffn_Wr, L0_ffn_br, L0_ffn_ln_g, L0_ffn_ln_b, L0_ffn_W1, L0_ffn_b1, L0_ffn_W2, L0_ffn_b2)[0]
    return x

_drawn_inputs = setup_inputs


def setup_inputs(seed=0):
    import zlib

    import numpy as np

    out = dict(_drawn_inputs(seed))
    spreads = {'L0_gnn_b_cent': (0.0, 2.0),
     'L0_gnn_b_vor': (0.0, 2.0),
     'L0_gnn_b_sum': (0.0, 0.1),
     'L0_ffn_br': (0.0, 0.305),
     'L0_ffn_ln_g': (1.0, 0.6),
     'L0_ffn_ln_b': (0.0, 0.759),
     'L0_ffn_b1': (0.0, 0.752),
     'L0_ffn_b2': (0.0, 0.525)}
    factors = {'node_vec1': 7.095,
     'node_vec1_n2': 6.544,
     'L0_gnn_W_cent': 3.584,
     'L0_gnn_W_vor': 3.805,
     'L0_mix_b_out': 23.811}
    for name, (base, spread) in spreads.items():
        noise = np.random.default_rng([zlib.crc32(name.encode()), seed]).standard_normal(out[name].shape)
        drawn = base * np.exp(spread * noise) if base else spread * noise
        out[name] = jnp.asarray(drawn.astype(out[name].dtype))
    for name, factor in factors.items():
        out[name] = (out[name] * factor).astype(out[name].dtype)
    return out
```

```python
from contextlib import ExitStack

import numpy as np

import concourse.bass as bass
from concourse import mybir

F32, I32, BF16 = mybir.dt.float32, mybir.dt.int32, mybir.dt.bfloat16
ALU, ACT, AX = mybir.AluOpType, mybir.ActivationFunctionType, mybir.AxisListType

P = 128
NODES, DIM, EDGES, EDIM = 6250, 256, 100000, 128
KC = DIM // P
TILES = -(-NODES // P)
LAST = NODES - (TILES - 1) * P
HEADS, DH = 8, 64
INNER = HEADS * DH
PAIRS = INNER // P
EXPERTS, HID = 8, 1024
HC = HID // P
DEG = 512
EPS = 1e-5

ECOLS = EDGES // P
EREST = EDGES - ECOLS * P
ETILES = ECOLS + 1
GROUP = 3
GROUPS = -(-ETILES // GROUP)
LOAD = 6
XRING, SRING, ORING = 4, 3, 4
TABLES = 4
XW = EDIM + 2
RW = EDIM + 1
ROWS = (TILES + 1) * P
ZERO = 645
HB = 4

SLOT = 256
BLOCKS = 2 * NODES // SLOT + EXPERTS
STILES = BLOCKS * SLOT // P


class Mark:

    def __init__(self, sem, value):
        self.sem, self.value = sem, value


class Line:

    def __init__(self, sem, step=1):
        self.sem, self.step, self.count = sem, step, 0

    def next(self):
        self.count += self.step
        return Mark(self.sem, self.count)


class Script:

    def __init__(self):
        self.items = {e: [] for e in ("tensor", "vector", "scalar", "gpsimd", "sync")}
        self.seen = {e: {} for e in self.items}

    def wait(self, engine, marks):
        for m in marks:
            if m is not None and self.seen[engine].get(m.sem, 0) < m.value:
                self.seen[engine][m.sem] = m.value
                self.items[engine].append(("wait", m))

    def do(self, engine, line, step, after=()):
        self.wait(engine, after)
        m = line.next() if line is not None else None
        self.items[engine].append(("do", step, line, m))
        return m

    def play(self, engine, handle):
        for item in self.items[engine]:
            if item[0] == "wait":
                handle.wait_ge(item[1].sem, item[1].value)
            else:
                ins = item[1](handle)
                if item[2] is not None:
                    ins.then_inc(item[2].sem, item[2].step)


def build_layer(nc, x, src, dst, edge_attr, vor, cent, z_in, z_out, w_cent, b_cent, w_vor, b_vor,
                w_sum, b_sum, w_qkv, w_out, b_out, wr, br, ln_g, ln_b, w1, b1, w2, b2, out):
    ctx = ExitStack()

    def sb(name, shape, dt=F32):
        return ctx.enter_context(nc.sbuf_tensor(name, shape, dt)).ap()

    def line(name, step=1):
        return Line(ctx.enter_context(nc.semaphore(name)), step)

    def lines(name, n, step=16):
        return [line(f"{name}{i}", step) for i in range(n)]

    q = Script()
    banks = [ctx.enter_context(nc.psum_tensor(f"bank{i}", [P, 512], F32)).ap() for i in range(8)]

    table = [nc.dram_tensor(f"node_table{i}", (ROWS, RW), F32, kind="Internal").ap() for i in range(TABLES)]
    xn_rows = nc.dram_tensor("xn_rows", (ROWS, DIM), F32, kind="Internal").ap()
    y_rows = nc.dram_tensor("y_rows", (ROWS, DIM), F32, kind="Internal").ap()
    w1g = nc.dram_tensor("w1_scaled", (EXPERTS, P, KC * HID), F32, kind="Internal").ap()
    b1g = nc.dram_tensor("b1_folded", (EXPERTS, P, HC), F32, kind="Internal").ap()

    g_c, v_c, d_c = line("const_pool"), line("const_dve"), line("const_dma", 16)
    ident = sb("ident", [P, P])
    identb = sb("identb", [P, P], BF16)
    before = sb("before", [P, P])
    ones = sb("ones", [P, P])
    lane_i = sb("lane_i", [P, 1], I32)
    lane = sb("lane", [P, 1])
    spare = sb("spare", [P, 1])
    spare_i = sb("spare_i", [P, 1], I32)
    pow_i = sb("pow_i", [P, 2], I32)
    iota_i = sb("iota_i", [P, P], I32)
    iota = sb("iota", [P, P])
    iotab = sb("iotab", [P, P], BF16)
    eps_t = sb("eps_t", [P, 1])
    thresh = sb("thresh", [P, 1])
    zeros = sb("zeros", [P, ZERO])

    def pool(fn, after=()):
        return q.do("gpsimd", g_c, fn, after)

    def dve(fn, after=()):
        return q.do("vector", v_c, fn, after)

    pool(lambda e: e.memset(identb, 0.0))
    m = pool(lambda e: e.memset(ident, 0.0))
    for t in (identb, ident):
        pool(lambda e, t=t: e.affine_select(out=t, in_=t, compare_op=ALU.not_equal, fill=1.0, base=0,
                                            pattern=[[-1, P]], channel_multiplier=1), [m])
    m = pool(lambda e: e.memset(before, 0.0))
    pool(lambda e: e.affine_select(out=before, in_=before, compare_op=ALU.is_ge, fill=1.0, base=0,
                                   pattern=[[-1, P]], channel_multiplier=1), [m])
    pool(lambda e: e.iota(lane_i, pattern=[[0, 1]], base=0, channel_multiplier=1))
    pool(lambda e: e.iota(spare_i, pattern=[[0, 1]], base=NODES, channel_multiplier=1))
    pool(lambda e: e.iota(pow_i, pattern=[[0, 2]], base=127 + 63, channel_multiplier=-1))
    m_iota = pool(lambda e: e.iota(iota_i, pattern=[[1, P]], base=0, channel_multiplier=0))
    m_zero = dve(lambda e: e.memset(zeros, 0.0))
    dve(lambda e: e.memset(ones, 1.0))
    dve(lambda e: e.memset(eps_t, EPS))
    dve(lambda e: e.tensor_copy(lane, lane_i), [m_iota])
    m_spare = dve(lambda e: e.tensor_copy(spare, spare_i))
    dve(lambda e: e.tensor_copy(iota, iota_i))
    dve(lambda e: e.tensor_copy(iotab, iota_i))
    m = dve(lambda e: e.tensor_scalar(pow_i, pow_i, 23, None, ALU.logical_shift_left))
    m_const = dve(lambda e: e.tensor_scalar(thresh, pow_i[:, 0:1].bitcast(F32), 2.5, None, ALU.mult), [m])
    powers = pow_i[:, 0:1].bitcast(F32)

    tz = lines("table_zero", TABLES)
    m_tz = []
    flat = ROWS * RW // P
    rep = flat // ZERO
    for i in range(TABLES):
        m_tz.append(q.do("scalar", tz[i], lambda e, i=i: e.dma_start(
            table[i].rearrange("(p a) w -> p (a w)", p=P).rearrange("p (r c) -> p r c", r=rep),
            zeros.unsqueeze(1).to_broadcast([P, rep, ZERO])), [m_zero]))
    pad_rows = ROWS - NODES
    zr = line("pad_zero", 16)
    for rows in (xn_rows, y_rows):
        for a in range(NODES, ROWS, 75):
            m_pad = q.do("scalar", zr, lambda e, rows=rows, a=a: e.dma_start(
                rows[a:a + 75, :], zeros[0:75, 0:DIM]))

    idx_d, v_i = line("index_dma", 16), line("index_dve")
    big = sb("big", [P, TILES * DIM])
    src_i = big[:, 5000:5000 + ETILES].bitcast(I32)
    tmp_i = big[:, 6000:6000 + ETILES].bitcast(I32)
    src_f = sb("src_f", [P, ETILES])
    to_spare = sb("to_spare", [P, ETILES])
    src_hi = sb("src_hi", [P, ETILES], BF16)
    src_lo = sb("src_lo", [P, ETILES], BF16)
    dst_hi = sb("dst_hi", [P, ETILES], BF16)
    dst_lo = sb("dst_lo", [P, ETILES], BF16)

    def idv(fn, after=()):
        return q.do("vector", v_i, fn, after)

    def load_ids(ids):
        q.do("sync", idx_d, lambda e: e.dma_start(src_i[:, 0:ECOLS], ids[0:ECOLS * P].rearrange("(p c) -> p c", c=ECOLS)))
        return q.do("sync", idx_d, lambda e: e.dma_start(
            src_i[0:EREST, ECOLS:ETILES], ids[ECOLS * P:EDGES].rearrange("(p c) -> p c", c=1)))

    m = idv(lambda e: e.tensor_copy(src_i[:, ECOLS:ETILES], spare_i), [m_iota])
    q.wait("sync", [m])
    m = load_ids(src)
    m1 = idv(lambda e: e.tensor_copy(src_f, src_i), [m])
    idv(lambda e: e.tensor_scalar(to_spare, src_f, -1.0, spare, ALU.mult, ALU.add), [m1, m_spare])
    m2 = idv(lambda e: e.tensor_scalar(tmp_i, src_i, 7, None, ALU.arith_shift_right), [m])
    m3 = idv(lambda e: e.tensor_scalar(src_hi, tmp_i, 128.0, None, ALU.mult), [m2])
    m4 = idv(lambda e: e.tensor_scalar(tmp_i, src_i, 127, None, ALU.bitwise_and), [m3])
    m_src = idv(lambda e: e.tensor_copy(src_lo, tmp_i), [m4])
    m = idv(lambda e: e.memset(src_i[:, ECOLS:ETILES], TILES * P), [m_src])
    q.wait("sync", [m])
    m = load_ids(dst)
    m2 = idv(lambda e: e.tensor_scalar(tmp_i, src_i, 7, None, ALU.arith_shift_right), [m])
    m3 = idv(lambda e: e.tensor_copy(dst_hi, tmp_i), [m2])
    m4 = idv(lambda e: e.tensor_scalar(tmp_i, src_i, 127, None, ALU.bitwise_and), [m3])
    m_dst = idv(lambda e: e.tensor_copy(dst_lo, tmp_i), [m4])

    X = sb("edge_rows", [P, XRING, LOAD, XW])
    S = sb("same_node", [P, SRING, GROUP * P])
    O = sb("edge_sums", [P, ORING, GROUP, XW])
    dup = sb("dup", [P, ORING, GROUP])
    row_i = sb("row_i", [P, ORING, GROUP], I32)
    x_l, t_l = lines("edge_load", XRING), lines("table_add", TABLES)
    pe_e, v_e, a_e = line("edge_pe"), line("edge_dve"), line("edge_act")
    ps_src, ps_sum = banks[0:2], banks[2:4]
    v_x = line("edge_const")
    q.do("vector", v_x, lambda e: e.memset(X[:, :, :, EDIM:EDIM + 1], 1.0))
    m_xc = q.do("vector", v_x, lambda e: e.tensor_copy(
        X[:, :, :, EDIM + 1:XW].rearrange("p a b c -> p (a b c)"), powers.to_broadcast([P, XRING * LOAD])), [m_const])
    loaded, srcs, sames, sums, evac, rowed, added = {}, {}, {}, {}, {}, {}, {}

    def group_tiles(g):
        return list(range(g * GROUP, min(ETILES, (g + 1) * GROUP)))

    def load_edges(k):
        if k * LOAD >= ETILES:
            return
        free = [sums[(k - XRING + 1) * LOAD // GROUP - 1]] if k >= XRING else [m_xc]
        lo, hi = k * LOAD, min((k + 1) * LOAD, ECOLS)
        b = k % XRING
        if (k + 1) * LOAD > ECOLS:
            m = q.do("vector", v_x, lambda e: e.memset(X[:, b, ECOLS - lo, 0:EDIM], 0.0), free)
            q.wait("sync", [m])
            q.do("sync", x_l[b], lambda e: e.dma_start(X[0:EREST, b, ECOLS - lo, 0:EDIM], edge_attr[ECOLS * P:EDGES, :]))
        rows = edge_attr[0:ECOLS * P, :].rearrange("(p c) w -> p c w", c=ECOLS)
        loaded[k] = q.do("sync", x_l[b], lambda e: e.dma_start(X[:, b, 0:hi - lo, 0:EDIM], rows[:, lo:hi, :]), free)

    def edge_match(g):
        cs = group_tiles(g)
        ps = ps_src[g % 2]
        for i, c in enumerate(cs):
            after = [m_src, sames.get(g - 2)]
            cols = ps[:, i * P:(i + 1) * P]
            q.do("tensor", None, lambda e, c=c, cols=cols: e.matmul(
                cols, src_hi[:, c:c + 1].to_broadcast([P, P]), identb, start=True, stop=False), after)
            srcs[g] = q.do("tensor", pe_e, lambda e, c=c, cols=cols: e.matmul(
                cols, src_lo[:, c:c + 1].to_broadcast([P, P]), identb, start=False, stop=True))
        n, c0 = len(cs), cs[0]
        sames[g] = q.do("vector", v_e, lambda e: e.tensor_tensor(
            S[:, g % SRING, 0:n * P].rearrange("p (a b) -> p a b", a=n),
            ps[:, 0:n * P].rearrange("p (a b) -> p a b", a=n),
            src_f[:, c0:c0 + n].unsqueeze(2).to_broadcast([P, n, P]), ALU.is_equal),
            [srcs[g], sums.get(g - SRING)])

    def edge_sum(g):
        cs = group_tiles(g)
        n, c0, o = len(cs), cs[0], g % ORING
        ps = ps_sum[g % 2]
        for i, c in enumerate(cs):
            k = c // LOAD
            sums[g] = q.do("tensor", pe_e, lambda e, i=i, c=c, k=k: e.matmul(
                ps[:, i * XW:(i + 1) * XW], S[:, g % SRING, i * P:(i + 1) * P], X[:, k % XRING, c % LOAD, :],
                start=True, stop=True), [sames[g], loaded[k], evac.get(g - 2)])
        psv = ps[:, 0:n * XW].rearrange("p (a b) -> p a b", a=n)
        free = [added[c] for c in group_tiles(g - ORING)] if g >= ORING else []
        evac[g] = q.do("scalar", a_e, lambda e: e.copy(O[:, o, 0:n, :], psv), [sums[g]] + free)
        m = q.do("vector", v_e, lambda e: e.scalar_tensor_tensor(
            dup[:, o, 0:n], O[:, o, 0:n, RW], thresh, to_spare[:, c0:c0 + n], ALU.is_gt, ALU.mult), [evac[g]])
        rowed[g] = q.do("vector", v_e, lambda e: e.tensor_tensor(
            row_i[:, o, 0:n], dup[:, o, 0:n], src_f[:, c0:c0 + n], ALU.add), [m] + free)
        for i, c in enumerate(cs):
            t = c % TABLES
            added[c] = q.do("gpsimd", t_l[t], lambda e, i=i, t=t: e.indirect_dma_start(
                table[t], bass.IndirectOffsetOnAxis(ap=row_i[:, o, i:i + 1], axis=0), O[:, o, i, 0:RW], None,
                compute_op=ALU.add, bounds_check=ROWS - 1, oob_is_err=True),
                [evac[g], rowed[g], added.get(c - TABLES, m_tz[t])])

    hotA = sb("hotA", [P, 2, HB * TILES], BF16)
    hotB = sb("hotB", [P, 2, HB * P], BF16)
    v_h, pe_h = line("degree_dve"), line("degree_pe")
    ps_deg = banks[4]
    in_deg = sb("in_deg", [P, TILES], I32)
    done = {}

    def degree_steps():
        for b in range(-(-ETILES // HB)):
            lo, hi = b * HB, min(ETILES, (b + 1) * HB)
            n, r = hi - lo, b % 2
            free = [done.get(("deg", b - 2))]
            q.do("vector", v_h, lambda e, n=n, r=r, lo=lo, hi=hi: e.tensor_tensor(
                hotA[:, r, 0:n * TILES].rearrange("p (a b) -> p a b", a=n),
                iotab[:, 0:TILES].unsqueeze(1).to_broadcast([P, n, TILES]),
                dst_hi[:, lo:hi].unsqueeze(2).to_broadcast([P, n, TILES]), ALU.is_equal), [m_dst, m_const] + free)
            hot = q.do("vector", v_h, lambda e, n=n, r=r, lo=lo, hi=hi: e.tensor_tensor(
                hotB[:, r, 0:n * P].rearrange("p (a b) -> p a b", a=n),
                iotab.unsqueeze(1).to_broadcast([P, n, P]),
                dst_lo[:, lo:hi].unsqueeze(2).to_broadcast([P, n, P]), ALU.is_equal))
            for i in range(n):
                c = lo + i
                done["deg", b] = q.do("tensor", pe_h, lambda e, i=i, r=r, c=c: e.matmul(
                    ps_deg[:, 0:TILES], hotB[:, r, i * P:(i + 1) * P], hotA[:, r, i * TILES:(i + 1) * TILES],
                    start=(c == 0), stop=(c == ETILES - 1)), [hot])
            yield
        done["in_deg"] = q.do("vector", v_h, lambda e: e.tensor_scalar(
            in_deg, ps_deg[:, 0:TILES], float(DEG - 1), None, ALU.min), [done["deg", b]])
        yield

    d_m, v_m, a_m, pe_m = line("mix_dma", 16), line("mix_dve"), line("mix_act"), line("mix_pe")
    state = sb("state", [P, TILES, DIM])
    xnT = big.rearrange("p (t k n) -> p t k n", t=TILES, k=KC)
    mixw = sb("mixw", [P, 10240])
    at = [0]

    def part(n):
        at[0] += n
        return mixw[:, at[0] - n:at[0]]

    wqkv = part(KC * 3 * INNER).rearrange("p (k n) -> p k n", k=KC)
    wout = part(PAIRS * DIM).rearrange("p (j n) -> p j n", j=PAIRS)
    wqT = part(PAIRS * DIM).rearrange("p (j n) -> p j n", j=PAIRS)
    folded = part(PAIRS * DIM).rearrange("p (j n) -> p j n", j=PAIRS)
    dotsT = part(INNER).rearrange("p (j n) -> p j n", j=PAIRS)
    squares = part(2 * INNER)
    ks = part(INNER)
    vs = part(INNER)
    xn = part(2 * DIM).rearrange("p (r n) -> p r n", r=2)
    mq = sb("mq", [P, KC, DIM])
    mv = sb("mv", [P, TILES, 2])
    stats = sb("stats", [P, 2, 6])
    rstd = sb("rstd", [P, TILES])
    wmean = sb("wmean", [P, KC * 2 * HEADS])
    ss = sb("ss", [P, 2 * HEADS])
    sd = sb("sd", [P, 2 * HEADS])
    rkv = sb("rkv", [P, HEADS])
    ps_dots, ps_kv = banks[5], banks[6:8]
    vec = {n: sb("bc_" + n, [P, DIM]) for n in ("w_cent", "b_cent", "w_vor", "b_vor", "b_out", "b_sum")}
    node_v = sb("node_v", [P, 2, TILES])
    node_r = big[:, 7000:7000 + 2 * P].rearrange("p (i n) -> p i n", i=2)
    x_d = lines("x_load", 7)
    term = sb("term", [P, 2, DIM])
    wsum = sb("wsum", [P, DIM])
    wr_t = sb("wr_t", [P, KC, EXPERTS])
    br_t = sb("br_t", [P, EXPERTS])

    def mixv(fn, after=()):
        return q.do("vector", v_m, fn, after)

    def mixa(fn, after=()):
        return q.do("scalar", a_m, fn, after)

    def mixp(fn, after=()):
        return q.do("tensor", pe_m, fn, after)

    def load_small():
        m = q.do("vector", v_m, lambda e: e.memset(state[:, TILES - 1, :], 0.0))
        m = q.do("vector", v_m, lambda e: e.memset(node_r, 0.0))
        q.wait("scalar", [m])
        per = TILES // 7
        for i in range(7):
            lo, hi = i * per, min((i + 1) * per, TILES - 1)
            q.do("scalar", x_d[i], lambda e, lo=lo, hi=hi: e.dma_start(
                state[:, lo:hi, :], x[lo * P:hi * P, :].rearrange("(t p) n -> p t n", p=P)))
        done["x"] = [Mark(l.sem, 16) for l in x_d]
        done["x"][6] = q.do("scalar", x_d[6], lambda e: e.dma_start(state[0:LAST, TILES - 1, :], x[(TILES - 1) * P:NODES, :]))
        q.do("scalar", d_m, lambda e: e.dma_start(wqkv, w_qkv.rearrange("(k p) n -> p k n", p=P)))
        q.do("scalar", d_m, lambda e: e.dma_start(wout, w_out.rearrange("(j p) n -> p j n", p=P)))
        for n, v in (("w_cent", w_cent[0]), ("b_cent", b_cent), ("w_vor", w_vor[0]), ("b_vor", b_vor),
                     ("b_out", b_out), ("b_sum", b_sum)):
            q.do("scalar", d_m, lambda e, n=n, v=v: e.dma_start(vec[n], v.partition_broadcast(P)))
        for i, v in enumerate((cent, vor)):
            q.do("scalar", d_m, lambda e, i=i, v=v: e.dma_start(
                node_r[0:TILES - 1, i, :], v[0:(TILES - 1) * P, :].rearrange("(t p) o -> t (p o)", p=P)))
            q.do("scalar", d_m, lambda e, i=i, v=v: e.dma_start(
                node_r[TILES - 1:TILES, i, 0:LAST], v[(TILES - 1) * P:NODES, :].rearrange("(a p) o -> a (p o)", a=1)))
        q.do("scalar", d_m, lambda e: e.dma_start(wsum, w_sum))
        q.do("scalar", d_m, lambda e: e.dma_start(wr_t, wr.rearrange("(k p) n -> p k n", p=P)))
        done["small"] = q.do("scalar", d_m, lambda e: e.dma_start(br_t, br.partition_broadcast(P)))

    def norm_stats(queue, rows, stat, to, after):
        m = queue(lambda e: e.bn_stats(stat, rows), after)
        return queue(lambda e: e.bn_aggr(to, stat), [m])

    def mix_steps():
        per = TILES // 7
        for t in range(TILES):
            m = norm_stats(mixv, state[:, t, :], stats[:, t % 2, :], mv[:, t, :], [done["x"][min(t // per, 6)]])
            if t % 2:
                yield
        m = mixa(lambda e: e.activation(rstd, mv[:, :, 1], ACT.Sqrt, bias=eps_t), [m])
        m_rstd = mixv(lambda e: e.reciprocal(rstd, rstd), [m])
        for i in range(2):
            m = mixp(lambda e, i=i: e.transpose(ps_kv[1][:, i * P:i * P + TILES], node_r[0:TILES, i, :],
                                                ident[0:TILES, 0:TILES]), [done["small"], m_const])
        done["node_v"] = mixv(lambda e: e.tensor_copy(
            node_v, ps_kv[1][:, 0:2 * P].rearrange("p (i n) -> p i n", i=2)[:, :, 0:TILES]), [m])
        kvw = wqkv[:, :, INNER:3 * INNER]
        for k in range(KC):
            mixv(lambda e, k=k: e.reduce_sum(wmean[:, k * 2 * HEADS:(k + 1) * 2 * HEADS],
                                             kvw[:, k, :].rearrange("p (h d) -> p h d", d=DH), AX.X), [done["small"]])
        m = Mark(v_m.sem, v_m.count)
        m = mixv(lambda e: e.tensor_scalar(wmean, wmean, 1.0 / DH, None, ALU.mult), [m])
        for k in range(KC):
            wk = kvw[:, k, :].rearrange("p (h d) -> p h d", d=DH)
            m_w = mixv(lambda e, k=k, wk=wk: e.tensor_tensor(
                wk, wk, wmean[:, k * 2 * HEADS:(k + 1) * 2 * HEADS].unsqueeze(2).to_broadcast([P, 2 * HEADS, DH]),
                ALU.subtract), [m])
        yield
        kv_free, xn_free, kv_used = done["node_v"], {}, None
        for t in range(TILES):
            r = t % 2
            m = mixv(lambda e, t=t, r=r: e.tensor_scalar(xn[:, r, :], state[:, t, :], mv[:, t, 0:1], rstd[:, t:t + 1],
                                                         ALU.subtract, ALU.mult), [m_rstd, xn_free.get(t - 2)])
            for k in range(KC):
                mt = mixp(lambda e, k=k, r=r: e.transpose(ps_kv[0][:, k * P:(k + 1) * P], xn[:, r, k * P:(k + 1) * P], ident),
                          [m, kv_free, m_const])
            xn_free[t] = mt
            mixv(lambda e, t=t, r=r: e.tensor_tensor(state[:, t, :], state[:, t, :], xn[:, r, :], ALU.add), [m])
            yield
            mt = mixa(lambda e, t=t: e.copy(big[:, t * DIM:(t + 1) * DIM], ps_kv[0][:, 0:DIM]), [mt, m_dst] + done["weights"])
            for h in range(2):
                for k in range(KC):
                    mk = mixp(lambda e, t=t, k=k, h=h: e.matmul(
                        ps_kv[h], xnT[:, t, k, :], kvw[:, k, h * INNER:(h + 1) * INNER],
                        start=(k == 0), stop=(k == KC - 1)), [mt, m_w, kv_free])
            yield
            for h in range(2):
                m = mixa(lambda e, h=h: e.activation(squares[:, h * INNER:(h + 1) * INNER], ps_kv[h], ACT.Square),
                         [mk, done.get("ss")])
            m_v = mixa(lambda e: e.copy(vs, ps_kv[1]), [kv_used])
            m = mixv(lambda e: e.reduce_sum(ss, squares.rearrange("p (h d) -> p h d", d=DH), AX.X), [m, done.get("sd")])
            done["ss"] = m
            yield
            m = mixa(lambda e: e.activation(sd, ss, ACT.Sqrt, bias=eps_t, scale=1.0 / DH), [m])
            done["sd"] = m
            m = mixv(lambda e: e.tensor_tensor(rkv, sd[:, 0:HEADS], sd[:, HEADS:2 * HEADS], ALU.mult), [m])
            m = mixv(lambda e: e.reciprocal(rkv, rkv), [m])
            kv_free = mixv(lambda e: e.tensor_tensor(
                ks.rearrange("p (h d) -> p h d", d=DH), ps_kv[0].rearrange("p (h d) -> p h d", d=DH),
                rkv.unsqueeze(2).to_broadcast([P, HEADS, DH]), ALU.mult), [m, kv_used])
            for j in range(PAIRS):
                kv_used = mixp(lambda e, t=t, j=j: e.matmul(
                    ps_dots[:, j * P:(j + 1) * P], vs[:, j * P:(j + 1) * P], ks[:, j * P:(j + 1) * P],
                    start=(t == 0 and j == 0), stop=(t == TILES - 1 and j == PAIRS - 1), skip_group_check=True),
                    [kv_free, m_v])
            yield
        for j in range(PAIRS):
            for k in range(KC):
                c = j * KC + k
                m = mixp(lambda e, j=j, k=k, c=c: e.transpose(
                    ps_kv[c // 4][:, c % 4 * P:(c % 4 + 1) * P], wqkv[:, k, j * P:(j + 1) * P], ident), [kv_free])
        for h in range(2):
            ma = mixa(lambda e, h=h: e.copy(wqT[:, 2 * h:2 * h + 2, :].rearrange("p a b -> p (a b)"), ps_kv[h]), [m])
        m = mixv(lambda e: e.memset(dotsT, 0.0))
        for s in range(2):
            w = slice(s * DH, (s + 1) * DH)
            md = mixv(lambda e, w=w: e.tensor_scalar(
                dotsT[w, :, w], ps_dots[w, :].rearrange("p (j n) -> p j n", j=PAIRS)[:, :, w], 1.0 / NODES, None, ALU.mult),
                [m, kv_used])
        for j in range(PAIRS):
            m = mixp(lambda e, j=j: e.matmul(ps_kv[j // 2][:, j % 2 * DIM:(j % 2 + 1) * DIM], dotsT[:, j, :],
                                             wout[:, j, :], start=True, stop=True), [md, ma])
        for h in range(2):
            m = mixa(lambda e, h=h: e.copy(folded[:, 2 * h:2 * h + 2, :].rearrange("p a b -> p (a b)"), ps_kv[h]), [m])
        yield
        for k in range(KC):
            for j in range(PAIRS):
                mp = mixp(lambda e, j=j, k=k: e.matmul(
                    ps_kv[k][:, 0:DIM], wqT[:, j, k * P:(k + 1) * P], folded[:, j, :],
                    start=(j == 0), stop=(j == PAIRS - 1)), [m])
        for k in range(KC):
            m_mq = mixa(lambda e, k=k: e.copy(mq[:, k, :], ps_kv[k][:, 0:DIM]), [mp])
        yield
        free = {}
        for t in range(TILES):
            b = ps_kv[t % 2][:, 0:DIM]
            for k in range(KC):
                mp = mixp(lambda e, t=t, k=k, b=b: e.matmul(b, xnT[:, t, k, :], mq[:, k, :], start=(k == 0),
                                                            stop=(k == KC - 1)), [m_mq, free.get(t - 2)])
            acts = []
            for i, n in enumerate(("cent", "vor")):
                m = mixv(lambda e, t=t, i=i, n=n: e.scalar_tensor_tensor(
                    term[:, i, :], vec["w_" + n], node_v[:, i, t:t + 1], vec["b_" + n], ALU.mult, ALU.add),
                    [done.get("term"), done["node_v"]])
                acts.append(mixa(lambda e, i=i: e.activation(term[:, i, :], term[:, i, :], ACT.Sigmoid), [m]))
            yield
            m = Mark(v_m.sem, v_m.count)
            for other, need in ((b, mp), (vec["b_out"], None), (term[:, 0, :], acts[0]), (term[:, 1, :], acts[1])):
                m = mixv(lambda e, t=t, other=other: e.tensor_tensor(state[:, t, :], state[:, t, :], other, ALU.add),
                         [m, need])
                free.setdefault(t, m)
            done["term"] = m
            yield
        done["mix"] = m

    w_l = lines("w1_load", 2)
    v_w, pe_w, w_s2 = line("w1_dve"), line("w1_pe"), lines("w1_store", 2)
    w_ld = line("small_load", 16)
    w1_t = big[:, 0:2 * KC * HID].rearrange("p (r k n) -> p r k n", r=2, k=KC)
    ln_t = sb("ln_t", [P, 2, EXPERTS, KC])
    ln_r = big[0:2 * EXPERTS * KC, 7500:7500 + P]
    b1_r = big[0:EXPERTS * HC, 7800:7800 + P]
    b1_t = sb("b1_t", [P, EXPERTS, HC])

    def weight_steps():
        for i, v in enumerate((ln_g, ln_b)):
            q.do("sync", w_ld, lambda e, i=i, v=v: e.dma_start(
                ln_r[i * EXPERTS * KC:(i + 1) * EXPERTS * KC, :], v.rearrange("e (k p) -> (e k) p", p=P)))
        m = q.do("sync", w_ld, lambda e: e.dma_start(b1_r, b1.rearrange("e (h p) -> (e h) p", p=P)))
        n = 2 * EXPERTS * KC
        q.do("tensor", pe_w, lambda e: e.transpose(ps_kv[0][:, 0:n], ln_r, ident[0:n, 0:n]), [m, m_const])
        m = q.do("tensor", pe_w, lambda e: e.transpose(ps_kv[0][:, P:P + EXPERTS * HC], b1_r,
                                                       ident[0:EXPERTS * HC, 0:EXPERTS * HC]))
        q.do("vector", v_w, lambda e: e.tensor_copy(ln_t.rearrange("p i e k -> p (i e k)"), ps_kv[0][:, 0:n]), [m])
        m_small = q.do("vector", v_w, lambda e: e.tensor_copy(b1_t.rearrange("p e h -> p (e h)"),
                                                              ps_kv[0][:, P:P + EXPERTS * HC]))
        yield
        stored = {}
        for ex in range(EXPERTS):
            r = ex % 2
            m = q.do("sync", w_l[r], lambda e, ex=ex, r=r: e.dma_start(
                w1_t[:, r], w1[ex].rearrange("(k p) n -> p k n", p=P)), [m_dst, stored.get(ex - 2)])
            yield
            for h in range(HC):
                for k in range(KC):
                    mp = q.do("tensor", pe_w, lambda e, ex=ex, r=r, h=h, k=k: e.matmul(
                        ps_deg[:, 256 + h:257 + h], w1_t[:, r, k, h * P:(h + 1) * P], ln_t[:, 1, ex, k:k + 1],
                        start=(k == 0), stop=(k == KC - 1)), [m, m_small, done["in_deg"], done.get("b1")])
            done["b1"] = q.do("vector", v_w, lambda e, ex=ex: e.tensor_tensor(
                b1_t[:, ex, :], b1_t[:, ex, :], ps_deg[:, 256:256 + HC], ALU.add), [mp])
            yield
            for k in range(KC):
                m = q.do("vector", v_w, lambda e, ex=ex, k=k, r=r: e.tensor_scalar(
                    w1_t[:, r, k, :], w1_t[:, r, k, :], ln_t[:, 0, ex, k:k + 1], None, ALU.mult), [mp])
                yield
            q.do("sync", w_s2[r], lambda e, ex=ex, r=r: e.dma_start(w1g[ex], w1_t[:, r].rearrange("p k n -> p (k n)")), [m])
            stored[ex] = q.do("sync", w_s2[r], lambda e, ex=ex: e.dma_start(b1g[ex], b1_t[:, ex, :]), [m])
        done["weights"] = [stored[EXPERTS - 2], stored[EXPERTS - 1]]
        yield

    load_small()
    for k in range(XRING - 1):
        load_edges(k)
    edge_match(0)

    def chain(*gens):
        for g in gens:
            yield from g

    side = chain(degree_steps(), weight_steps(), mix_steps())
    side_steps = 196 + 1 + 40 + 25 + TILES * 4 + 5 + TILES * 2 + 8
    due = 0.0
    for g in range(GROUPS):
        if g * GROUP % LOAD == 0:
            load_edges(g * GROUP // LOAD + XRING - 1)
        if g + 1 < GROUPS:
            edge_match(g + 1)
        edge_sum(g)
        due += side_steps / (GROUPS - 6)
        while due >= 1:
            next(side, None)
            due -= 1
    for _ in side:
        pass

    at[0] = 0
    NR = 3
    parts = part(NR * TABLES * RW).rearrange("p (r a w) -> p r a w", r=NR, a=TABLES)
    zin_t = part(NR * DIM).rearrange("p (r n) -> p r n", r=NR)
    zout_t = part(NR * DIM).rearrange("p (r n) -> p r n", r=NR)
    sumT = part(2 * P).rearrange("p (r n) -> p r n", r=2)
    y = part(2 * DIM).rearrange("p (r n) -> p r n", r=2)
    yT = part(2 * DIM).rearrange("p (r n) -> p r n", r=2)
    xn2 = part(3 * DIM).rearrange("p (r n) -> p r n", r=3)
    count = sb("count", [P, TILES])
    out_deg = sb("out_deg", [P, TILES], I32)
    mv2 = sb("mv2", [P, TILES, 2])
    r1 = sb("r1", [P, TILES])
    r2 = sb("r2", [P, TILES])
    p_l, zi_l, zo_l = lines("parts_load", NR), lines("zin_load", NR), lines("zout_load", NR)
    xs_l, ys_l = lines("xn_store", 3), line("y_store", 16)
    v_n, a_n, pe_n = line("node_dve"), line("node_act"), line("node_pe")
    ps_t, ps_s, ps_y, ps_log = banks[0:2], banks[2:4], banks[5:7], banks[7]
    all_added = [added[c] for c in range(ETILES - TABLES, ETILES)]
    last_mix = [done["mix"], Mark(pe_m.sem, pe_m.count), Mark(a_m.sem, a_m.count), Mark(v_e.sem, v_e.count),
                Mark(a_e.sem, a_e.count), Mark(pe_e.sem, pe_e.count)]
    nd = {}

    def nv(fn, after=()):
        return q.do("vector", v_n, fn, after)

    def na(fn, after=()):
        return q.do("scalar", a_n, fn, after)

    def npe(fn, after=()):
        return q.do("tensor", pe_n, fn, after)

    def node_load(t):
        r = t % NR
        free = [nd.get(("x2", t - NR))] + last_mix
        for a in range(TABLES):
            nd["parts", t] = q.do("sync", p_l[r], lambda e, a=a: e.dma_start(
                parts[:, r, a, :], table[a][t * P:(t + 1) * P, :]), all_added + free)
        nd["zin", t] = q.do("gpsimd", zi_l[r], lambda e: e.indirect_dma_start(
            zin_t[:, r, :], None, z_in, bass.IndirectOffsetOnAxis(ap=in_deg[:, t:t + 1], axis=0),
            bounds_check=DEG - 1, oob_is_err=True), [done["in_deg"]] + free)
        m = nv(lambda e: e.reduce_sum(count[:, t:t + 1], parts[:, r, :, EDIM:RW].rearrange("p a w -> p (a w)"), AX.X),
               [nd["parts", t]])
        m = nv(lambda e: e.tensor_scalar(out_deg[:, t:t + 1], count[:, t:t + 1], float(DEG - 1), None, ALU.min), [m])
        nd["zout", t] = q.do("gpsimd", zo_l[r], lambda e: e.indirect_dma_start(
            zout_t[:, r, :], None, z_out, bass.IndirectOffsetOnAxis(ap=out_deg[:, t:t + 1], axis=0),
            bounds_check=DEG - 1, oob_is_err=True), [m] + free)

    def node_sum(t):
        r, r2_ = t % NR, t % 2
        for a in range(TABLES):
            m = npe(lambda e, a=a: e.matmul(ps_t[r2_][:, 0:P], parts[:, r, a, 0:EDIM], ident,
                                            start=(a == 0), stop=(a == TABLES - 1)),
                    [nd["parts", t], nd.get(("sumT", t - 2))] + last_mix)
        m = na(lambda e: e.copy(sumT[:, r2_, :], ps_t[r2_][:, 0:P]), [m, nd.get(("proj", t - 2))] + last_mix)
        nd["sumT", t] = m
        m = npe(lambda e: e.matmul(ps_s[r2_][:, 0:DIM], sumT[:, r2_, :], wsum, start=True, stop=True),
                [m, nd.get(("x2a", t - 2))])
        nd["proj", t] = m
        st = state[:, t, :]
        m = nv(lambda e: e.tensor_tensor(st, st, ps_s[r2_][:, 0:DIM], ALU.add), [m])
        nd["x2a", t] = m
        m = nv(lambda e: e.scalar_tensor_tensor(st, vec["b_sum"], count[:, t:t + 1], st, ALU.mult, ALU.add), [m])
        m = nv(lambda e: e.tensor_tensor(st, st, zin_t[:, r, :], ALU.add), [m, nd["zin", t]])
        m = nv(lambda e: e.tensor_tensor(st, st, zout_t[:, r, :], ALU.add), [m, nd["zout", t]])
        nd["x2", t] = m
        m = norm_stats(nv, st, stats[:, t % 2, :], mv2[:, t, :], [m])
        m = na(lambda e: e.activation(r1[:, t:t + 1], mv2[:, t, 1:2], ACT.Sqrt, bias=eps_t), [m])
        nd["sq", t] = m
        rows = LAST if t == TILES - 1 else P
        q.do("sync", ys_l, lambda e: e.dma_start(y_rows[t * P:t * P + rows, :], st[0:rows, :]), [nd["x2", t]])

    def node_norm(t):
        r = t % 2
        one = slice(t, t + 1)
        m = nv(lambda e: e.reciprocal(r1[:, one], r1[:, one]), [nd["sq", t]])
        m2 = nv(lambda e: e.tensor_scalar(r2[:, one], r1[:, one], r1[:, one], mv2[:, t, 1:2], ALU.mult, ALU.mult), [m])
        m2 = na(lambda e: e.activation(r2[:, one], r2[:, one], ACT.Sqrt, bias=eps_t), [m2])
        m = nv(lambda e: e.tensor_scalar(y[:, r, :], state[:, t, :], mv2[:, t, 0:1], r1[:, one], ALU.subtract, ALU.mult),
               [m, nd.get(("yT", t - 2)), nd.get(("xn2", t - 2))] + last_mix)
        for k in range(KC):
            mp = npe(lambda e, k=k: e.transpose(ps_y[r][:, k * P:(k + 1) * P], y[:, r, k * P:(k + 1) * P], ident),
                     [m, nd.get(("yTc", t - 2))])
        nd["yT", t] = mp
        nd["r2", t] = nv(lambda e: e.reciprocal(r2[:, one], r2[:, one]), [m2])
        ma = na(lambda e: e.copy(yT[:, r, :], ps_y[r][:, 0:DIM]), [mp, nd.get(("log", t - 2))])
        nd["yTc", t] = ma
        nd["xn2", t] = nv(lambda e: e.tensor_scalar(xn2[:, t % 3, :], y[:, r, :], r2[:, one], None, ALU.mult),
                          [nd["r2", t], nd.get(("xs", t - 3))])
        for k in range(KC):
            mp = npe(lambda e, k=k: e.matmul(ps_log[:, t * EXPERTS:(t + 1) * EXPERTS], yT[:, r, k * P:(k + 1) * P],
                                             wr_t[:, k, :], start=(k == 0), stop=(k == KC - 1)), [ma])
        nd["log", t] = mp
        rows = LAST if t == TILES - 1 else P
        nd["xs", t] = q.do("sync", xs_l[t % 3], lambda e: e.dma_start(
            xn_rows[t * P:t * P + rows, :], xn2[0:rows, t % 3, :]), [nd["xn2", t]])

    for t in range(TILES + 3):
        if t < TILES:
            node_load(t)
        if 0 <= t - 2 < TILES:
            node_sum(t - 2)
        if 0 <= t - 3 < TILES:
            node_norm(t - 3)

    v_r, a_r, pe_r, g_r, d_r = (line("route_dve"), line("route_act"), line("route_pe"), line("route_pool"),
                                line("route_dma", 16))
    at[0] = 0
    N8 = TILES * EXPERTS
    nodes_done = [Mark(l.sem, l.count) for l in (v_n, a_n, pe_n)] + [nd["xs", t] for t in range(TILES - 3, TILES)]
    logit, hot1, hot2, tmp, tmp2, cums, cums2 = (part(N8).rearrange("p (t e) -> p t e", e=EXPERTS) for _ in range(7))
    rank = part(EXPERTS)
    base = part(EXPERTS)
    base2 = part(EXPERTS)
    tiles_e = part(EXPERTS)
    cnt_i = part(EXPERTS).bitcast(I32)
    top1, top2, wt1, wt2, num, pos = (part(TILES) for _ in range(6))
    pos_i = part(TILES).bitcast(I32)
    p_hi, p_lo = part(2 * TILES).rearrange("p (k t) -> p k t", k=2), part(2 * TILES).rearrange("p (k t) -> p k t", k=2)
    valid = part(1)
    MR = 4
    lo_hot = part(MR * P).rearrange("p (r n) -> p r n", r=MR)
    hi_hot = part(MR * 2 * STILES).rearrange("p (r a n) -> p r a n", r=MR, a=2)
    slot_tok = sb("slot_tok", [P, STILES], I32)
    slot_w = sb("slot_w", [P, STILES])
    slot_f = part(STILES)
    empty = part(STILES)
    blk = part(BLOCKS)
    owner = part(BLOCKS)
    owner_i = sb("owner_i", [P, BLOCKS], I32)

    chainm = [None]

    def rv(fn, after=()):
        chainm[0] = q.do("vector", v_r, fn, [chainm[0], *after])
        return chainm[0]

    def b8(v):
        return v.unsqueeze(2).to_broadcast([P, TILES, EXPERTS])

    def over_tiles(v):
        return v.unsqueeze(1).to_broadcast([P, TILES, EXPERTS])

    rv(lambda e: e.tensor_tensor(logit, ps_log[:, 0:N8].rearrange("p (t e) -> p t e", e=EXPERTS), over_tiles(br_t), ALU.add),
       nodes_done)
    rv(lambda e: e.tensor_scalar(rank, iota[:, 0:EXPERTS], -1.0, float(EXPERTS), ALU.mult, ALU.add))
    rv(lambda e: e.tensor_scalar(valid, lane, float(LAST), None, ALU.is_lt))

    def pick(top, hot):
        rv(lambda e: e.reduce_max(top, logit, AX.X))
        rv(lambda e: e.tensor_tensor(tmp, logit, b8(top), ALU.is_equal))
        rv(lambda e: e.tensor_tensor(tmp, tmp, over_tiles(rank), ALU.mult))
        rv(lambda e: e.reduce_max(num, tmp, AX.X))
        rv(lambda e: e.tensor_tensor(hot, tmp, b8(num), ALU.is_equal))

    pick(top1, hot1)
    rv(lambda e: e.tensor_scalar(tmp2, hot1, -3.0e38, None, ALU.mult))
    rv(lambda e: e.tensor_scalar(tmp, hot1, -1.0, 1.0, ALU.mult, ALU.add))
    rv(lambda e: e.tensor_tensor(logit, logit, tmp, ALU.mult))
    rv(lambda e: e.tensor_tensor(logit, logit, tmp2, ALU.add))
    pick(top2, hot2)
    m = rv(lambda e: e.tensor_tensor(wt2, top2, top1, ALU.subtract))
    m = q.do("scalar", a_r, lambda e: e.activation(wt2, wt2, ACT.Exp), [m])
    rv(lambda e: e.tensor_scalar(wt1, wt2, 1.0, None, ALU.add), [m])
    rv(lambda e: e.reciprocal(wt1, wt1))
    rv(lambda e: e.tensor_tensor(wt2, wt2, wt1, ALU.mult))
    for h in (hot1, hot2):
        rv(lambda e, h=h: e.tensor_scalar(h[:, TILES - 1, :], h[:, TILES - 1, :], valid, None, ALU.mult))
    m = rv(lambda e: e.tensor_tensor(tmp, hot1, hot2, ALU.add))
    flat_t = tmp.rearrange("p t e -> p (t e)")
    q.do("tensor", pe_r, lambda e: e.matmul(banks[0][:, 0:N8], before, flat_t, start=True, stop=True), [m])
    m = q.do("tensor", pe_r, lambda e: e.matmul(banks[1][:, 0:N8], ones, flat_t, start=True, stop=True), [m])
    rv(lambda e: e.tensor_copy(cums.rearrange("p t e -> p (t e)"), banks[1][:, 0:N8]), [m])
    a, b, d = cums, cums2, 1
    while d < TILES:
        rv(lambda e, a=a, b=b, d=d: e.tensor_copy(b[:, 0:d, :], a[:, 0:d, :]))
        rv(lambda e, a=a, b=b, d=d: e.tensor_tensor(b[:, d:TILES, :], a[:, d:TILES, :], a[:, 0:TILES - d, :], ALU.add))
        a, b, d = b, a, 2 * d
    shift = SLOT.bit_length() - 1
    rv(lambda e, a=a: e.tensor_scalar(cnt_i, a[:, TILES - 1, :], float(SLOT - 1), None, ALU.add))
    rv(lambda e: e.tensor_scalar(cnt_i, cnt_i, shift, None, ALU.arith_shift_right))
    rv(lambda e: e.tensor_copy(tiles_e, cnt_i))
    rv(lambda e: e.tensor_copy(base, tiles_e))
    c, f, d = base, base2, 1
    while d < EXPERTS:
        rv(lambda e, c=c, f=f, d=d: e.tensor_copy(f[:, 0:d], c[:, 0:d]))
        rv(lambda e, c=c, f=f, d=d: e.tensor_tensor(f[:, d:EXPERTS], c[:, d:EXPERTS], c[:, 0:EXPERTS - d], ALU.add))
        c, f, d = f, c, 2 * d
    rv(lambda e: e.memset(owner, 0.0))
    for ex in range(EXPERTS - 1):
        rv(lambda e, ex=ex, c=c: e.scalar_tensor_tensor(owner, iota[:, 0:BLOCKS], c[:, ex:ex + 1], owner, ALU.is_ge, ALU.add))
    m_owner = rv(lambda e: e.tensor_copy(owner_i, owner))
    rv(lambda e, c=c, f=f: e.tensor_tensor(f, c, tiles_e, ALU.subtract))
    rv(lambda e, f=f: e.tensor_scalar(f, f, float(SLOT), None, ALU.mult))
    rv(lambda e, a=a, b=b: e.tensor_tensor(b, a, banks[1][:, 0:N8].rearrange("p (t e) -> p t e", e=EXPERTS), ALU.subtract))
    rv(lambda e, b=b: e.tensor_tensor(b, b, banks[0][:, 0:N8].rearrange("p (t e) -> p t e", e=EXPERTS), ALU.add))
    rv(lambda e, b=b, f=f: e.tensor_tensor(b, b, over_tiles(f), ALU.add))
    rv(lambda e: e.tensor_scalar(num, iota[:, 0:TILES], float(P), 1.0, ALU.mult, ALU.add))
    rv(lambda e: e.tensor_scalar(num, num, lane, None, ALU.add))
    rv(lambda e: e.tensor_scalar(num[:, TILES - 1:TILES], num[:, TILES - 1:TILES], valid, None, ALU.mult))
    for k, h in enumerate((hot1, hot2)):
        rv(lambda e, h=h, b=b: e.tensor_tensor(tmp, h, b, ALU.mult))
        rv(lambda e: e.reduce_sum(pos, tmp, AX.X))
        rv(lambda e: e.tensor_copy(pos_i, pos))
        rv(lambda e: e.tensor_scalar(cnt_i if False else tmp2.rearrange("p t e -> p (t e)")[:, 0:TILES].bitcast(I32), pos_i, 7, None, ALU.arith_shift_right))
        rv(lambda e, k=k: e.tensor_copy(p_hi[:, k, :], tmp2.rearrange("p t e -> p (t e)")[:, 0:TILES].bitcast(I32)))
        rv(lambda e: e.tensor_scalar(pos_i, pos_i, 127, None, ALU.bitwise_and))
        m_pos = rv(lambda e, k=k: e.tensor_copy(p_lo[:, k, :], pos_i))
    for w in (wt1, wt2):
        m_pos = rv(lambda e, w=w: e.tensor_scalar(w[:, TILES - 1:TILES], w[:, TILES - 1:TILES], valid, None, ALU.mult))

    mapped = {}
    for n in range(2 * TILES):
        k, t = n // TILES, n % TILES
        r = n % MR
        w = (wt1, wt2)[k]
        engine, ln = ("gpsimd", g_r) if n % 3 == 2 else ("vector", v_r)
        free = [mapped.get(n - MR), m_pos]
        q.do(engine, ln, lambda e, r=r, k=k, t=t: e.tensor_scalar(
            lo_hot[:, r, :], iota, p_lo[:, k, t:t + 1], None, ALU.is_equal), free)
        q.do(engine, ln, lambda e, r=r, k=k, t=t: e.tensor_scalar(
            hi_hot[:, r, 0, :], iota[:, 0:STILES], p_hi[:, k, t:t + 1], num[:, t:t + 1], ALU.is_equal, ALU.mult))
        m = q.do(engine, ln, lambda e, r=r, k=k, t=t, w=w: e.tensor_scalar(
            hi_hot[:, r, 1, :], iota[:, 0:STILES], p_hi[:, k, t:t + 1], w[:, t:t + 1], ALU.is_equal, ALU.mult))
        mapped[n] = q.do("tensor", pe_r, lambda e, r=r, n=n: e.matmul(
            banks[2][:, 0:2 * STILES], lo_hot[:, r, :], hi_hot[:, r].rearrange("p a n -> p (a n)"),
            start=(n == 0), stop=(n == 2 * TILES - 1)), [m])
    chainm[0] = Mark(v_r.sem, v_r.count)
    rv(lambda e: e.tensor_scalar(empty, banks[2][:, 0:STILES], 0.5, None, ALU.is_lt), [mapped[2 * TILES - 1]])
    rv(lambda e: e.tensor_scalar(valid, spare, 1.0, None, ALU.add))
    rv(lambda e: e.tensor_scalar(empty, empty, valid, -1.0, ALU.mult, ALU.add))
    rv(lambda e: e.tensor_copy(slot_w, banks[2][:, STILES:2 * STILES]))
    m_slots = rv(lambda e: e.tensor_tensor(slot_tok, empty, banks[2][:, 0:STILES], ALU.add))

    mix_at = [0]

    def slab(n):
        mix_at[0] += n
        return big[:, mix_at[0] - n:mix_at[0]]

    W1r = slab(2 * KC * HID).rearrange("p (r k n) -> p r k n", r=2, k=KC)
    W2r = slab(2 * HC * DIM).rearrange("p (r h n) -> p r h n", r=2, h=HC)
    hT = slab(2 * HC * SLOT).rearrange("p (r h n) -> p r h n", r=2, h=HC)
    at[0] = 0
    routed = [m_slots, m_owner, Mark(pe_r.sem, pe_r.count)]
    XG = 3
    edge_mem = X.rearrange("p a b c -> p (a b c)")
    xg = edge_mem[:, 0:XG * 2 * DIM].rearrange("p (r n) -> p r n", r=XG)
    xT = edge_mem[:, XG * 2 * DIM:(XG + 2) * 2 * DIM].rearrange("p (r n) -> p r n", r=2)
    yo = part(2 * 2 * DIM).rearrange("p (r h n) -> p r h n", r=2, h=2)
    b1r = sb("b1r", [P, 2, HC])
    b2r = sb("b2r", [P, 2, DIM])
    wl, gl, ad = lines("w_load", 2), lines("gather", 2 * XG), line("row_add", 16)
    a_x, v_x2, pe_x = line("expert_act"), line("expert_dve"), line("expert_pe")
    ps_x, ps_h, ps_o = banks[0], banks[1:5], banks[5:7]
    ex = {}
    y_stored = [Mark(ys_l.sem, ys_l.count), m_pad]
    xn_stored = [nd["xs", t] for t in range(TILES - 3, TILES)] + [m_pad]

    def block_load(j):
        if j >= BLOCKS:
            return
        r = j % 2
        free = [ex.get(("y", j - 2)), ex.get(("gelu", j - 2)), ex.get(("bias", j - 2))]
        q.wait("sync", routed + done["weights"] + free)
        where = {}

        def first(e):
            where["v"] = e.value_load(owner_i[0:1, j:j + 1], min_val=0, max_val=EXPERTS - 1)
            return e.dma_start(W1r[:, r].rearrange("p k n -> p (k n)"),
                               w1g[bass.ds(where["v"], 1)].rearrange("o p n -> p (o n)"))

        q.do("sync", wl[r], first)
        q.do("sync", wl[r], lambda e: e.dma_start(
            b1r[:, r, :], b1g[bass.ds(where["v"], 1)].rearrange("o p n -> p (o n)")))
        q.do("sync", wl[r], lambda e: e.dma_start(
            b2r[:, r, :], b2[bass.ds(where["v"], 1)].rearrange("o n -> (o n)").partition_broadcast(P)))
        ex["w", j] = q.do("sync", wl[r], lambda e: e.dma_start(
            W2r[:, r], w2[bass.ds(where["v"], 1)].rearrange("o (h p) n -> p (o h) n", p=P)))

    def block_gather(j):
        if j >= BLOCKS:
            return
        for h in range(2):
            l, s = gl[(j % XG) * 2 + h], 2 * j + h
            ex["g", j, h] = q.do("gpsimd", l, lambda e, h=h, s=s: e.indirect_dma_start(
                xg[:, j % XG, h * DIM:(h + 1) * DIM], None, xn_rows,
                bass.IndirectOffsetOnAxis(ap=slot_tok[:, s:s + 1], axis=0), bounds_check=ROWS - 1, oob_is_err=True),
                routed + xn_stored + [ex.get(("T", j - XG))])

    def block_turn(j):
        if j >= BLOCKS:
            return
        for k in range(KC):
            for h in range(2):
                m = q.do("tensor", pe_x, lambda e, k=k, h=h: e.transpose(
                    ps_x[:, k * SLOT + h * P:k * SLOT + (h + 1) * P],
                    xg[:, j % XG, h * DIM + k * P:h * DIM + (k + 1) * P], ident),
                    [ex["g", j, h], ex.get(("xT", j - 1))] + routed)
        ex["T", j] = m
        ex["xT", j] = q.do("vector", v_x2, lambda e: e.tensor_copy(xT[:, j % 2, :], ps_x), [m, ex.get(("up", j - 2))])

    def block_up(j):
        r = j % 2
        for h in range(HC):
            ps = ps_h[h % 4][:, 0:SLOT]
            for k in range(KC):
                m = q.do("tensor", pe_x, lambda e, k=k, h=h, ps=ps: e.matmul(
                    ps, W1r[:, r, k, h * P:(h + 1) * P], xT[:, r, k * SLOT:(k + 1) * SLOT],
                    start=(k == 0), stop=(k == KC - 1)),
                    [ex["w", j], ex["xT", j], ex.get(("g", j, "h", h - 4)) if h >= 4 else ex.get(("g", j - 1, "h", h + 4))])
            ex["g", j, "h", h] = q.do("scalar", a_x, lambda e, h=h, ps=ps: e.activation(
                hT[:, r, h, :], ps, ACT.Gelu, bias=b1r[:, r, h:h + 1]), [m, ex.get(("y", j - 2)), ex["w", j]])
        ex["up", j] = m
        ex["gelu", j] = ex["g", j, "h", HC - 1]

    def block_down(j):
        r = j % 2
        for s in range(2):
            ps = ps_o[s][:, 0:DIM]
            for h in range(HC):
                m = q.do("tensor", pe_x, lambda e, s=s, h=h, ps=ps: e.matmul(
                    ps, hT[:, r, h, s * P:(s + 1) * P], W2r[:, r, h, :], start=(h == 0), stop=(h == HC - 1)),
                    [ex["g", j, "h", h], ex.get(("o", j - 1, s))])
            ex["y", j] = m
            ex["o", j, s] = q.do("vector", v_x2, lambda e, s=s, ps=ps: e.tensor_tensor(
                yo[:, r, s, :], ps, b2r[:, r, :], ALU.add), [m, ex.get(("add", j - 2))] + routed)
            m = q.do("vector", v_x2, lambda e, s=s: e.tensor_scalar(
                yo[:, r, s, :], yo[:, r, s, :], slot_w[:, 2 * j + s:2 * j + s + 1], None, ALU.mult), [ex["o", j, s]])
            ex["add", j] = q.do("gpsimd", ad, lambda e, s=s: e.indirect_dma_start(
                y_rows, bass.IndirectOffsetOnAxis(ap=slot_tok[:, 2 * j + s:2 * j + s + 1], axis=0), yo[:, r, s, :], None,
                compute_op=ALU.add, bounds_check=ROWS - 1, oob_is_err=True),
                [m, Mark(ad.sem, ad.count) if ad.count else None] + y_stored)
        ex["bias", j] = ex["o", j, 1]

    block_load(0)
    block_load(1)
    block_gather(0)
    block_gather(1)
    block_turn(0)
    for j in range(BLOCKS):
        block_up(j)
        block_turn(j + 1)
        block_down(j)
        block_load(j + 2)
        block_gather(j + 2)

    fin = line("result", 16)
    m = q.do("sync", fin, lambda e: e.dma_start(out, y_rows[0:NODES, :]), [ex["add", BLOCKS - 1]])
    q.wait("sync", [m])

    with ctx:
        block = ctx.enter_context(nc.Block())

        @block.tensor
        def _(e):
            q.play("tensor", e)

        @block.vector
        def _(e):
            q.play("vector", e)

        @block.scalar
        def _(e):
            q.play("scalar", e)

        @block.gpsimd
        def _(e):
            q.play("gpsimd", e)

        @block.sync
        def _(e):
            q.play("sync", e)


INPUTS = ["x", "src", "dst", "edge_attr_128", "node_vec1", "node_vec1_n2", "L0_gnn_z_in", "L0_gnn_z_out",
          "L0_gnn_W_cent", "L0_gnn_b_cent", "L0_gnn_W_vor", "L0_gnn_b_vor", "L0_gnn_W_sum", "L0_gnn_b_sum",
          "L0_mix_w_qkv", "L0_mix_w_out", "L0_mix_b_out", "L0_ffn_Wr", "L0_ffn_br", "L0_ffn_ln_g", "L0_ffn_ln_b",
          "L0_ffn_W1", "L0_ffn_b1", "L0_ffn_W2", "L0_ffn_b2"]


def kernel(**inputs):
    import concourse.bacc as bacc
    from concourse.bass_utils import run_bass_kernel_spmd

    nc = bacc.Bacc("TRN2", target_bir_lowering=False, num_devices=1)
    arrays, args = {}, []
    for name in INPUTS:
        a = np.ascontiguousarray(inputs[name])
        arrays[name] = a
        args.append(nc.dram_tensor(name, a.shape, mybir.dt.from_np(a.dtype), kind="ExternalInput").ap())
    result = nc.dram_tensor("result", (NODES, DIM), F32, kind="ExternalOutput").ap()
    build_layer(nc, *args, result)
    r = run_bass_kernel_spmd(nc, [arrays], core_ids=[0])
    return r.results[0]["result"]
```

```python
from contextlib import ExitStack

import numpy as np

import concourse.bass as bass
from concourse import mybir

F32, I32, BF16, F16 = mybir.dt.float32, mybir.dt.int32, mybir.dt.bfloat16, mybir.dt.float16
ALU, ACT, AX = mybir.AluOpType, mybir.ActivationFunctionType, mybir.AxisListType

P = 128
NODES, DIM, EDGES, EDIM = 6250, 256, 100000, 128
KC = DIM // P
TILES = -(-NODES // P)
LAST = NODES - (TILES - 1) * P
HEADS, DH = 8, 64
INNER = HEADS * DH
PAIRS = INNER // P
EXPERTS, HID = 8, 1024
HC = HID // P
DEG = 512
EPS = 1e-5

ECOLS = EDGES // P
EREST = EDGES - ECOLS * P
ETILES = ECOLS + 1
GROUP = 3
GROUPS = -(-ETILES // GROUP)
LOAD = 6
XRING, SRING, ORING = 4, 3, 6
TABLES = 4
XW = EDIM + 2
RW = EDIM + 1
ROWS = (TILES + 1) * P
ZERO = 645
IDLOAD = 12

SLOT = 256
BLOCKS = 2 * NODES // SLOT + EXPERTS
STILES = BLOCKS * SLOT // P

TOP = 14
XSCALE = 256.0
BIAS = 127
META = HC + 3


class Mark:

    def __init__(self, sem, value):
        self.sem, self.value = sem, value


class Line:

    def __init__(self, sem, step=1):
        self.sem, self.step, self.count = sem, step, 0

    def next(self):
        self.count += self.step
        return Mark(self.sem, self.count)


class Script:

    def __init__(self):
        self.items = {e: [] for e in ("tensor", "vector", "scalar", "gpsimd", "sync")}
        self.seen = {e: {} for e in self.items}

    def wait(self, engine, marks):
        for m in marks:
            if m is not None and self.seen[engine].get(m.sem, 0) < m.value:
                self.seen[engine][m.sem] = m.value
                self.items[engine].append(("wait", m))

    def do(self, engine, line, step, after=()):
        self.wait(engine, after)
        m = line.next() if line is not None else None
        self.items[engine].append(("do", step, line, m))
        return m

    def skewed(self, n, every, stages):
        for tick in range((n - 1) * every + len(stages)):
            for k in range(len(stages) - 1, -1, -1):
                if (tick - k) % every == 0 and 0 <= (tick - k) // every < n:
                    stages[k]((tick - k) // every)
            yield

    def play(self, engine, handle):
        for item in self.items[engine]:
            if item[0] == "wait":
                handle.wait_ge(item[1].sem, item[1].value)
            else:
                ins = item[1](handle)
                if item[2] is not None:
                    ins.then_inc(item[2].sem, item[2].step)


def build_layer(nc, x, src, dst, edge_attr, vor, cent, z_in, z_out, w_cent, b_cent, w_vor, b_vor,
                w_sum, b_sum, w_qkv, w_out, b_out, wr, br, ln_g, ln_b, w1, b1, w2, b2, out):
    ctx = ExitStack()

    def sb(name, shape, dt=F32):
        return ctx.enter_context(nc.sbuf_tensor(name, shape, dt)).ap()

    def line(name, step=1):
        return Line(ctx.enter_context(nc.semaphore(name)), step)

    def lines(name, n, step=16):
        return [line(f"{name}{i}", step) for i in range(n)]

    q = Script()
    banks = [ctx.enter_context(nc.psum_tensor(f"bank{i}", [P, 512], F32)).ap() for i in range(8)]

    table = [nc.dram_tensor(f"node_table{i}", (ROWS, RW), F32, kind="Internal").ap() for i in range(TABLES)]
    xn_rows = nc.dram_tensor("xn_rows", (ROWS, 2 * DIM), F16, kind="Internal").ap()
    y_rows = nc.dram_tensor("y_rows", (ROWS, DIM), F32, kind="Internal").ap()
    w_parts = [nc.dram_tensor(f"w{i}_parts", (EXPERTS, P, 2 * KC * HID), F16, kind="Internal").ap() for i in (1, 2)]
    meta = nc.dram_tensor("expert_meta", (EXPERTS, P, META), F32, kind="Internal").ap()
    id_rows = nc.dram_tensor("id_rows", (2, ETILES * P), BF16, kind="Internal").ap()

    g_c, v_c, d_c = line("const_pool"), line("const_dve"), line("const_dma", 16)
    ident = sb("ident", [P, P])
    identb = sb("identb", [P, P], BF16)
    before = sb("before", [P, P])
    ones = sb("ones", [P, P])
    onesb = sb("onesb", [P, P], BF16)
    identh = sb("identh", [P, P], F16)
    lane_i = sb("lane_i", [P, 1], I32)
    lane = sb("lane", [P, 1])
    spare = sb("spare", [P, 1])
    spare_i = sb("spare_i", [P, 1], I32)
    pow_i = sb("pow_i", [P, 2], I32)
    iota_i = sb("iota_i", [P, P], I32)
    iota = sb("iota", [P, P])
    iotab = sb("iotab", [P, P], BF16)
    eps_t = sb("eps_t", [P, 1])
    thresh = sb("thresh", [P, 1])
    zeros = sb("zeros", [P, ZERO])

    def pool(fn, after=()):
        return q.do("gpsimd", g_c, fn, after)

    def dve(fn, after=()):
        return q.do("vector", v_c, fn, after)

    pool(lambda e: e.memset(identb, 0.0))
    pool(lambda e: e.memset(identh, 0.0))
    m = pool(lambda e: e.memset(ident, 0.0))
    for t in (identb, identh, ident):
        pool(lambda e, t=t: e.affine_select(out=t, in_=t, compare_op=ALU.not_equal, fill=1.0, base=0,
                                            pattern=[[-1, P]], channel_multiplier=1), [m])
    m = pool(lambda e: e.memset(before, 0.0))
    pool(lambda e: e.affine_select(out=before, in_=before, compare_op=ALU.is_ge, fill=1.0, base=0,
                                   pattern=[[-1, P]], channel_multiplier=1), [m])
    pool(lambda e: e.iota(lane_i, pattern=[[0, 1]], base=0, channel_multiplier=1))
    pool(lambda e: e.iota(spare_i, pattern=[[0, 1]], base=NODES, channel_multiplier=1))
    pool(lambda e: e.iota(pow_i, pattern=[[0, 2]], base=127 + 63, channel_multiplier=-1))
    m_iota = pool(lambda e: e.iota(iota_i, pattern=[[1, P]], base=0, channel_multiplier=0))
    m_zero = dve(lambda e: e.memset(zeros, 0.0))
    dve(lambda e: e.memset(ones, 1.0))
    dve(lambda e: e.memset(onesb, 1.0))
    dve(lambda e: e.memset(eps_t, EPS))
    dve(lambda e: e.tensor_copy(lane, lane_i), [m_iota])
    m_spare = dve(lambda e: e.tensor_copy(spare, spare_i))
    dve(lambda e: e.tensor_copy(iota, iota_i))
    dve(lambda e: e.tensor_copy(iotab, iota_i))
    m = dve(lambda e: e.tensor_scalar(pow_i, pow_i, 23, None, ALU.logical_shift_left))
    m_const = dve(lambda e: e.tensor_scalar(thresh, pow_i[:, 0:1].bitcast(F32), 2.5, None, ALU.mult), [m])
    powers = pow_i[:, 0:1].bitcast(F32)

    tz = lines("table_zero", TABLES)
    m_tz = []
    flat = ROWS * RW // P
    rep = flat // ZERO
    for i in range(TABLES):
        m_tz.append(q.do("scalar", tz[i], lambda e, i=i: e.dma_start(
            table[i].rearrange("(p a) w -> p (a w)", p=P).rearrange("p (r c) -> p r c", r=rep),
            zeros.unsqueeze(1).to_broadcast([P, rep, ZERO])), [m_zero]))
    pad_rows = ROWS - NODES
    zr = line("pad_zero", 16)
    for rows in (xn_rows, y_rows):
        for a in range(NODES, ROWS, 75):
            m_pad = q.do("scalar", zr, lambda e, rows=rows, a=a: e.dma_start(
                rows[a:a + 75, :], zeros[0:75, 0:DIM] if rows is y_rows else zeros[0:75, 0:DIM].bitcast(F16)))

    idx_d, v_i = line("index_dma", 16), line("index_dve")
    big = sb("big", [P, TILES * DIM])
    src_i = big[:, 5000:5000 + ETILES].bitcast(I32)
    tmp_i = big[:, 6000:6000 + ETILES].bitcast(I32)
    src_f = sb("src_f", [P, ETILES])
    to_spare = sb("to_spare", [P, ETILES])
    src_hi = big[:, 7000:7000 + ETILES // 2].bitcast(BF16)
    src_lo = big[:, 7500:7500 + ETILES // 2].bitcast(BF16)
    dst_hi = sb("dst_hi", [P, ETILES], BF16)
    dst_lo = sb("dst_lo", [P, ETILES], BF16)

    def idv(fn, after=()):
        return q.do("vector", v_i, fn, after)

    def load_ids(ids):
        q.do("sync", idx_d, lambda e: e.dma_start(src_i[:, 0:ECOLS], ids[0:ECOLS * P].rearrange("(p c) -> p c", c=ECOLS)))
        return q.do("sync", idx_d, lambda e: e.dma_start(
            src_i[0:EREST, ECOLS:ETILES], ids[ECOLS * P:EDGES].rearrange("(p c) -> p c", c=1)))

    m = idv(lambda e: e.tensor_copy(src_i[:, ECOLS:ETILES], spare_i), [m_iota])
    q.wait("sync", [m])
    m = load_ids(src)
    m1 = idv(lambda e: e.tensor_copy(src_f, src_i), [m])
    idv(lambda e: e.tensor_scalar(to_spare, src_f, -1.0, spare, ALU.mult, ALU.add), [m1, m_spare])
    m2 = idv(lambda e: e.tensor_scalar(tmp_i, src_i, 7, None, ALU.arith_shift_right), [m])
    m3 = idv(lambda e: e.tensor_scalar(src_hi, tmp_i, 128.0, None, ALU.mult), [m2])
    m4 = idv(lambda e: e.tensor_scalar(tmp_i, src_i, 127, None, ALU.bitwise_and), [m3])
    m_src = idv(lambda e: e.tensor_copy(src_lo, tmp_i), [m4])
    m = idv(lambda e: e.memset(src_i[:, ECOLS:ETILES], TILES * P), [m_src])
    q.wait("sync", [m])
    m = load_ids(dst)
    m2 = idv(lambda e: e.tensor_scalar(tmp_i, src_i, 7, None, ALU.arith_shift_right), [m])
    m3 = idv(lambda e: e.tensor_copy(dst_hi, tmp_i), [m2])
    m4 = idv(lambda e: e.tensor_scalar(tmp_i, src_i, 127, None, ALU.bitwise_and), [m3])
    m_dst = idv(lambda e: e.tensor_copy(dst_lo, tmp_i), [m4])

    CH = -(-ETILES // P)
    id_t = big[:, 8000:8000 + CH * P].bitcast(BF16).rearrange("p (q i n) -> p q i n", q=CH, i=2)
    id_l, pe_i, a_i = line("id_rows_store", 16), line("index_pe"), line("index_act")
    for c in range(CH):
        n = min(P, ETILES - c * P)
        bank = banks[c].bitcast(BF16)
        for i, v in enumerate((src_hi, src_lo)):
            m = q.do("tensor", pe_i, lambda e, c=c, n=n, i=i, v=v, bank=bank: e.transpose(
                bank[0:n, i * P:(i + 1) * P], v[:, c * P:c * P + n], identb), [m_src, m_const])
        m = q.do("scalar", a_i, lambda e, c=c, n=n, bank=bank: e.copy(
            id_t[0:n, c].rearrange("p i n -> p (i n)"), bank[0:n, 0:2 * P]), [m])
        for i in range(2):
            m_ids = q.do("sync", id_l, lambda e, c=c, n=n, i=i: e.dma_start(
                id_rows[i:i + 1, c * P * P:(c * P + n) * P].rearrange("a (c n) -> (a c) n", n=P), id_t[0:n, c, i, :]), [m])

    X = sb("edge_rows", [P, XRING, LOAD, XW])
    S = sb("same_node", [P, SRING, GROUP * P])
    O = sb("edge_sums", [P, ORING, GROUP, XW])
    IDR = sb("node_numbers", [P, 2, IDLOAD * P], BF16)
    dup = sb("dup", [P, ORING, GROUP])
    row_i = sb("row_i", [P, ORING, GROUP], I32)
    x_l, t_l, i_l = lines("edge_load", XRING), lines("table_add", TABLES), lines("ids_load", 2)
    pe_e, v_e, a_e = line("edge_pe"), line("edge_dve"), line("edge_act")
    ps_src, ps_sum = banks[0:2], banks[2]
    v_x = line("edge_const")
    m_idz = q.do("vector", v_x, lambda e: e.memset(IDR, 0.0))
    q.do("vector", v_x, lambda e: e.memset(X[:, :, :, EDIM:EDIM + 1], 1.0))
    m_xc = q.do("vector", v_x, lambda e: e.tensor_copy(
        X[:, :, :, EDIM + 1:XW].rearrange("p a b c -> p (a b c)"), powers.to_broadcast([P, XRING * LOAD])), [m_const])
    loaded, id_loaded, srcs, sames, sums, evac, rowed, added = {}, {}, {}, {}, {}, {}, {}, {}

    def group_tiles(g):
        return list(range(g * GROUP, min(ETILES, (g + 1) * GROUP)))

    def load_edges(k):
        if k * LOAD >= ETILES:
            return
        free = [sums[(k - XRING + 1) * LOAD // GROUP - 1]] if k >= XRING else [m_xc]
        lo, hi = k * LOAD, min((k + 1) * LOAD, ECOLS)
        b = k % XRING
        if (k + 1) * LOAD > ECOLS:
            m = q.do("vector", v_x, lambda e: e.memset(X[:, b, ECOLS - lo, 0:EDIM], 0.0), free)
            q.do("sync", x_l[b], lambda e: e.dma_start(
                X[0:EREST, b, ECOLS - lo, 0:EDIM], edge_attr[ECOLS * P:EDGES, :]), [m])
        rows = edge_attr[0:ECOLS * P, :].rearrange("(p c) w -> p c w", c=ECOLS)
        loaded[k] = q.do("sync", x_l[b], lambda e: e.dma_start(X[:, b, 0:hi - lo, 0:EDIM], rows[:, lo:hi, :]), free)

    def load_ids_rows(k):
        lo, hi, b = k * IDLOAD * P, min((k + 1) * IDLOAD, ETILES) * P, k % 2
        if lo < hi:
            free = [srcs[(k - 1) * IDLOAD // GROUP - 1]] if k >= 2 else [m_idz]
            id_loaded[k] = q.do("sync", i_l[b], lambda e: e.dma_start(IDR[0:2, b, 0:hi - lo], id_rows[:, lo:hi]),
                                free + [m_ids])

    def edge_match(g):
        c0, n = g * GROUP, len(group_tiles(g))
        k, at_ = c0 // IDLOAD, c0 % IDLOAD * P
        srcs[g] = q.do("tensor", pe_e, lambda e: e.matmul(
            ps_src[g % 2][:, 0:n * P], onesb, IDR[:, k % 2, at_:at_ + n * P], start=True, stop=True),
            [id_loaded[k], sames.get(g - 2), m_const])

    def edge_same(g):
        c0, n = g * GROUP, len(group_tiles(g))
        sames[g] = q.do("vector", v_e, lambda e: e.tensor_tensor(
            S[:, g % SRING, 0:n * P].rearrange("p (a b) -> p a b", a=n),
            ps_src[g % 2][:, 0:n * P].rearrange("p (a b) -> p a b", a=n),
            src_f[:, c0:c0 + n].unsqueeze(2).to_broadcast([P, n, P]), ALU.is_equal),
            [srcs[g], m_src, sums.get(g - SRING)])

    def edge_sum(g):
        cs = group_tiles(g)
        for i, c in enumerate(cs):
            k = c // LOAD
            sums[g] = q.do("tensor", pe_e, lambda e, i=i, c=c, k=k: e.matmul(
                ps_sum[:, i * XW:(i + 1) * XW], S[:, g % SRING, i * P:(i + 1) * P], X[:, k % XRING, c % LOAD, :],
                start=True, stop=True), [sames[g], loaded[k], evac.get(g - 1)])
        n, o = len(cs), g % ORING
        free = [added[c] for c in group_tiles(g - ORING)] if g >= ORING else []
        evac[g] = q.do("scalar", a_e, lambda e: e.copy(
            O[:, o, 0:n, :], ps_sum[:, 0:n * XW].rearrange("p (a b) -> p a b", a=n)), [sums[g]] + free)

    def edge_rows_of(g):
        c0, n, o = g * GROUP, len(group_tiles(g)), g % ORING
        free = [added[c] for c in group_tiles(g - ORING)] if g >= ORING else []
        m = q.do("vector", v_e, lambda e: e.scalar_tensor_tensor(
            dup[:, o, 0:n], O[:, o, 0:n, RW], thresh, to_spare[:, c0:c0 + n], ALU.is_gt, ALU.mult), [evac[g]])
        rowed[g] = q.do("vector", v_e, lambda e: e.tensor_tensor(
            row_i[:, o, 0:n], dup[:, o, 0:n], src_f[:, c0:c0 + n], ALU.add), [m] + free)

    def edge_add(g):
        o = g % ORING
        for i, c in enumerate(group_tiles(g)):
            t = c % TABLES
            added[c] = q.do("gpsimd", t_l[t], lambda e, i=i, t=t: e.indirect_dma_start(
                table[t], bass.IndirectOffsetOnAxis(ap=row_i[:, o, i:i + 1], axis=0), O[:, o, i, 0:RW], None,
                compute_op=ALU.add, bounds_check=ROWS - 1, oob_is_err=True),
                [evac[g], rowed[g], added.get(c - TABLES, m_tz[t])])

    hotA = sb("hotA", [P, 2, GROUP * TILES], BF16)
    hotB = sb("hotB", [P, 2, GROUP * P], BF16)
    v_h, pe_h = line("degree_dve"), line("degree_pe")
    ps_deg = banks[4]
    in_deg = sb("in_deg", [P, TILES], I32)
    done, hots = {}, {}

    def degree_hot(b):
        lo, n, r = b * GROUP, len(group_tiles(b)), b % 2
        q.do("vector", v_h, lambda e: e.tensor_tensor(
            hotA[:, r, 0:n * TILES].rearrange("p (a b) -> p a b", a=n),
            iotab[:, 0:TILES].unsqueeze(1).to_broadcast([P, n, TILES]),
            dst_hi[:, lo:lo + n].unsqueeze(2).to_broadcast([P, n, TILES]), ALU.is_equal),
            [m_dst, m_const, done.get(("deg", b - 2))])
        hots[b] = q.do("vector", v_h, lambda e: e.tensor_tensor(
            hotB[:, r, 0:n * P].rearrange("p (a b) -> p a b", a=n),
            iotab.unsqueeze(1).to_broadcast([P, n, P]),
            dst_lo[:, lo:lo + n].unsqueeze(2).to_broadcast([P, n, P]), ALU.is_equal))

    def degree_sum(b):
        r = b % 2
        for i, c in enumerate(group_tiles(b)):
            done["deg", b] = q.do("tensor", pe_h, lambda e, i=i, c=c: e.matmul(
                ps_deg[:, 0:TILES], hotB[:, r, i * P:(i + 1) * P], hotA[:, r, i * TILES:(i + 1) * TILES],
                start=(c == 0), stop=(c == ETILES - 1)), [hots[b]])

    d_m, v_m, a_m, pe_m = line("mix_dma", 16), line("mix_dve"), line("mix_act"), line("mix_pe")
    state = sb("state", [P, TILES, DIM])
    xnT = big.rearrange("p (t k n) -> p t k n", t=TILES, k=KC)
    mixw = sb("mixw", [P, 8192])
    at = [0]

    def part(n):
        at[0] += n
        return mixw[:, at[0] - n:at[0]]

    wqkv = part(KC * 3 * INNER).rearrange("p (k n) -> p k n", k=KC)
    wout = part(PAIRS * DIM).rearrange("p (j n) -> p j n", j=PAIRS)
    squares = part(2 * INNER)
    ks = part(INNER)
    k_raw = part(2 * INNER).rearrange("p (r n) -> p r n", r=2)
    vs = part(2 * INNER).rearrange("p (r n) -> p r n", r=2)
    xn = part(2 * DIM).rearrange("p (r n) -> p r n", r=2)
    folded = squares.rearrange("p (j n) -> p j n", j=PAIRS)
    wqT = k_raw.rearrange("p r n -> p (r n)").rearrange("p (j n) -> p j n", j=PAIRS)
    dotsT = ks.rearrange("p (j n) -> p j n", j=PAIRS)
    term = mixw[:, 0:3 * 2 * DIM].rearrange("p (r i n) -> p r i n", r=3, i=2)
    mq = sb("mq", [P, KC, DIM])
    mv = sb("mv", [P, TILES, 2])
    stats = sb("stats", [P, 2, 6])
    rstd = sb("rstd", [P, TILES])
    wmean = sb("wmean", [P, KC * 2 * HEADS])
    ss = sb("ss", [P, 2 * HEADS])
    sd = sb("sd", [P, 2 * HEADS])
    rkv = sb("rkv", [P, HEADS])
    ps_xT, ps_dots, ps_kv = banks[3], banks[5], banks[6:8]
    vec = {n: sb("bc_" + n, [P, DIM]) for n in ("w_cent", "b_cent", "w_vor", "b_vor", "b_out", "b_sum")}
    node_v = sb("node_v", [P, 2, TILES])
    node_r = big[:, 3000:3000 + 2 * P].rearrange("p (i n) -> p i n", i=2)
    x_d = lines("x_load", 7)
    wsum = sb("wsum", [P, DIM])
    wr_t = sb("wr_t", [P, KC, EXPERTS])
    br_t = sb("br_t", [P, EXPERTS])

    def mixv(fn, after=()):
        return q.do("vector", v_m, fn, after)

    def mixa(fn, after=()):
        return q.do("scalar", a_m, fn, after)

    def mixp(fn, after=()):
        return q.do("tensor", pe_m, fn, after)

    def load_small():
        m = q.do("vector", v_m, lambda e: e.memset(state[:, TILES - 1, :], 0.0))
        m = q.do("vector", v_m, lambda e: e.memset(node_r, 0.0))
        q.wait("scalar", [m])
        per = TILES // 7
        for i in range(7):
            lo, hi = i * per, min((i + 1) * per, TILES - 1)
            q.do("scalar", x_d[i], lambda e, lo=lo, hi=hi: e.dma_start(
                state[:, lo:hi, :], x[lo * P:hi * P, :].rearrange("(t p) n -> p t n", p=P)))
        done["x"] = [Mark(l.sem, 16) for l in x_d]
        done["x"][6] = q.do("scalar", x_d[6], lambda e: e.dma_start(state[0:LAST, TILES - 1, :], x[(TILES - 1) * P:NODES, :]))
        q.do("scalar", d_m, lambda e: e.dma_start(wqkv, w_qkv.rearrange("(k p) n -> p k n", p=P)))
        q.do("scalar", d_m, lambda e: e.dma_start(wout, w_out.rearrange("(j p) n -> p j n", p=P)))
        for n, v in (("w_cent", w_cent[0]), ("b_cent", b_cent), ("w_vor", w_vor[0]), ("b_vor", b_vor),
                     ("b_out", b_out), ("b_sum", b_sum)):
            q.do("scalar", d_m, lambda e, n=n, v=v: e.dma_start(vec[n], v.partition_broadcast(P)))
        for i, v in enumerate((cent, vor)):
            q.do("scalar", d_m, lambda e, i=i, v=v: e.dma_start(
                node_r[0:TILES - 1, i, :], v[0:(TILES - 1) * P, :].rearrange("(t p) o -> t (p o)", p=P)))
            q.do("scalar", d_m, lambda e, i=i, v=v: e.dma_start(
                node_r[TILES - 1:TILES, i, 0:LAST], v[(TILES - 1) * P:NODES, :].rearrange("(a p) o -> a (p o)", a=1)))
        q.do("scalar", d_m, lambda e: e.dma_start(wsum, w_sum))
        q.do("scalar", d_m, lambda e: e.dma_start(wr_t, wr.rearrange("(k p) n -> p k n", p=P)))
        done["small"] = q.do("scalar", d_m, lambda e: e.dma_start(br_t, br.partition_broadcast(P)))

    def norm_stats(queue, rows, stat, to, after):
        m = queue(lambda e: e.bn_stats(stat, rows), after)
        return queue(lambda e: e.bn_aggr(to, stat), [m])

    def norm_steps():
        per = TILES // 7
        for t in range(TILES):
            m = norm_stats(mixv, state[:, t, :], stats[:, t % 2, :], mv[:, t, :], [done["x"][min(t // per, 6)]])
            if t % 2:
                yield
        m = mixa(lambda e: e.activation(rstd, mv[:, :, 1], ACT.Sqrt, bias=eps_t), [m])
        done["rstd"] = mixv(lambda e: e.reciprocal(rstd, rstd), [m])
        for i in range(2):
            m = mixp(lambda e, i=i: e.transpose(ps_kv[1][:, i * P:i * P + TILES], node_r[0:TILES, i, :],
                                                ident[0:TILES, 0:TILES]), [done["small"], done["b1"], m_const])
        done["node_v"] = mixv(lambda e: e.tensor_copy(
            node_v, ps_kv[1][:, 0:2 * P].rearrange("p (i n) -> p i n", i=2)[:, :, 0:TILES]), [m])
        for k in range(KC):
            m = mixv(lambda e, k=k: e.reduce_sum(wmean[:, k * 2 * HEADS:(k + 1) * 2 * HEADS],
                                                 kvw[:, k, :].rearrange("p (h d) -> p h d", d=DH), AX.X), [done["small"]])
        m = mixv(lambda e: e.tensor_scalar(wmean, wmean, 1.0 / DH, None, ALU.mult), [m])
        for k in range(KC):
            wk = kvw[:, k, :].rearrange("p (h d) -> p h d", d=DH)
            done["kvw"] = mixv(lambda e, k=k, wk=wk: e.tensor_tensor(
                wk, wk, wmean[:, k * 2 * HEADS:(k + 1) * 2 * HEADS].unsqueeze(2).to_broadcast([P, 2 * HEADS, DH]),
                ALU.subtract), [m])
        yield

    kvw = wqkv[:, :, INNER:3 * INNER]
    mx = {}

    def mix_norm(t):
        r = t % 2
        m = mixv(lambda e: e.tensor_scalar(xn[:, r, :], state[:, t, :], mv[:, t, 0:1], rstd[:, t:t + 1],
                                           ALU.subtract, ALU.mult), [done["rstd"], mx.get(("turn", t - 2))])
        mx["xn", t] = m
        mixv(lambda e: e.tensor_tensor(state[:, t, :], state[:, t, :], xn[:, r, :], ALU.add), [m])

    def mix_turn(t):
        for k in range(KC):
            mx["turn", t] = mixp(lambda e, k=k: e.transpose(
                ps_xT[:, k * P:(k + 1) * P], xn[:, t % 2, k * P:(k + 1) * P], ident),
                [mx["xn", t], mx.get(("xT", t - 1)), m_const])

    def mix_keep(t):
        mx["xT", t] = mixa(lambda e: e.copy(big[:, t * DIM:(t + 1) * DIM], ps_xT[:, 0:DIM]),
                           [mx["turn", t], m_ids, m_dst, done["node_v"]] + (done["weights"] if t >= W_AT // DIM else done["pass1"]))

    def mix_half(h):
        def product(t):
            for k in range(KC):
                mx["kv", h, t] = mixp(lambda e, k=k: e.matmul(
                    ps_kv[h], xnT[:, t, k, :], kvw[:, k, h * INNER:(h + 1) * INNER],
                    start=(k == 0), stop=(k == KC - 1)),
                    [mx["xT", t], done["kvw"], mx.get(("out", h, t - 1)), done["node_v"]])
        return product

    def mix_out(h):
        def out_of(t):
            mixa(lambda e: e.activation(squares[:, h * INNER:(h + 1) * INNER], ps_kv[h], ACT.Square),
                 [mx["kv", h, t], mx.get(("ss", t - 1))])
            mx["out", h, t] = mixa(lambda e: e.copy((k_raw, vs)[h][:, t % 2, :], ps_kv[h]),
                                   [mx.get(("dots", t - 2)), mx.get(("ks", t - 2))])
        return out_of

    def mix_squares(t):
        mx["ss", t] = mixv(lambda e: e.reduce_sum(ss, squares.rearrange("p (h d) -> p h d", d=DH), AX.X),
                           [mx["out", 1, t], mx.get(("sd", t - 1))])

    def mix_sd(t):
        mx["sd", t] = mixa(lambda e: e.activation(sd, ss, ACT.Sqrt, bias=eps_t, scale=1.0 / DH),
                           [mx["ss", t], mx.get(("ks", t - 1))])

    def mix_keys(t):
        m = mixv(lambda e: e.tensor_tensor(rkv, sd[:, 0:HEADS], sd[:, HEADS:2 * HEADS], ALU.mult), [mx["sd", t]])
        m = mixv(lambda e: e.reciprocal(rkv, rkv), [m])
        mx["ks", t] = mixv(lambda e: e.tensor_tensor(
            ks.rearrange("p (h d) -> p h d", d=DH), k_raw[:, t % 2, :].rearrange("p (h d) -> p h d", d=DH),
            rkv.unsqueeze(2).to_broadcast([P, HEADS, DH]), ALU.mult), [m, mx.get(("dots", t - 1))])

    def mix_dots(t):
        for j in range(PAIRS):
            mx["dots", t] = mixp(lambda e, j=j: e.matmul(
                ps_dots[:, j * P:(j + 1) * P], vs[:, t % 2, j * P:(j + 1) * P], ks[:, j * P:(j + 1) * P],
                start=(t == 0 and j == 0), stop=(t == TILES - 1 and j == PAIRS - 1), skip_group_check=True),
                [mx["ks", t], mx["out", 1, t]])

    def fold_steps():
        last = TILES - 1
        for j in range(PAIRS):
            for k in range(KC):
                c = j * KC + k
                m = mixp(lambda e, j=j, k=k, c=c: e.transpose(
                    ps_kv[c // 4][:, c % 4 * P:(c % 4 + 1) * P], wqkv[:, k, j * P:(j + 1) * P], ident),
                    [mx["out", 0, last], mx["out", 1, last]])
        for h in range(2):
            ma = mixa(lambda e, h=h: e.copy(wqT[:, 2 * h:2 * h + 2, :].rearrange("p a b -> p (a b)"), ps_kv[h]), [m, mx["ks", last]])
        m = mixv(lambda e: e.memset(dotsT, 0.0), [mx["dots", last]])
        for s in range(2):
            w = slice(s * DH, (s + 1) * DH)
            md = mixv(lambda e, w=w: e.tensor_scalar(
                dotsT[w, :, w], ps_dots[w, :].rearrange("p (j n) -> p j n", j=PAIRS)[:, :, w], 1.0 / NODES, None, ALU.mult),
                [m, mx["dots", last]])
        yield
        for j in range(PAIRS):
            m = mixp(lambda e, j=j: e.matmul(ps_kv[j // 2][:, j % 2 * DIM:(j % 2 + 1) * DIM], dotsT[:, j, :],
                                             wout[:, j, :], start=True, stop=True), [md, ma])
        for h in range(2):
            m = mixa(lambda e, h=h: e.copy(folded[:, 2 * h:2 * h + 2, :].rearrange("p a b -> p (a b)"), ps_kv[h]), [m, mx["ss", last]])
        yield
        for k in range(KC):
            for j in range(PAIRS):
                mp = mixp(lambda e, j=j, k=k: e.matmul(
                    ps_kv[k][:, 0:DIM], wqT[:, j, k * P:(k + 1) * P], folded[:, j, :],
                    start=(j == 0), stop=(j == PAIRS - 1)), [m])
        for k in range(KC):
            done["mq"] = mixa(lambda e, k=k: e.copy(mq[:, k, :], ps_kv[k][:, 0:DIM]), [mp])
        yield

    def rest_products(t):
        for k in range(KC):
            mx["rest", t] = mixp(lambda e, k=k: e.matmul(
                ps_kv[t % 2][:, 0:DIM], xnT[:, t, k, :], mq[:, k, :], start=(k == 0), stop=(k == KC - 1)),
                [done["mq"], mx.get(("rest added", t - 2))])
        for i, n in enumerate(("cent", "vor")):
            mx["lin", t] = mixv(lambda e, i=i, n=n: e.scalar_tensor_tensor(
                term[:, t % 3, i, :], vec["w_" + n], node_v[:, i, t:t + 1], vec["b_" + n], ALU.mult, ALU.add),
                [mx.get(("state", t - 3)), done["node_v"], done["mq"]])

    def rest_sigmoid(t):
        tt = term[:, t % 3].rearrange("p i n -> p (i n)")
        mx["sig", t] = mixa(lambda e: e.activation(tt, tt, ACT.Sigmoid), [mx["lin", t]])

    def rest_add(t):
        st, m = state[:, t, :], mx["sig", t]
        for n, other in enumerate((ps_kv[t % 2][:, 0:DIM], vec["b_out"], term[:, t % 3, 0, :], term[:, t % 3, 1, :])):
            m = mixv(lambda e, other=other: e.tensor_tensor(st, st, other, ALU.add), [m, mx["rest", t]])
            if n == 0:
                mx["rest added", t] = m
        mx["state", t] = m
        done["mix"] = m

    W_AT = 17 * DIM
    WN = KC * HID
    assert W_AT + 4 * WN <= TILES * DIM
    w_l, w_s2 = lines("w_raw_load", 2), lines("w_parts_store", 2)
    v_w, pe_w, a_w = line("w_dve"), line("w_pe"), line("w_act")
    w_ld, m_s = line("small_load", 16), line("meta_store", 16)
    raw = [big[:, W_AT + r * 2 * WN:W_AT + r * 2 * WN + WN] for r in range(2)]
    halves = [big[:, W_AT + r * 2 * WN + WN:W_AT + (r + 1) * 2 * WN].bitcast(F16) for r in range(2)]
    ln_t = sb("ln_t", [P, 2, EXPERTS, KC])
    ln_r = big[0:2 * EXPERTS * KC, 3400:3400 + P]
    b1_r = big[0:EXPERTS * HC, 3600:3600 + P]
    b1_t = sb("b1_t", [P, EXPERTS, META])
    peaks = sb("peaks", [P, 3 * EXPERTS])
    peak_v = sb("peak_v", [3 * EXPERTS, 1])
    tops = sb("tops", [P, 3 * EXPERTS])
    expo = sb("expo", [P, 3, EXPERTS], I32)
    sc_i = sb("sc_i", [P, 2, EXPERTS], I32)
    gain_s = sb("gain_s", [P, EXPERTS, KC])
    scale_of = sc_i.bitcast(F32)

    def wv(fn, after=()):
        return q.do("vector", v_w, fn, after)

    def raw_load(n, r, after):
        ex, which = n // 2, n % 2
        src_ = w2[ex].rearrange("(h p) n -> p h n", p=P) if which else w1[ex].rearrange("(k p) n -> p k n", p=P)
        to = raw[r].rearrange("p (h n) -> p h n", h=HC if which else KC)
        return q.do("sync", w_l[r], lambda e: e.dma_start(to, src_), after)

    def peak_steps():
        for i, v in enumerate((ln_g, ln_b)):
            q.do("sync", w_ld, lambda e, i=i, v=v: e.dma_start(
                ln_r[i * EXPERTS * KC:(i + 1) * EXPERTS * KC, :], v.rearrange("e (k p) -> (e k) p", p=P)))
        m = q.do("sync", w_ld, lambda e: e.dma_start(b1_r, b1.rearrange("e (h p) -> (e h) p", p=P)))
        nl = 2 * EXPERTS * KC
        q.do("tensor", pe_w, lambda e: e.transpose(ps_kv[0][:, 0:nl], ln_r, ident[0:nl, 0:nl]), [m, m_const, m_ids])
        m = q.do("tensor", pe_w, lambda e: e.transpose(ps_kv[0][:, P:P + EXPERTS * HC], b1_r,
                                                       ident[0:EXPERTS * HC, 0:EXPERTS * HC]))
        wv(lambda e: e.tensor_copy(ln_t.rearrange("p i e k -> p (i e k)"), ps_kv[0][:, 0:nl]), [m])
        m_small = wv(lambda e: e.tensor_copy(
            b1_t[:, :, 0:HC], ps_kv[0][:, P:P + EXPERTS * HC].rearrange("p (e h) -> p e h", h=HC)))
        used, got = {}, {}
        got[0] = raw_load(0, 0, [m_ids, m_dst])
        got[1] = raw_load(1, 1, [])
        yield
        for n in range(2 * EXPERTS):
            ex, which, r = n // 2, n % 2, n % 2
            if which == 0:
                for h in range(HC):
                    for k in range(KC):
                        m = q.do("tensor", pe_w, lambda e, ex=ex, r=r, h=h, k=k: e.matmul(
                            ps_kv[1][:, ex * HC + h:ex * HC + h + 1], raw[r][:, k * HID + h * P:k * HID + (h + 1) * P],
                            ln_t[:, 1, ex, k:k + 1], start=(k == 0), stop=(k == KC - 1)), [got[n], m_small])
                done["b1 pe"] = m
                for k in range(KC):
                    part_ = raw[r][:, k * HID:(k + 1) * HID]
                    m = q.do("scalar", a_w, lambda e, ex=ex, k=k, part_=part_: e.activation(
                        part_, part_, ACT.Copy, scale=ln_t[:, 0, ex, k:k + 1]), [m])
            else:
                m = got[n]
            yield
            used[n] = wv(lambda e, ex=ex, which=which, r=r: e.tensor_reduce(
                peaks[:, which * EXPERTS + ex:which * EXPERTS + ex + 1], raw[r], AX.X, ALU.max,
                apply_absolute_value=True), [m])
            if n + 2 < 2 * EXPERTS:
                got[n + 2] = raw_load(n + 2, r, [used[n]])
        done["pass1"] = [used[2 * EXPERTS - 2], used[2 * EXPERTS - 1]]
        done["b1"] = wv(lambda e: e.tensor_tensor(
            b1_t[:, :, 0:HC], b1_t[:, :, 0:HC], ps_kv[1][:, 0:EXPERTS * HC].rearrange("p (e h) -> p e h", h=HC), ALU.add),
            [done["b1 pe"]])
        m = wv(lambda e: e.tensor_reduce(peaks[:, 2 * EXPERTS:3 * EXPERTS], b1_t[:, :, 0:HC], AX.X, ALU.max,
                                         apply_absolute_value=True), [done["b1"]])
        n3 = 3 * EXPERTS
        m = q.do("tensor", pe_w, lambda e: e.transpose(ps_kv[0][0:n3, 0:P], peaks, ident), [m])
        m = wv(lambda e: e.reduce_max(peak_v, ps_kv[0][0:n3, 0:P], AX.X), [m])
        yield
        m = q.do("tensor", pe_w, lambda e: e.matmul(ps_kv[0][:, 256:256 + n3], peak_v.to_broadcast([n3, P]), ident[0:n3, 0:n3],
                                                    start=True, stop=True), [m])
        m = wv(lambda e: e.tensor_copy(tops, ps_kv[0][:, 256:256 + n3]), [m])
        m = wv(lambda e: e.scalar_tensor_tensor(tops[:, 2 * EXPERTS:n3], tops[:, 0:EXPERTS], float(DIM),
                                                tops[:, 2 * EXPERTS:n3], ALU.mult, ALU.add), [m])
        ef = expo.rearrange("p a b -> p (a b)")
        m = wv(lambda e: e.tensor_scalar(ef, tops.bitcast(I32), 23, None, ALU.logical_shift_right), [m])
        m = wv(lambda e: e.tensor_scalar(ef, ef, 30.0, 240.0, ALU.max, ALU.min), [m])
        yield
        m = wv(lambda e: e.tensor_scalar(sc_i, expo[:, 0:2, :], -1.0, float(2 * BIAS + TOP), ALU.mult, ALU.add), [m])
        m_inv = wv(lambda e: e.tensor_scalar(sc_i, sc_i, 23, None, ALU.logical_shift_left), [m])
        bi = b1_t.bitcast(I32)
        x_exp = XSCALE.hex().split("p")[1]
        wv(lambda e: e.tensor_scalar(bi[:, :, HC], expo[:, 0, :], float(-TOP - int(x_exp)), None, ALU.add))
        wv(lambda e: e.tensor_scalar(bi[:, :, HC + 1], expo[:, 2, :], -1.0, float(2 * BIAS + TOP), ALU.mult, ALU.add))
        m = wv(lambda e: e.tensor_tensor(bi[:, :, HC + 2], expo[:, 1, :], expo[:, 2, :], ALU.add))
        m = wv(lambda e: e.tensor_scalar(bi[:, :, HC + 2], bi[:, :, HC + 2], float(-BIAS - 2 * TOP), 1.0, ALU.add, ALU.max), [m])
        m = wv(lambda e: e.tensor_scalar(bi[:, :, HC + 2], bi[:, :, HC + 2], 254.0, None, ALU.min), [m])
        m = wv(lambda e: e.tensor_scalar(bi[:, :, HC:META], bi[:, :, HC:META], 23, None, ALU.logical_shift_left), [m])
        for k in range(KC):
            done["gain"] = wv(lambda e, k=k: e.tensor_tensor(gain_s[:, :, k], ln_t[:, 0, :, k], scale_of[:, 0, :], ALU.mult), [m_inv])
        done["meta"] = q.do("sync", m_s, lambda e: e.dma_start(meta.rearrange("e p n -> p e n"), b1_t), [m])
        yield

    def parts_steps():
        got, stored = {}, {}
        for n in range(2):
            got[n] = raw_load(n, n, done["pass1"])
        for n in range(2 * EXPERTS):
            ex, which, r = n // 2, n % 2, n % 2
            hi, lo = halves[r][:, 0:WN], halves[r][:, WN:2 * WN]
            for k in range(KC):
                w = slice(k * HID, (k + 1) * HID)
                s_ = scale_of[:, 1, ex:ex + 1] if which else gain_s[:, ex, k:k + 1]
                m = q.do("scalar", a_w, lambda e, w=w, s_=s_, hi=hi, r=r: e.activation(
                    hi[:, w], raw[r][:, w], ACT.Copy, scale=s_), [got[n], done["gain"], stored.get(n - 2)])
            yield
            for k in range(KC):
                w = slice(k * HID, (k + 1) * HID)
                s_ = scale_of[:, 1, ex:ex + 1] if which else gain_s[:, ex, k:k + 1]
                m = wv(lambda e, w=w, s_=s_, hi=hi, lo=lo, r=r: e.scalar_tensor_tensor(
                    lo[:, w], raw[r][:, w], s_, hi[:, w], ALU.mult, ALU.subtract), [m, stored.get(n - 2)])
                yield
            stored[n] = q.do("sync", w_s2[r], lambda e, ex=ex, which=which, r=r: e.dma_start(
                w_parts[which][ex], halves[r]), [m])
            if n + 2 < 2 * EXPERTS:
                got[n + 2] = raw_load(n + 2, r, [m])
        done["weights"] = [stored[2 * EXPERTS - 2], stored[2 * EXPERTS - 1], done["meta"]]
        yield

    load_small()
    load_ids_rows(0)
    for k in range(XRING - 1):
        load_edges(k)

    def load_step(g):
        if g * GROUP % LOAD == 0:
            load_edges(g * GROUP // LOAD + XRING - 1)
        if g * GROUP % IDLOAD == 0:
            load_ids_rows(g * GROUP // IDLOAD + 1)

    def chain(*gens):
        for g in gens:
            yield from g

    def beside(a, b):
        alive = [a, b]
        while alive:
            alive = [g for g in alive if next(g, alive) is not alive]
            yield

    edges = q.skewed(GROUPS, 1, [edge_match, edge_same, lambda g: (edge_sum(g), load_step(g)), edge_rows_of, edge_add])
    degree = q.skewed(GROUPS, 1, [degree_hot, degree_sum])
    mix1 = q.skewed(TILES, 3, [mix_norm, mix_turn, mix_keep, mix_half(0),
                               lambda t: (mix_out(0)(t), mix_half(1)(t)), mix_out(1), mix_squares, mix_sd, mix_keys, mix_dots])
    mix2 = q.skewed(TILES, 1, [rest_products, rest_sigmoid, rest_add])
    side = chain(peak_steps(), norm_steps(), beside(parts_steps(), mix1), fold_steps(), mix2)
    side_steps = 21 + 25 + (TILES * 3 + 7) + 3 + TILES + 2
    due, ended = 0.0, []
    for g, _ in enumerate(edges):
        next(degree, None)
        due += side_steps / (GROUPS - 4)
        while due >= 1:
            if next(side, ended) is ended:
                due = -1e9
            due -= 1
    for _ in side:
        pass
    for _ in degree:
        pass
    done["in_deg"] = q.do("vector", v_h, lambda e: e.tensor_scalar(
        in_deg, ps_deg[:, 0:TILES], float(DEG - 1), None, ALU.min), [done["deg", GROUPS - 1]])

    at[0] = 0
    PR, YR, HR = 4, 4, 3
    parts = part(PR * TABLES * RW).rearrange("p (r a w) -> p r a w", r=PR, a=TABLES)
    sumT = part(2 * P).rearrange("p (r n) -> p r n", r=2)
    y = part(YR * DIM).rearrange("p (r n) -> p r n", r=YR)
    yT = part(2 * DIM).rearrange("p (r n) -> p r n", r=2)
    xh = part(HR * DIM).bitcast(F16).rearrange("p (r i n) -> p r i n", r=HR, i=2)
    count = sb("count", [P, TILES])
    out_deg = sb("out_deg", [P, TILES], I32)
    mv2 = sb("mv2", [P, TILES, 2])
    r1 = sb("r1", [P, TILES])
    r2 = sb("r2", [P, TILES])
    p_l, zi_l, zo_l = lines("parts_load", PR), lines("zin_add", 4), lines("zout_add", 4)
    xs_l, ys_l = lines("xn_store", HR), line("y_store", 16)
    v_n, a_n, pe_n = line("node_dve"), line("node_act"), line("node_pe")
    ps_t, ps_s, ps_y, ps_log = banks[0:2], banks[2:4], banks[5:7], banks[7]
    all_added = [added[c] for c in range(ETILES - TABLES, ETILES)]
    edges_done = [Mark(l.sem, l.count) for l in (v_m, pe_m, a_m, v_e, a_e, pe_e, v_h)]
    nd = {}

    def nv(fn, after=()):
        return q.do("vector", v_n, fn, after)

    def na(fn, after=()):
        return q.do("scalar", a_n, fn, after)

    def npe(fn, after=()):
        return q.do("tensor", pe_n, fn, after)

    def rows_of(t):
        return LAST if t == TILES - 1 else P

    def degree_row(t, lines_, z, deg, after):
        return q.do("gpsimd", lines_[t % 4], lambda e: e.indirect_dma_start(
            state[:, t, :], None, z, bass.IndirectOffsetOnAxis(ap=deg[:, t:t + 1], axis=0),
            compute_op=ALU.add, bounds_check=DEG - 1, oob_is_err=True), after)

    def node_load(t):
        for a in range(TABLES):
            nd["parts", t] = q.do("sync", p_l[t % PR], lambda e, a=a: e.dma_start(
                parts[:, t % PR, a, :], table[a][t * P:(t + 1) * P, :]),
                all_added + edges_done + [nd.get(("sum", t - PR)), nd.get(("count", t - PR))])
        nd["zin", t] = degree_row(t, zi_l, z_in, in_deg, [done["in_deg"], done["mix"], nd.get(("zin", t - 4))])

    def node_count(t):
        m = nv(lambda e: e.reduce_sum(count[:, t:t + 1], parts[:, t % PR, :, EDIM:RW].rearrange("p a w -> p (a w)"), AX.X),
               [nd["parts", t]])
        nd["count", t] = nv(lambda e: e.tensor_scalar(
            out_deg[:, t:t + 1], count[:, t:t + 1], float(DEG - 1), None, ALU.min), [m])

    def node_sum(t):
        nd["zout", t] = degree_row(t, zo_l, z_out, out_deg, [nd["count", t], nd["zin", t], nd.get(("zout", t - 4))])
        for a in range(TABLES):
            nd["sum", t] = npe(lambda e, a=a: e.matmul(
                ps_t[t % 2][:, 0:P], parts[:, t % PR, a, 0:EDIM], ident, start=(a == 0), stop=(a == TABLES - 1)),
                [nd["parts", t], nd.get(("sumT", t - 2))] + edges_done)

    def node_sumT(t):
        nd["sumT", t] = na(lambda e: e.copy(sumT[:, t % 2, :], ps_t[t % 2][:, 0:P]),
                           [nd["sum", t], nd.get(("proj", t - 2))] + edges_done)

    def node_project(t):
        nd["proj", t] = npe(lambda e: e.matmul(ps_s[t % 2][:, 0:DIM], sumT[:, t % 2, :], wsum, start=True, stop=True),
                            [nd["sumT", t], nd.get(("projected", t - 2))])

    def node_state(t):
        st = state[:, t, :]
        m = nv(lambda e: e.tensor_tensor(st, st, ps_s[t % 2][:, 0:DIM], ALU.add), [nd["proj", t], nd["zout", t]])
        nd["projected", t] = m
        m = nv(lambda e: e.scalar_tensor_tensor(st, vec["b_sum"], count[:, t:t + 1], st, ALU.mult, ALU.add), [m])
        nd["state", t] = m
        nd["stat", t] = norm_stats(nv, st, stats[:, t % 2, :], mv2[:, t, :], [m])
        n = rows_of(t)
        q.do("sync", ys_l, lambda e: e.dma_start(y_rows[t * P:t * P + n, :], st[0:n, :]), [m])

    def node_sd(t):
        one = slice(t, t + 1)
        nd["sd", t] = na(lambda e: e.activation(r1[:, one], mv2[:, t, 1:2], ACT.Sqrt, bias=eps_t), [nd["stat", t]])

    def node_norm(t):
        one, r = slice(t, t + 1), t % YR
        m = nv(lambda e: e.reciprocal(r1[:, one], r1[:, one]), [nd["sd", t]])
        nd["var", t] = nv(lambda e: e.tensor_scalar(r2[:, one], r1[:, one], r1[:, one], mv2[:, t, 1:2], ALU.mult, ALU.mult), [m])
        nd["y", t] = nv(lambda e: e.tensor_scalar(y[:, r, :], state[:, t, :], mv2[:, t, 0:1], r1[:, one], ALU.subtract, ALU.mult),
                        [m, nd.get(("lo", t - YR)), nd.get(("turn", t - YR))] + edges_done)

    def node_turn(t):
        one, r = slice(t, t + 1), t % YR
        nd["sd2", t] = na(lambda e: e.activation(r2[:, one], r2[:, one], ACT.Sqrt, bias=eps_t), [nd["var", t]])
        for k in range(KC):
            nd["turn", t] = npe(lambda e, k=k: e.transpose(
                ps_y[t % 2][:, k * P:(k + 1) * P], y[:, r, k * P:(k + 1) * P], ident), [nd["y", t], nd.get(("yT", t - 2))])

    def node_second(t):
        one, r = slice(t, t + 1), t % YR
        m = nv(lambda e: e.reciprocal(r2[:, one], r2[:, one]), [nd["sd2", t]])
        nd["r2", t] = nv(lambda e: e.tensor_scalar(r2[:, one], r2[:, one], XSCALE, None, ALU.mult), [m])
        nd["yT", t] = na(lambda e: e.copy(yT[:, t % 2, :], ps_y[t % 2][:, 0:DIM]), [nd["turn", t], nd.get(("logit", t - 2))])

    def node_high(t):
        nd["hi", t] = na(lambda e: e.activation(xh[:, t % HR, 0, :], y[:, t % YR, :], ACT.Copy, scale=r2[:, t:t + 1]),
                         [nd["r2", t], nd.get(("stored", t - HR))])
        for k in range(KC):
            nd["logit", t] = npe(lambda e, k=k: e.matmul(
                ps_log[:, t * EXPERTS:(t + 1) * EXPERTS], yT[:, t % 2, k * P:(k + 1) * P],
                wr_t[:, k, :], start=(k == 0), stop=(k == KC - 1)), [nd["yT", t]])

    def node_low(t):
        nd["lo", t] = nv(lambda e: e.scalar_tensor_tensor(
            xh[:, t % HR, 1, :], y[:, t % YR, :], r2[:, t:t + 1], xh[:, t % HR, 0, :], ALU.mult, ALU.subtract), [nd["hi", t]])
        n = rows_of(t)
        nd["stored", t] = q.do("sync", xs_l[t % HR], lambda e: e.dma_start(
            xn_rows[t * P:t * P + n, :], xh[0:n, t % HR].rearrange("p i n -> p (i n)")), [nd["lo", t]])

    for _ in q.skewed(TILES, 1, [node_load, node_count, node_sum, node_sumT, node_project, node_state, node_sd,
                                 node_norm, node_turn, node_second, node_high, node_low]):
        pass

    v_r, a_r, pe_r = line("route_dve"), line("route_act"), line("route_pe")
    at[0] = 0
    N8 = TILES * EXPERTS
    nodes_done = [Mark(l.sem, l.count) for l in (v_n, a_n, pe_n)] + [nd["stored", t] for t in range(TILES - HR, TILES)]
    logit, hot1, hot2, tmp, tmp2, cums, cums2 = (part(N8).rearrange("p (t e) -> p t e", e=EXPERTS) for _ in range(7))
    rank = part(EXPERTS)
    base = part(EXPERTS)
    base2 = part(EXPERTS)
    tiles_e = part(EXPERTS)
    cnt_i = part(EXPERTS).bitcast(I32)
    top1, top2, wt1, wt2, num, pos = (part(TILES) for _ in range(6))
    pos_i = part(TILES).bitcast(I32)
    p_hi, p_lo = part(2 * TILES).rearrange("p (k t) -> p k t", k=2), part(2 * TILES).rearrange("p (k t) -> p k t", k=2)
    valid = part(1)
    MR = 4
    lo_hot = part(MR * P).rearrange("p (r n) -> p r n", r=MR)
    hi_hot = part(MR * 2 * STILES).rearrange("p (r a n) -> p r a n", r=MR, a=2)
    slot_tok = sb("slot_tok", [P, STILES], I32)
    slot_w = sb("slot_w", [P, STILES])
    slot_f = part(STILES)
    empty = part(STILES)
    blk = part(BLOCKS)
    owner = part(BLOCKS)
    owner_i = sb("owner_i", [P, BLOCKS], I32)

    chainm = [None]

    def rv(fn, after=()):
        chainm[0] = q.do("vector", v_r, fn, [chainm[0], *after])
        return chainm[0]

    def b8(v):
        return v.unsqueeze(2).to_broadcast([P, TILES, EXPERTS])

    def over_tiles(v):
        return v.unsqueeze(1).to_broadcast([P, TILES, EXPERTS])

    rv(lambda e: e.tensor_tensor(logit, ps_log[:, 0:N8].rearrange("p (t e) -> p t e", e=EXPERTS), over_tiles(br_t), ALU.add),
       nodes_done)
    rv(lambda e: e.tensor_scalar(rank, iota[:, 0:EXPERTS], -1.0, float(EXPERTS), ALU.mult, ALU.add))
    rv(lambda e: e.tensor_scalar(valid, lane, float(LAST), None, ALU.is_lt))

    def pick(top, hot):
        rv(lambda e: e.reduce_max(top, logit, AX.X))
        rv(lambda e: e.tensor_tensor(tmp, logit, b8(top), ALU.is_equal))
        rv(lambda e: e.tensor_tensor(tmp, tmp, over_tiles(rank), ALU.mult))
        rv(lambda e: e.reduce_max(num, tmp, AX.X))
        rv(lambda e: e.tensor_tensor(hot, tmp, b8(num), ALU.is_equal))

    pick(top1, hot1)
    rv(lambda e: e.tensor_scalar(tmp2, hot1, -3.0e38, None, ALU.mult))
    rv(lambda e: e.tensor_scalar(tmp, hot1, -1.0, 1.0, ALU.mult, ALU.add))
    rv(lambda e: e.tensor_tensor(logit, logit, tmp, ALU.mult))
    rv(lambda e: e.tensor_tensor(logit, logit, tmp2, ALU.add))
    pick(top2, hot2)
    m = rv(lambda e: e.tensor_tensor(wt2, top2, top1, ALU.subtract))
    m = q.do("scalar", a_r, lambda e: e.activation(wt2, wt2, ACT.Exp), [m])
    rv(lambda e: e.tensor_scalar(wt1, wt2, 1.0, None, ALU.add), [m])
    rv(lambda e: e.reciprocal(wt1, wt1))
    rv(lambda e: e.tensor_tensor(wt2, wt2, wt1, ALU.mult))
    for h in (hot1, hot2):
        rv(lambda e, h=h: e.tensor_scalar(h[:, TILES - 1, :], h[:, TILES - 1, :], valid, None, ALU.mult))
    m = rv(lambda e: e.tensor_tensor(tmp, hot1, hot2, ALU.add))
    flat_t = tmp.rearrange("p t e -> p (t e)")
    q.do("tensor", pe_r, lambda e: e.matmul(banks[0][:, 0:N8], before, flat_t, start=True, stop=True), [m])
    m = q.do("tensor", pe_r, lambda e: e.matmul(banks[1][:, 0:N8], ones, flat_t, start=True, stop=True), [m])
    rv(lambda e: e.tensor_copy(cums.rearrange("p t e -> p (t e)"), banks[1][:, 0:N8]), [m])
    a, b, d = cums, cums2, 1
    while d < TILES:
        rv(lambda e, a=a, b=b, d=d: e.tensor_copy(b[:, 0:d, :], a[:, 0:d, :]))
        rv(lambda e, a=a, b=b, d=d: e.tensor_tensor(b[:, d:TILES, :], a[:, d:TILES, :], a[:, 0:TILES - d, :], ALU.add))
        a, b, d = b, a, 2 * d
    shift = SLOT.bit_length() - 1
    rv(lambda e, a=a: e.tensor_scalar(cnt_i, a[:, TILES - 1, :], float(SLOT - 1), None, ALU.add))
    rv(lambda e: e.tensor_scalar(cnt_i, cnt_i, shift, None, ALU.arith_shift_right))
    rv(lambda e: e.tensor_copy(tiles_e, cnt_i))
    rv(lambda e: e.tensor_copy(base, tiles_e))
    c, f, d = base, base2, 1
    while d < EXPERTS:
        rv(lambda e, c=c, f=f, d=d: e.tensor_copy(f[:, 0:d], c[:, 0:d]))
        rv(lambda e, c=c, f=f, d=d: e.tensor_tensor(f[:, d:EXPERTS], c[:, d:EXPERTS], c[:, 0:EXPERTS - d], ALU.add))
        c, f, d = f, c, 2 * d
    rv(lambda e: e.memset(owner, 0.0))
    for ex in range(EXPERTS - 1):
        rv(lambda e, ex=ex, c=c: e.scalar_tensor_tensor(owner, iota[:, 0:BLOCKS], c[:, ex:ex + 1], owner, ALU.is_ge, ALU.add))
    m_owner = rv(lambda e: e.tensor_copy(owner_i, owner))
    rv(lambda e, c=c, f=f: e.tensor_tensor(f, c, tiles_e, ALU.subtract))
    rv(lambda e, f=f: e.tensor_scalar(f, f, float(SLOT), None, ALU.mult))
    rv(lambda e, a=a, b=b: e.tensor_tensor(b, a, banks[1][:, 0:N8].rearrange("p (t e) -> p t e", e=EXPERTS), ALU.subtract))
    rv(lambda e, b=b: e.tensor_tensor(b, b, banks[0][:, 0:N8].rearrange("p (t e) -> p t e", e=EXPERTS), ALU.add))
    rv(lambda e, b=b, f=f: e.tensor_tensor(b, b, over_tiles(f), ALU.add))
    rv(lambda e: e.tensor_scalar(num, iota[:, 0:TILES], float(P), 1.0, ALU.mult, ALU.add))
    rv(lambda e: e.tensor_scalar(num, num, lane, None, ALU.add))
    rv(lambda e: e.tensor_scalar(num[:, TILES - 1:TILES], num[:, TILES - 1:TILES], valid, None, ALU.mult))
    for k, h in enumerate((hot1, hot2)):
        rv(lambda e, h=h, b=b: e.tensor_tensor(tmp, h, b, ALU.mult))
        rv(lambda e: e.reduce_sum(pos, tmp, AX.X))
        rv(lambda e: e.tensor_copy(pos_i, pos))
        rv(lambda e: e.tensor_scalar(cnt_i if False else tmp2.rearrange("p t e -> p (t e)")[:, 0:TILES].bitcast(I32), pos_i, 7, None, ALU.arith_shift_right))
        rv(lambda e, k=k: e.tensor_copy(p_hi[:, k, :], tmp2.rearrange("p t e -> p (t e)")[:, 0:TILES].bitcast(I32)))
        rv(lambda e: e.tensor_scalar(pos_i, pos_i, 127, None, ALU.bitwise_and))
        m_pos = rv(lambda e, k=k: e.tensor_copy(p_lo[:, k, :], pos_i))
    for w in (wt1, wt2):
        m_pos = rv(lambda e, w=w: e.tensor_scalar(w[:, TILES - 1:TILES], w[:, TILES - 1:TILES], valid, None, ALU.mult))

    mapped = {}
    for n in range(2 * TILES):
        k, t = n // TILES, n % TILES
        r = n % MR
        w = (wt1, wt2)[k]
        engine, ln = "vector", v_r
        free = [mapped.get(n - MR), m_pos]
        q.do(engine, ln, lambda e, r=r, k=k, t=t: e.tensor_scalar(
            lo_hot[:, r, :], iota, p_lo[:, k, t:t + 1], None, ALU.is_equal), free)
        q.do(engine, ln, lambda e, r=r, k=k, t=t: e.tensor_scalar(
            hi_hot[:, r, 0, :], iota[:, 0:STILES], p_hi[:, k, t:t + 1], num[:, t:t + 1], ALU.is_equal, ALU.mult))
        m = q.do(engine, ln, lambda e, r=r, k=k, t=t, w=w: e.tensor_scalar(
            hi_hot[:, r, 1, :], iota[:, 0:STILES], p_hi[:, k, t:t + 1], w[:, t:t + 1], ALU.is_equal, ALU.mult))
        mapped[n] = q.do("tensor", pe_r, lambda e, r=r, n=n: e.matmul(
            banks[2][:, 0:2 * STILES], lo_hot[:, r, :], hi_hot[:, r].rearrange("p a n -> p (a n)"),
            start=(n == 0), stop=(n == 2 * TILES - 1)), [m])
    chainm[0] = Mark(v_r.sem, v_r.count)
    rv(lambda e: e.tensor_scalar(empty, banks[2][:, 0:STILES], 0.5, None, ALU.is_lt), [mapped[2 * TILES - 1]])
    rv(lambda e: e.tensor_scalar(valid, spare, 1.0, None, ALU.add))
    rv(lambda e: e.tensor_scalar(empty, empty, valid, -1.0, ALU.mult, ALU.add))
    rv(lambda e: e.tensor_copy(slot_w, banks[2][:, STILES:2 * STILES]))
    m_slots = rv(lambda e: e.tensor_tensor(slot_tok, empty, banks[2][:, 0:STILES], ALU.add))

    slab_at = [0]

    def slab(n):
        slab_at[0] += n
        return big[:, slab_at[0] - n:slab_at[0]]

    W1r = slab(2 * WN).bitcast(F16).rearrange("p (r i k n) -> p r i k n", r=2, i=2, k=KC)
    W2r = slab(2 * WN).bitcast(F16).rearrange("p (r i h n) -> p r i h n", r=2, i=2, h=HC)
    hT = slab(2 * HC * SLOT).bitcast(F16).rearrange("p (r i h n) -> p r i h n", r=2, i=2, h=HC)
    at[0] = 0
    routed = [m_slots, m_owner, Mark(pe_r.sem, pe_r.count)]
    XG = 3
    edge_mem = X.rearrange("p a b c -> p (a b c)")
    xg = edge_mem[:, 0:XG * 2 * DIM].bitcast(F16).rearrange("p (r s i k n) -> p r s i k n", r=XG, s=2, i=2, k=KC)
    xT = edge_mem[:, XG * 2 * DIM:(XG + 2) * 2 * DIM].bitcast(F16).rearrange("p (r i k n) -> p r i k n", r=2, i=2, k=KC)
    yo = part(2 * 2 * DIM).rearrange("p (r h n) -> p r h n", r=2, h=2)
    h32 = part(HC * SLOT).rearrange("p (h n) -> p h n", h=HC)
    NM = 3
    m_r = sb("m_r", [P, NM, META])
    b2r = sb("b2r", [P, NM, DIM])
    w1_l, w2_l, ml, gl, ad = lines("w1_load", 2), lines("w2_load", 2), lines("meta_load", NM), lines("gather", 2 * XG), line("row_add", 16)
    a_x, v_x2, pe_x = line("expert_act"), line("expert_dve"), line("expert_pe")
    ps_x, ps_h, ps_o = banks[0].bitcast(F16), banks[1:5], banks[5:7]
    ex = {}
    y_stored = [Mark(ys_l.sem, ys_l.count), m_pad]
    xn_stored = [nd["stored", t] for t in range(TILES - HR, TILES)] + [m_pad]
    THREE = ((0, 0), (0, 1), (1, 0))

    def block_load(j):
        if j >= BLOCKS:
            return
        r = j % 2
        where = {}

        def first(e):
            where["v"] = e.value_load(owner_i[0:1, j:j + 1], min_val=0, max_val=EXPERTS - 1)
            return e.dma_start(W1r[:, r].rearrange("p i k n -> p (i k n)"),
                               w_parts[0][bass.ds(where["v"], 1)].rearrange("o p n -> p (o n)"))

        ex["w1", j] = q.do("sync", w1_l[r], first, routed + done["weights"] + [ex.get(("up", j - 2))])
        q.do("sync", ml[j % NM], lambda e: e.dma_start(
            m_r[:, j % NM, :], meta[bass.ds(where["v"], 1)].rearrange("o p n -> p (o n)")),
            [ex.get(("o", j - NM, 1)), ex.get(("g", j - NM, HC - 1)), ex.get(("lo", j - NM, HC // 2 - 1))])
        ex["m", j] = q.do("sync", ml[j % NM], lambda e: e.dma_start(
            b2r[:, j % NM, :], b2[bass.ds(where["v"], 1)].rearrange("o n -> (o n)").partition_broadcast(P)))
        ex["w2", j] = q.do("sync", w2_l[r], lambda e: e.dma_start(
            W2r[:, r].rearrange("p i h n -> p (i h n)"), w_parts[1][bass.ds(where["v"], 1)].rearrange("o p n -> p (o n)")),
            [ex.get(("down", j - 2))])

    def block_gather(j):
        if j >= BLOCKS:
            return
        for h in range(2):
            l, s = gl[(j % XG) * 2 + h], 2 * j + h
            ex["g", j, "rows", h] = q.do("gpsimd", l, lambda e, h=h, s=s: e.indirect_dma_start(
                xg[:, j % XG, h].rearrange("p i k n -> p (i k n)"), None, xn_rows,
                bass.IndirectOffsetOnAxis(ap=slot_tok[:, s:s + 1], axis=0), bounds_check=ROWS - 1, oob_is_err=True),
                routed + xn_stored + [ex.get(("T", j - XG))])

    def block_turn(j):
        if j >= BLOCKS:
            return
        for i in range(2):
            for k in range(KC):
                for h in range(2):
                    c = (i * KC + k) * SLOT + h * P
                    m = q.do("tensor", pe_x, lambda e, i=i, k=k, h=h, c=c: e.transpose(
                        ps_x[:, c:c + P], xg[:, j % XG, h, i, k, :], identh),
                        [ex["g", j, "rows", 0], ex["g", j, "rows", 1], ex.get(("xT", j - 1))] + routed)
        ex["T", j] = m
        ex["xT", j] = q.do("vector", v_x2, lambda e: e.tensor_copy(
            xT[:, j % 2].rearrange("p i k n -> p (i k n)"), ps_x), [m, ex.get(("up", j - 2))])

    def block_up(j):
        if j >= BLOCKS:
            return
        r, n = j % 2, j % NM
        for h in range(HC):
            ps = ps_h[h % 4][:, 0:SLOT]
            steps = [(a, b, k) for k in range(KC) for a, b in THREE]
            for s, (a, b, k) in enumerate(steps):
                m = q.do("tensor", pe_x, lambda e, a=a, b=b, k=k, h=h, ps=ps, s=s: e.matmul(
                    ps, W1r[:, r, a, k, h * P:(h + 1) * P], xT[:, r, b, k, :], start=(s == 0), stop=(s == len(steps) - 1)),
                    [ex["w1", j], ex["xT", j], ex.get(("g", j, h - 4)) if h >= 4 else ex.get(("g", j - 1, h + 4))])
            ex["g", j, h] = q.do("scalar", a_x, lambda e, h=h, ps=ps: e.activation(
                h32[:, h, :], ps, ACT.Gelu, bias=m_r[:, n, h:h + 1], scale=m_r[:, n, HC:HC + 1]),
                [m, ex["m", j], ex.get(("lo", j - 1, h // 2))])
            if h % 2:
                pair = slice(h - 1, h + 1)
                hs = h32[:, pair, :].rearrange("p h n -> p (h n)")
                parts_ = [hT[:, r, i, pair, :].rearrange("p h n -> p (h n)") for i in range(2)]
                m = q.do("vector", v_x2, lambda e, hs=hs, o_=parts_[0]: e.tensor_scalar(
                    o_, hs, m_r[:, n, HC + 1:HC + 2], None, ALU.mult), [ex["g", j, h], ex["m", j], ex.get(("down", j - 2))])
                ex["lo", j, h // 2] = q.do("vector", v_x2, lambda e, hs=hs, p_=parts_: e.scalar_tensor_tensor(
                    p_[1], hs, m_r[:, n, HC + 1:HC + 2], p_[0], ALU.mult, ALU.subtract), [m])
        ex["up", j] = Mark(pe_x.sem, pe_x.count)

    def block_down(j):
        r, n = j % 2, j % NM
        for s in range(2):
            ps = ps_o[s][:, 0:DIM]
            steps = [(a, b, h) for h in range(HC) for a, b in THREE]
            for i, (a, b, h) in enumerate(steps):
                m = q.do("tensor", pe_x, lambda e, a=a, b=b, h=h, s=s, ps=ps, i=i: e.matmul(
                    ps, hT[:, r, a, h, s * P:(s + 1) * P], W2r[:, r, b, h, :], start=(i == 0), stop=(i == len(steps) - 1)),
                    [ex["lo", j, h // 2], ex["w2", j], ex.get(("o", j - 1, s))])
            ex["down", j] = m
            ex["o", j, s] = q.do("vector", v_x2, lambda e, s=s, ps=ps: e.scalar_tensor_tensor(
                yo[:, r, s, :], ps, m_r[:, n, HC + 2:HC + 3], b2r[:, n, :], ALU.mult, ALU.add),
                [m, ex["m", j], ex.get(("add", j - 2))] + routed)
            m = q.do("vector", v_x2, lambda e, s=s: e.tensor_scalar(
                yo[:, r, s, :], yo[:, r, s, :], slot_w[:, 2 * j + s:2 * j + s + 1], None, ALU.mult), [ex["o", j, s]])
            ex["add", j] = q.do("gpsimd", ad, lambda e, s=s: e.indirect_dma_start(
                y_rows, bass.IndirectOffsetOnAxis(ap=slot_tok[:, 2 * j + s:2 * j + s + 1], axis=0), yo[:, r, s, :], None,
                compute_op=ALU.add, bounds_check=ROWS - 1, oob_is_err=True),
                [m, Mark(ad.sem, ad.count) if ad.count else None] + y_stored)

    for j in range(2):
        block_load(j)
        block_gather(j)
    block_turn(0)
    block_turn(1)
    block_up(0)
    for j in range(BLOCKS):
        block_gather(j + 2)
        block_up(j + 1)
        block_turn(j + 2)
        block_down(j)
        block_load(j + 2)

    fin = line("result", 16)
    m = q.do("sync", fin, lambda e: e.dma_start(out, y_rows[0:NODES, :]), [ex["add", BLOCKS - 1]])
    q.wait("sync", [m])

    with ctx:
        block = ctx.enter_context(nc.Block())

        @block.tensor
        def _(e):
            q.play("tensor", e)

        @block.vector
        def _(e):
            q.play("vector", e)

        @block.scalar
        def _(e):
            q.play("scalar", e)

        @block.gpsimd
        def _(e):
            q.play("gpsimd", e)

        @block.sync
        def _(e):
            q.play("sync", e)


INPUTS = ["x", "src", "dst", "edge_attr_128", "node_vec1", "node_vec1_n2", "L0_gnn_z_in", "L0_gnn_z_out",
          "L0_gnn_W_cent", "L0_gnn_b_cent", "L0_gnn_W_vor", "L0_gnn_b_vor", "L0_gnn_W_sum", "L0_gnn_b_sum",
          "L0_mix_w_qkv", "L0_mix_w_out", "L0_mix_b_out", "L0_ffn_Wr", "L0_ffn_br", "L0_ffn_ln_g", "L0_ffn_ln_b",
          "L0_ffn_W1", "L0_ffn_b1", "L0_ffn_W2", "L0_ffn_b2"]


def kernel(**inputs):
    import concourse.bacc as bacc
    from concourse.bass_utils import run_bass_kernel_spmd

    nc = bacc.Bacc("TRN2", target_bir_lowering=False, num_devices=1)
    arrays, args = {}, []
    for name in INPUTS:
        a = np.ascontiguousarray(inputs[name])
        arrays[name] = a
        args.append(nc.dram_tensor(name, a.shape, mybir.dt.from_np(a.dtype), kind="ExternalInput").ap())
    result = nc.dram_tensor("result", (NODES, DIM), F32, kind="ExternalOutput").ap()
    build_layer(nc, *args, result)
    r = run_bass_kernel_spmd(nc, [arrays], core_ids=[0])
    return r.results[0]["result"]
```

```python
from contextlib import ExitStack

import numpy as np

import concourse.bass as bass
from concourse import mybir

F32, I32, BF16, F16 = mybir.dt.float32, mybir.dt.int32, mybir.dt.bfloat16, mybir.dt.float16
ALU, ACT, AX = mybir.AluOpType, mybir.ActivationFunctionType, mybir.AxisListType

P = 128
NODES, DIM, EDGES, EDIM = 6250, 256, 100000, 128
KC = DIM // P
TILES = -(-NODES // P)
LAST = NODES - (TILES - 1) * P
HEADS, DH = 8, 64
INNER = HEADS * DH
PAIRS = INNER // P
EXPERTS, HID = 8, 1024
HC = HID // P
DEG = 512
EPS = 1e-5

ECOLS = EDGES // P
EREST = EDGES - ECOLS * P
ETILES = ECOLS + 1
GROUP = 3
GROUPS = -(-ETILES // GROUP)
LOAD = 6
XRING, SRING, ORING = 4, 3, 6
TABLES = 4
XW = EDIM + 2
RW = EDIM + 1
ROWS = (TILES + 1) * P
ZERO = 645
WEVERY = 5
DEGREES = 1.5
START = 8
IDLOAD = 12

SLOT = 256
STILES = (2 * NODES + EXPERTS * (P - 1)) // P
FULL = 2 * NODES // P // 2
BLOCKS = FULL + STILES - 2 * FULL
SPREAD = FULL // (BLOCKS - FULL)
assert EXPERTS <= STILES - 2 * FULL

TOP = 14
XSCALE = 256.0
BIAS = 127
META = HC + 3


class Mark:

    def __init__(self, sem, value):
        self.sem, self.value = sem, value


class Line:

    def __init__(self, sem, step=1):
        self.sem, self.step, self.count = sem, step, 0

    def next(self):
        self.count += self.step
        return Mark(self.sem, self.count)


class Script:

    def __init__(self):
        self.items = {e: [] for e in ("tensor", "vector", "scalar", "gpsimd", "sync")}
        self.seen = {e: {} for e in self.items}

    def wait(self, engine, marks):
        for m in marks:
            if m is not None and self.seen[engine].get(m.sem, 0) < m.value:
                self.seen[engine][m.sem] = m.value
                self.items[engine].append(("wait", m))

    def do(self, engine, line, step, after=()):
        self.wait(engine, after)
        m = line.next() if line is not None else None
        self.items[engine].append(("do", step, line, m))
        return m

    def skewed(self, n, every, stages):
        stages = [s if isinstance(s, tuple) else (s,) for s in stages]
        for tick in range((n - 1) * every + len(stages)):
            for step in range(max(len(s) for s in stages)):
                for k in range(len(stages) - 1, -1, -1):
                    if step < len(stages[k]) and (tick - k) % every == 0 and 0 <= (tick - k) // every < n:
                        stages[k][step]((tick - k) // every)
            yield

    def play(self, engine, handle):
        for item in self.items[engine]:
            if item[0] == "wait":
                handle.wait_ge(item[1].sem, item[1].value)
            else:
                ins = item[1](handle)
                if item[2] is not None:
                    ins.then_inc(item[2].sem, item[2].step)


def build_layer(nc, x, src, dst, edge_attr, vor, cent, z_in, z_out, w_cent, b_cent, w_vor, b_vor,
                w_sum, b_sum, w_qkv, w_out, b_out, wr, br, ln_g, ln_b, w1, b1, w2, b2, out):
    ctx = ExitStack()

    def sb(name, shape, dt=F32):
        return ctx.enter_context(nc.sbuf_tensor(name, shape, dt)).ap()

    def line(name, step=1):
        return Line(ctx.enter_context(nc.semaphore(name)), step)

    def lines(name, n, step=16):
        return [line(f"{name}{i}", step) for i in range(n)]

    q = Script()
    banks = [ctx.enter_context(nc.psum_tensor(f"bank{i}", [P, 512], F32)).ap() for i in range(8)]

    table = [nc.dram_tensor(f"node_table{i}", (ROWS, RW), F32, kind="Internal").ap() for i in range(TABLES)]
    xn_rows = nc.dram_tensor("xn_rows", (ROWS, 2 * DIM), F16, kind="Internal").ap()
    y_rows = out
    w_parts = [nc.dram_tensor(f"w{i}_parts", (EXPERTS, P, 2 * KC * HID), F16, kind="Internal").ap() for i in (1, 2)]
    peak_rows = nc.dram_tensor("peak_rows", (2 * EXPERTS, P), F32, kind="Internal").ap()
    b1_peak_rows = nc.dram_tensor("b1_peak_rows", (P, EXPERTS), F32, kind="Internal").ap()
    meta = nc.dram_tensor("expert_meta", (EXPERTS, P, META), F32, kind="Internal").ap()
    id_rows = nc.dram_tensor("id_rows", (2, ETILES * P), BF16, kind="Internal").ap()

    idx_d, v_i = line("index_dma", 16), line("index_dve")
    big = sb("big", [P, TILES * DIM])
    src_i = big[:, 5000:5000 + ETILES].bitcast(I32)
    tmp_i = big[:, 6000:6000 + ETILES].bitcast(I32)
    src_f = sb("src_f", [P, ETILES])
    to_spare = sb("to_spare", [P, ETILES])
    src_hi = big[:, 7000:7000 + ETILES // 2].bitcast(BF16)
    src_lo = big[:, 7500:7500 + ETILES // 2].bitcast(BF16)
    dst_hi = sb("dst_hi", [P, ETILES], BF16)
    dst_lo = sb("dst_lo", [P, ETILES], BF16)


    g_c, v_c = line("const_pool"), line("const_dve")
    ident = sb("ident", [P, P])
    identb = sb("identb", [P, P], BF16)
    before = sb("before", [P, P], BF16)
    ones = sb("ones", [P, P])
    onesb = sb("onesb", [P, P], BF16)
    identh = sb("identh", [P, P], F16)
    lane_i = sb("lane_i", [P, 1], I32)
    lane = sb("lane", [P, 1])
    spare = sb("spare", [P, 1])
    spare_i = sb("spare_i", [P, 1], I32)
    pow_i = sb("pow_i", [P, 2], I32)
    iota_i = sb("iota_i", [P, P], I32)
    iota = sb("iota", [P, P])
    iotab = sb("iotab", [P, P], BF16)
    eps_t = sb("eps_t", [P, 1])
    eps_s = sb("eps_s", [P, 1])
    thresh = sb("thresh", [P, 1])
    zeros = sb("zeros", [P, ZERO])

    def pool(fn, after=()):
        return q.do("gpsimd", g_c, fn, after)

    def dve(fn, after=()):
        return q.do("vector", v_c, fn, after)

    pool(lambda e: e.iota(spare_i, pattern=[[0, 1]], base=NODES, channel_multiplier=1))
    m_spare_i = pool(lambda e: e.iota(pow_i, pattern=[[0, 2]], base=127 + 63, channel_multiplier=-1))
    pool(lambda e: e.memset(identb, 0.0))
    pool(lambda e: e.memset(identh, 0.0))
    m = pool(lambda e: e.memset(ident, 0.0))
    m_identb = None
    for t in (identb, identh, ident):
        m_id = pool(lambda e, t=t: e.affine_select(out=t, in_=t, compare_op=ALU.not_equal, fill=1.0, base=0,
                                            pattern=[[-1, P]], channel_multiplier=1), [m])
        m_identb = m_identb or m_id
    m = pool(lambda e: e.memset(before, 0.0))
    pool(lambda e: e.affine_select(out=before, in_=before, compare_op=ALU.is_ge, fill=1.0, base=0,
                                   pattern=[[-1, P]], channel_multiplier=1), [m])
    pool(lambda e: e.iota(lane_i, pattern=[[0, 1]], base=0, channel_multiplier=1))
    m_iota = pool(lambda e: e.iota(iota_i, pattern=[[1, P]], base=0, channel_multiplier=0))
    m_idle = q.do("vector", v_i, lambda e: e.tensor_copy(src_i[:, ECOLS:ETILES], spare_i), [m_spare_i])
    m_zero = dve(lambda e: e.memset(zeros, 0.0))
    dve(lambda e: e.memset(ones, 1.0))
    dve(lambda e: e.memset(onesb, 1.0))
    dve(lambda e: e.memset(eps_t, EPS))
    dve(lambda e: e.memset(eps_s, EPS * XSCALE ** -2))
    dve(lambda e: e.tensor_copy(lane, lane_i), [m_iota])
    m_spare = dve(lambda e: e.tensor_copy(spare, spare_i))
    dve(lambda e: e.tensor_copy(iota, iota_i))
    dve(lambda e: e.tensor_copy(iotab, iota_i))
    m = dve(lambda e: e.tensor_scalar(pow_i, pow_i, 23, None, ALU.logical_shift_left))
    m_const = dve(lambda e: e.tensor_scalar(thresh, pow_i[:, 0:1].bitcast(F32), 2.5, None, ALU.mult), [m])
    powers = pow_i[:, 0:1].bitcast(F32)

    def idv(fn, after=()):
        return q.do("vector", v_i, fn, after)

    def load_ids(ids):
        q.do("sync", idx_d, lambda e: e.dma_start(src_i[:, 0:ECOLS], ids[0:ECOLS * P].rearrange("(p c) -> p c", c=ECOLS)))
        return q.do("sync", idx_d, lambda e: e.dma_start(
            src_i[0:EREST, ECOLS:ETILES], ids[ECOLS * P:EDGES].rearrange("(p c) -> p c", c=1)))

    q.wait("sync", [m_idle])
    m = load_ids(src)
    m2 = idv(lambda e: e.tensor_scalar(tmp_i, src_i, 7, None, ALU.arith_shift_right), [m])
    m3 = idv(lambda e: e.tensor_scalar(src_hi, tmp_i, 128.0, None, ALU.mult), [m2])
    m4 = idv(lambda e: e.tensor_scalar(tmp_i, src_i, 127, None, ALU.bitwise_and), [m3])
    m_parts = idv(lambda e: e.tensor_copy(src_lo, tmp_i), [m4])
    m1 = idv(lambda e: e.tensor_copy(src_f, src_i), [m])
    m_src = idv(lambda e: e.tensor_scalar(to_spare, src_f, -1.0, spare, ALU.mult, ALU.add), [m1, m_spare])

    tz = lines("table_zero", TABLES)
    m_tz = {}
    pieces = 5
    share = ROWS * RW // P // pieces
    rep = share // ZERO

    def zero_table(i, which):
        for a in which:
            m_tz[i] = q.do("sync", tz[i], lambda e, a=a: e.dma_start(
                table[i].rearrange("(p a) w -> p (a w)", p=P)[:, a * share:(a + 1) * share].rearrange(
                    "p (r c) -> p r c", r=rep),
                zeros.unsqueeze(1).to_broadcast([P, rep, ZERO])), [m_zero])

    zr = line("pad_zero", 16)

    def zero_pads():
        for rows in (xn_rows, y_rows):
            for a in range(NODES, ROWS, 75):
                m = q.do("sync", zr, lambda e, rows=rows, a=a: e.dma_start(
                    rows[a:a + 75, :], zeros[0:75, 0:DIM] if rows is y_rows else zeros[0:75, 0:DIM].bitcast(F16)))
        return m

    def load_dst():
        m = idv(lambda e: e.memset(src_i[:, ECOLS:ETILES], TILES * P), [m_src])
        q.wait("sync", [m])
        return load_ids(dst)

    def split_dst(m):
        m2 = idv(lambda e: e.tensor_scalar(tmp_i, src_i, 7, None, ALU.arith_shift_right), [m])
        m3 = idv(lambda e: e.tensor_copy(dst_hi, tmp_i), [m2])
        m4 = idv(lambda e: e.tensor_scalar(tmp_i, src_i, 127, None, ALU.bitwise_and), [m3])
        return idv(lambda e: e.tensor_copy(dst_lo, tmp_i), [m4])

    CH = -(-ETILES // P)
    id_t = big[:, 8000:8000 + CH * P].bitcast(BF16).rearrange("p (q i n) -> p q i n", q=CH, i=2)
    id_l, pe_i, a_i = line("id_rows_store", 16), line("index_pe"), line("index_act")
    m_turned, m_ids = {}, {}
    for c in range(CH):
        n = min(P, ETILES - c * P)
        bank = banks[c].bitcast(BF16)
        for i, v in enumerate((src_hi, src_lo)):
            m = q.do("tensor", pe_i, lambda e, c=c, n=n, i=i, v=v, bank=bank: e.transpose(
                bank[0:n, i * P:(i + 1) * P], v[:, c * P:c * P + n], identb), [m_parts, m_identb])
        m_turned[c] = q.do("scalar", a_i, lambda e, c=c, n=n, bank=bank: e.copy(
            id_t[0:n, c].rearrange("p i n -> p (i n)"), bank[0:n, 0:2 * P]), [m])

    def store_ids(c):
        n = min(P, ETILES - c * P)
        m_ids[c] = q.do("sync", id_l, lambda e: e.dma_start(
            id_rows[:, c * P * P:(c * P + n) * P].rearrange("a (c n) -> c a n", n=P), id_t[0:n, c]), [m_turned[c]])

    X = sb("edge_rows", [P, XRING, LOAD, XW])
    S = sb("same_node", [P, SRING, GROUP * P])
    O = sb("edge_sums", [P, ORING, GROUP, XW])
    IDR = sb("node_numbers", [P, 2, IDLOAD * P], BF16)
    dup = sb("dup", [P, ORING, GROUP])
    row_i = sb("row_i", [P, ORING, GROUP], I32)
    x_l, t_l, i_l = lines("edge_load", XRING), lines("table_add", TABLES), lines("ids_load", 2)
    pe_e, v_e, a_e = line("edge_pe"), line("edge_dve"), line("edge_act")
    ps_src, ps_sum = banks[0:2], banks[2]
    v_x = line("edge_const")
    m_idz = q.do("gpsimd", g_c, lambda e: e.memset(IDR, 0.0))
    q.do("vector", v_x, lambda e: e.memset(X[:, :, :, EDIM:EDIM + 1], 1.0))
    m_xc = q.do("vector", v_x, lambda e: e.tensor_copy(
        X[:, :, :, EDIM + 1:XW].rearrange("p a b c -> p (a b c)"), powers.to_broadcast([P, XRING * LOAD])), [m_const])
    loaded, id_loaded, srcs, sames, sums, evac, rowed, added = {}, {}, {}, {}, {}, {}, {}, {}

    def group_tiles(g):
        return list(range(g * GROUP, min(ETILES, (g + 1) * GROUP)))

    def load_edges(k):
        if k * LOAD >= ETILES:
            return
        free = [sums[(k - XRING + 1) * LOAD // GROUP - 1]] if k >= XRING else [m_xc]
        lo, hi = k * LOAD, min((k + 1) * LOAD, ECOLS)
        b = k % XRING
        if (k + 1) * LOAD > ECOLS:
            m = q.do("vector", v_x, lambda e: e.memset(X[:, b, ECOLS - lo, 0:EDIM], 0.0), free)
            q.do("sync", x_l[b], lambda e: e.dma_start(
                X[0:EREST, b, ECOLS - lo, 0:EDIM], edge_attr[ECOLS * P:EDGES, :]), [m])
        rows = edge_attr[0:ECOLS * P, :].rearrange("(p c) w -> p c w", c=ECOLS)
        loaded[k] = q.do("sync", x_l[b], lambda e: e.dma_start(X[:, b, 0:hi - lo, 0:EDIM], rows[:, lo:hi, :]), free)

    def load_ids_rows(k):
        lo, hi, b = k * IDLOAD * P, min((k + 1) * IDLOAD, ETILES) * P, k % 2
        if lo < hi:
            free = [srcs[(k - 1) * IDLOAD // GROUP - 1]] if k >= 2 else [m_idz]
            id_loaded[k] = q.do("sync", i_l[b], lambda e: e.dma_start(IDR[0:2, b, 0:hi - lo], id_rows[:, lo:hi]),
                                free + [m_ids[((k + 1) * IDLOAD - 1) // P if (k + 1) * IDLOAD < ETILES else CH - 1]])

    def edge_match(g):
        c0, n = g * GROUP, len(group_tiles(g))
        k, at_ = c0 // IDLOAD, c0 % IDLOAD * P
        srcs[g] = q.do("tensor", pe_e, lambda e: e.matmul(
            ps_src[g % 2][:, 0:n * P], onesb, IDR[:, k % 2, at_:at_ + n * P], start=True, stop=True),
            [id_loaded[k], sames.get(g - 2), m_const, m_turned[CH - 1]])

    def edge_same(g):
        c0, n = g * GROUP, len(group_tiles(g))
        sames[g] = q.do("vector", v_e, lambda e: e.tensor_tensor(
            S[:, g % SRING, 0:n * P].rearrange("p (a b) -> p a b", a=n),
            ps_src[g % 2][:, 0:n * P].rearrange("p (a b) -> p a b", a=n),
            src_f[:, c0:c0 + n].unsqueeze(2).to_broadcast([P, n, P]), ALU.is_equal),
            [srcs[g], m_src, sums.get(g - SRING)])

    def edge_sum(g):
        cs = group_tiles(g)
        for i, c in enumerate(cs):
            k = c // LOAD
            sums[g] = q.do("tensor", pe_e, lambda e, i=i, c=c, k=k: e.matmul(
                ps_sum[:, i * XW:(i + 1) * XW], S[:, g % SRING, i * P:(i + 1) * P], X[:, k % XRING, c % LOAD, :],
                start=True, stop=True), [sames[g], loaded[k], evac.get(g - 1)])
        n, o = len(cs), g % ORING
        free = [added[c] for c in group_tiles(g - ORING)] if g >= ORING else []
        evac[g] = q.do("scalar", a_e, lambda e: e.copy(
            O[:, o, 0:n, :], ps_sum[:, 0:n * XW].rearrange("p (a b) -> p a b", a=n)), [sums[g]] + free)

    def edge_rows_of(g):
        if g % 2 == 0 and g + 1 < GROUPS:
            return
        gs = [g - 1, g] if g % 2 else [g]
        cs = group_tiles(gs[0]) + (group_tiles(g) if g % 2 else [])
        n, o = len(cs), gs[0] % ORING
        free = [added[c] for h in gs for c in group_tiles(h - ORING)] if gs[0] >= ORING else []
        powers_ = O[:, o:o + len(gs), :, RW].rearrange("p a b -> p (a b)")[:, 0:n]
        d, r = (v[:, o:o + len(gs), :].rearrange("p a b -> p (a b)")[:, 0:n] for v in (dup, row_i))
        c0 = cs[0]
        m = q.do("vector", v_e, lambda e: e.scalar_tensor_tensor(
            d, powers_, thresh, to_spare[:, c0:c0 + n], ALU.is_gt, ALU.mult), [evac[g]])
        m = q.do("vector", v_e, lambda e: e.tensor_tensor(r, d, src_f[:, c0:c0 + n], ALU.add), [m] + free)
        for h in gs:
            rowed[h] = m

    def edge_add(g):
        o = g % ORING
        for i, c in enumerate(group_tiles(g)):
            t = c % TABLES
            added[c] = q.do("gpsimd", t_l[t], lambda e, i=i, t=t: e.indirect_dma_start(
                table[t], bass.IndirectOffsetOnAxis(ap=row_i[:, o, i:i + 1], axis=0), O[:, o, i, 0:RW], None,
                compute_op=ALU.add, bounds_check=ROWS - 1, oob_is_err=True),
                [evac[g], rowed[g], added.get(c - TABLES, m_tz[t])])

    hotA = sb("hotA", [P, 2, GROUP * TILES], BF16)
    hotB = sb("hotB", [P, 2, GROUP * P], BF16)
    v_h, pe_h = line("degree_dve"), line("degree_pe")
    ps_deg = banks[4]
    in_deg = sb("in_deg", [P, TILES], I32)
    done, hots = {}, {}

    def degree_hot(b):
        lo, n, r = b * GROUP, len(group_tiles(b)), b % 2
        q.do("vector", v_h, lambda e: e.tensor_tensor(
            hotA[:, r, 0:n * TILES].rearrange("p (a b) -> p a b", a=n),
            iotab[:, 0:TILES].unsqueeze(1).to_broadcast([P, n, TILES]),
            dst_hi[:, lo:lo + n].unsqueeze(2).to_broadcast([P, n, TILES]), ALU.is_equal),
            [done["dst"], m_const, done.get(("deg", b - 2))])
        hots[b] = q.do("vector", v_h, lambda e: e.tensor_tensor(
            hotB[:, r, 0:n * P].rearrange("p (a b) -> p a b", a=n),
            iotab.unsqueeze(1).to_broadcast([P, n, P]),
            dst_lo[:, lo:lo + n].unsqueeze(2).to_broadcast([P, n, P]), ALU.is_equal))

    def degree_sum(b):
        r = b % 2
        for i, c in enumerate(group_tiles(b)):
            done["deg", b] = q.do("tensor", pe_h, lambda e, i=i, c=c: e.matmul(
                ps_deg[:, 0:TILES], hotB[:, r, i * P:(i + 1) * P], hotA[:, r, i * TILES:(i + 1) * TILES],
                start=(c == 0), stop=(c == ETILES - 1)), [hots[b]])

    d_m, v_m, a_m, pe_m = line("mix_dma", 16), line("mix_dve"), line("mix_act"), line("mix_pe")
    state = sb("state", [P, TILES, DIM])
    xnT = big.rearrange("p (t k n) -> p t k n", t=TILES, k=KC)
    mixw = sb("mixw", [P, 8192])
    at = [0]

    def part(n):
        at[0] += n
        return mixw[:, at[0] - n:at[0]]

    wqkv = part(KC * 3 * INNER).rearrange("p (k n) -> p k n", k=KC)
    wout = part(PAIRS * DIM).rearrange("p (j n) -> p j n", j=PAIRS)
    squares = part(2 * INNER)
    ks = part(INNER)
    k_raw = part(2 * INNER).rearrange("p (r n) -> p r n", r=2)
    vs = part(2 * INNER).rearrange("p (r n) -> p r n", r=2)
    xn = part(2 * DIM).rearrange("p (r n) -> p r n", r=2)
    folded = squares.rearrange("p (j n) -> p j n", j=PAIRS)
    wqT = k_raw.rearrange("p r n -> p (r n)").rearrange("p (j n) -> p j n", j=PAIRS)
    dotsT = ks.rearrange("p (j n) -> p j n", j=PAIRS)
    term = mixw[:, 0:3 * 2 * DIM].rearrange("p (r i n) -> p r i n", r=3, i=2)
    mq = sb("mq", [P, KC, DIM])
    mv = sb("mv", [P, TILES, 2])
    stats = sb("stats", [P, 2, 6])
    rstd = sb("rstd", [P, TILES])
    both = sb("both", [P, 2, TILES])
    wmean = sb("wmean", [P, KC * 2 * HEADS])
    ss = sb("ss", [P, 2 * HEADS])
    sd = sb("sd", [P, 2 * HEADS])
    rkv = sb("rkv", [P, HEADS])
    ps_xT, ps_dots, ps_kv = banks[3], banks[5], banks[6:8]
    vec = {n: sb("bc_" + n, [P, DIM]) for n in ("w_cent", "b_cent", "w_vor", "b_vor", "b_sum")}
    b_out0 = sb("b_out0", [P, DIM])
    node_v = sb("node_v", [P, 2, TILES])
    node_r = big[:, 3000:3000 + 2 * P].rearrange("p (i n) -> p i n", i=2)
    x_d = lines("x_load", 7)
    wsum = sb("wsum", [P, DIM])
    wr_t = sb("wr_t", [P, KC, EXPERTS])
    br_t = sb("br_t", [P, EXPERTS])

    def mixv(fn, after=()):
        return q.do("vector", v_m, fn, after)

    def mixa(fn, after=()):
        return q.do("scalar", a_m, fn, after)

    def mixp(fn, after=()):
        return q.do("tensor", pe_m, fn, after)

    def load_x(i):
        per = TILES // 7
        lo, hi = i * per, min((i + 1) * per, TILES - 1)
        for a in range(lo, hi, 2):
            b = min(a + 2, hi)
            m = q.do("sync", x_d[i], lambda e, a=a, b=b: e.dma_start(
                state[:, a:b, :], x[a * P:b * P, :].rearrange("(t p) n -> p t n", p=P)))
        if i == 6:
            m = q.do("sync", x_d[i], lambda e: e.dma_start(state[0:LAST, TILES - 1, :], x[(TILES - 1) * P:NODES, :]), [m_padded])
        return m

    m_padded = mixv(lambda e: e.memset(state[:, TILES - 1, :], 0.0))
    mixv(lambda e: e.memset(b_out0, 0.0))
    m_blank = mixv(lambda e: e.memset(node_r, 0.0))

    def load_small():
        for k in range(KC):
            for c in range(3):
                q.do("sync", d_m, lambda e, k=k, c=c: e.dma_start(
                    wqkv[:, k, c * INNER:(c + 1) * INNER], w_qkv[k * P:(k + 1) * P, c * INNER:(c + 1) * INNER]), [m_blank])
            yield
        for j in range(PAIRS):
            q.do("sync", d_m, lambda e, j=j: e.dma_start(wout[:, j, :], w_out[j * P:(j + 1) * P, :]))
        yield
        for n, v in (("w_cent", w_cent[0]), ("b_cent", b_cent), ("w_vor", w_vor[0]), ("b_vor", b_vor),
                     ("b_sum", b_sum)):
            q.do("sync", d_m, lambda e, n=n, v=v: e.dma_start(vec[n], v.partition_broadcast(P)))
        yield
        for i, v in enumerate((cent, vor)):
            q.do("sync", d_m, lambda e, i=i, v=v: e.dma_start(
                node_r[0:TILES - 1, i, :], v[0:(TILES - 1) * P, :].rearrange("(t p) o -> t (p o)", p=P)))
            q.do("sync", d_m, lambda e, i=i, v=v: e.dma_start(
                node_r[TILES - 1:TILES, i, 0:LAST], v[(TILES - 1) * P:NODES, :].rearrange("(a p) o -> a (p o)", a=1)))
        q.do("sync", d_m, lambda e: e.dma_start(b_out0[0:1, :], b_out.rearrange("(a n) -> a n", a=1)))
        q.do("sync", d_m, lambda e: e.dma_start(wsum, w_sum))
        q.do("sync", d_m, lambda e: e.dma_start(wr_t, wr.rearrange("(k p) n -> p k n", p=P)))
        done["small"] = q.do("sync", d_m, lambda e: e.dma_start(br_t, br.partition_broadcast(P)))
        yield

    def norm_stats(queue, rows, stat, to, after):
        m = queue(lambda e: e.bn_stats(stat, rows), after)
        return queue(lambda e: e.bn_aggr(to, stat), [m])

    def norm_steps():
        per = TILES // 7
        small = load_small()
        got = {0: load_x(0)}
        yield
        for i in range(7):
            if i < 6:
                got[i + 1] = load_x(i + 1)
            for t in range(i * per, TILES if i == 6 else (i + 1) * per):
                m = norm_stats(mixv, state[:, t, :], stats[:, t % 2, :], mv[:, t, :], [got[i]])
                if t % 2:
                    yield
            next(small, None)
            yield
        m = mixa(lambda e: e.activation(rstd, mv[:, :, 1], ACT.Sqrt, bias=eps_t), [m])
        m = mixv(lambda e: e.reciprocal(rstd, rstd), [m])
        mixv(lambda e: e.tensor_scalar(both[:, 0, :], rstd, 1.0, None, ALU.add), [m])
        done["rstd"] = mixv(lambda e: e.scalar_tensor_tensor(both[:, 1, :], rstd, -1.0, mv[:, :, 0], ALU.mult, ALU.mult), [m])
        for i in range(2):
            m = mixp(lambda e, i=i: e.transpose(ps_xT[:, i * P:i * P + TILES], node_r[0:TILES, i, :],
                                                ident[0:TILES, 0:TILES]), [done["small"], m_const])
        done["node_v"] = mixv(lambda e: e.tensor_copy(
            node_v, ps_xT[:, 0:2 * P].rearrange("p (i n) -> p i n", i=2)[:, :, 0:TILES]), [m])
        for k in range(KC):
            m = mixv(lambda e, k=k: e.reduce_sum(wmean[:, k * 2 * HEADS:(k + 1) * 2 * HEADS],
                                                 kvw[:, k, :].rearrange("p (h d) -> p h d", d=DH), AX.X), [done["small"]])
        m = mixv(lambda e: e.tensor_scalar(wmean, wmean, 1.0 / DH, None, ALU.mult), [m])
        for k in range(KC):
            wk = kvw[:, k, :].rearrange("p (h d) -> p h d", d=DH)
            done["kvw"] = mixv(lambda e, k=k, wk=wk: e.tensor_tensor(
                wk, wk, wmean[:, k * 2 * HEADS:(k + 1) * 2 * HEADS].unsqueeze(2).to_broadcast([P, 2 * HEADS, DH]),
                ALU.subtract), [m])
        yield

    kvw = wqkv[:, :, INNER:3 * INNER]
    mx = {}

    def mix_norm(t):
        r = t % 2
        m = mixa(lambda e: e.activation(xn[:, r, :], state[:, t, :], ACT.Identity, bias=both[:, 1, t:t + 1],
                                        scale=rstd[:, t:t + 1]), [done["rstd"], mx.get(("turn", t - 2))])
        mx["xn", t] = m
        mixa(lambda e: e.activation(state[:, t, :], state[:, t, :], ACT.Identity, bias=both[:, 1, t:t + 1],
                                    scale=both[:, 0, t:t + 1]), [m])

    def mix_turn(t):
        for k in range(KC):
            mx["turn", t] = mixp(lambda e, k=k: e.transpose(
                ps_xT[:, k * P:(k + 1) * P], xn[:, t % 2, k * P:(k + 1) * P], ident),
                [mx["xn", t], mx.get(("xT", t - 1)), done["node_v"], m_const])

    def mix_keep(t):
        mx["xT", t] = mixa(lambda e: e.copy(big[:, t * DIM:(t + 1) * DIM], ps_xT[:, 0:DIM]),
                           [mx["turn", t], m_ids[CH - 1], done["dst"], done["node_v"]] + (done["weights"] if t >= W_AT // DIM else done["b1 all"]))

    def mix_half(h):
        def product(t):
            for k in range(KC):
                mx["kv", h, t] = mixp(lambda e, k=k: e.matmul(
                    ps_kv[h], xnT[:, t, k, :], kvw[:, k, h * INNER:(h + 1) * INNER],
                    start=(k == 0), stop=(k == KC - 1)),
                    [mx["xT", t], done["kvw"], mx.get(("out", h, t - 1)), done["b1"]])
        return product

    def mix_out(h):
        def out_of(t):
            mixa(lambda e: e.activation(squares[:, h * INNER:(h + 1) * INNER], ps_kv[h], ACT.Square),
                 [mx["kv", h, t], mx.get(("ss", h, t - 1))])
            mx["out", h, t] = mixa(lambda e: e.copy((k_raw, vs)[h][:, t % 2, :], ps_kv[h]),
                                   [mx.get(("dots", t - 2)), mx.get(("ks", t - 2))])
        return out_of

    def mix_squares(h):
        def sums(t):
            mx["ss", h, t] = mixv(lambda e: e.reduce_sum(
                ss[:, h * HEADS:(h + 1) * HEADS], squares[:, h * INNER:(h + 1) * INNER].rearrange("p (h d) -> p h d", d=DH),
                AX.X), [mx["out", h, t], mx.get(("sd", t - 1))])
        return sums

    def mix_sd(t):
        mx["sd", t] = mixa(lambda e: e.activation(sd, ss, ACT.Sqrt, bias=eps_t, scale=1.0 / DH),
                           [mx["ss", 1, t], mx.get(("ks", t - 1))])

    def mix_keys(t):
        m = mixv(lambda e: e.tensor_tensor(rkv, sd[:, 0:HEADS], sd[:, HEADS:2 * HEADS], ALU.mult), [mx["sd", t]])
        m = mixv(lambda e: e.reciprocal(rkv, rkv), [m])
        mx["ks", t] = mixv(lambda e: e.tensor_tensor(
            ks.rearrange("p (h d) -> p h d", d=DH), k_raw[:, t % 2, :].rearrange("p (h d) -> p h d", d=DH),
            rkv.unsqueeze(2).to_broadcast([P, HEADS, DH]), ALU.mult), [m, mx.get(("dots", t - 1))])

    def mix_dots(t):
        for j in range(PAIRS):
            mx["dots", t] = mixp(lambda e, j=j: e.matmul(
                ps_dots[:, j * P:(j + 1) * P], vs[:, t % 2, j * P:(j + 1) * P], ks[:, j * P:(j + 1) * P],
                start=(t == 0 and j == 0), stop=(t == TILES - 1 and j == PAIRS - 1), skip_group_check=True),
                [mx["ks", t], mx["out", 1, t]])

    def fold_steps():
        last = TILES - 1
        for j in range(PAIRS):
            for k in range(KC):
                c = j * KC + k
                m = mixp(lambda e, j=j, k=k, c=c: e.transpose(
                    ps_kv[c // 4][:, c % 4 * P:(c % 4 + 1) * P], wqkv[:, k, j * P:(j + 1) * P], ident),
                    [mx["out", 0, last], mx["out", 1, last]])
        for h in range(2):
            ma = mixa(lambda e, h=h: e.copy(wqT[:, 2 * h:2 * h + 2, :].rearrange("p a b -> p (a b)"), ps_kv[h]), [m, mx["ks", last]])
        m = mixv(lambda e: e.memset(dotsT, 0.0), [mx["dots", last]])
        for s in range(2):
            w = slice(s * DH, (s + 1) * DH)
            md = mixv(lambda e, w=w: e.tensor_scalar(
                dotsT[w, :, w], ps_dots[w, :].rearrange("p (j n) -> p j n", j=PAIRS)[:, :, w], 1.0 / NODES, None, ALU.mult),
                [m, mx["dots", last]])
        yield
        for j in range(PAIRS):
            m = mixp(lambda e, j=j: e.matmul(ps_kv[j // 2][:, j % 2 * DIM:(j % 2 + 1) * DIM], dotsT[:, j, :],
                                             wout[:, j, :], start=True, stop=True), [md, ma])
        for h in range(2):
            m = mixa(lambda e, h=h: e.copy(folded[:, 2 * h:2 * h + 2, :].rearrange("p a b -> p (a b)"), ps_kv[h]), [m, mx["ss", 1, last]])
        yield
        for k in range(KC):
            for j in range(PAIRS):
                mp = mixp(lambda e, j=j, k=k: e.matmul(
                    ps_kv[k][:, 0:DIM], wqT[:, j, k * P:(k + 1) * P], folded[:, j, :],
                    start=(j == 0), stop=(j == PAIRS - 1)), [m])
        for k in range(KC):
            done["mq"] = mixa(lambda e, k=k: e.copy(mq[:, k, :], ps_kv[k][:, 0:DIM]), [mp])
        yield

    ps_rest = [ps_kv[0], ps_kv[1], ps_xT, ps_dots]

    def rest_products(t):
        for k in range(KC):
            mixp(lambda e, k=k: e.matmul(
                ps_rest[t % 4][:, 0:DIM], xnT[:, t, k, :], mq[:, k, :], start=(k == 0), stop=False),
                [done["mq"], mx.get(("rest added", t - 4))])
        mixp(lambda e: e.matmul(ps_rest[t % 4][:, 0:DIM], ones, b_out0, start=False, stop=False), [done["small"], m_const])
        for i, n in enumerate(("cent", "vor")):
            mx["lin", t] = mixv(lambda e, i=i, n=n: e.scalar_tensor_tensor(
                term[:, t % 3, i, :], vec["w_" + n], node_v[:, i, t:t + 1], vec["b_" + n], ALU.mult, ALU.add),
                [mx.get(("state", t - 3)), done["node_v"], done["mq"]])

    def rest_sigmoid(t):
        tt = term[:, t % 3].rearrange("p i n -> p (i n)")
        mx["sig", t] = mixa(lambda e: e.activation(tt, tt, ACT.Sigmoid), [mx["lin", t]])

    def rest_more(t):
        mx["rest", t] = mixp(lambda e: e.matmul(ps_rest[t % 4][:, 0:DIM], ident, term[:, t % 3, 1, :], start=False, stop=True),
                             [mx["sig", t]])

    def rest_add(t):
        st = state[:, t, :]
        mx["half", t] = mixv(lambda e: e.tensor_tensor(st, st, term[:, t % 3, 0, :], ALU.add), [mx["sig", t]])

    def rest_last(t):
        st = state[:, t, :]
        mx["rest added", t] = mixv(lambda e: e.tensor_tensor(st, st, ps_rest[t % 4][:, 0:DIM], ALU.add),
                                   [mx["half", t], mx["rest", t]])
        mx["state", t] = done["mix"] = mx["rest added", t]

    W_AT = 17 * DIM
    WN = KC * HID
    assert W_AT + 4 * WN <= TILES * DIM
    w_l, hi_s, lo_s = lines("w_raw_load", 3), lines("w_high_store", 2), lines("w_low_store", 3)
    v_w, pe_w, a_w = line("w_dve"), line("w_pe"), line("w_act")
    w_ld, m_s = line("small_load", 16), line("meta_store", 16)
    pk_s, pk_l, bp_d = lines("peak_store", 2), lines("peak_load", 2), line("b1_peak_dma", 16)
    RAW = 3
    raw = [big[:, W_AT + r * WN:W_AT + (r + 1) * WN] for r in range(RAW)]
    high = [big[:, W_AT + RAW * WN + r * WN // 2:W_AT + RAW * WN + (r + 1) * WN // 2].bitcast(F16) for r in range(2)]
    low = [v[:, 0:WN // 2].bitcast(F16) for v in raw]
    ln_t = sb("ln_t", [P, 2, EXPERTS, KC])
    ln_r = big[0:2 * EXPERTS * KC, 3400:3400 + P]
    b1_r = big[0:EXPERTS * HC, 3600:3600 + P]
    b1_fold = big[0:EXPERTS, 0:HID]
    b1_all = big[:, HID:HID + EXPERTS * P]
    offset = sb("offset", [P, KC, EXPERTS * EXPERTS])
    b1_t = sb("b1_t", [P, EXPERTS, META])
    peak_k = sb("peak_k", [P, 2 * EXPERTS, KC])
    peaks = sb("peaks", [P, 3 * EXPERTS])
    peak_all = sb("peak_all", [P, 2, P])
    tops = sb("tops", [P, 3 * EXPERTS])
    expo = sb("expo", [P, 3 * EXPERTS], I32)
    sc_i = sb("sc_i", [P, 2 * EXPERTS], I32)
    gain_a = sb("gain_a", [P, EXPERTS, KC])
    gain_s = sb("gain_s", [P, EXPERTS, KC])
    scale_of = sc_i.bitcast(F32)
    got, stored, looked, folds, tall = {}, {}, {}, {}, {}

    def wv(fn, after=()):
        return q.do("vector", v_w, fn, after)

    def matrix(n):
        return n // EXPERTS, n % EXPERTS, n % RAW

    def w_load(n):
        which, ex, r = matrix(n)
        src_ = w2[ex].rearrange("(h p) n -> p h n", p=P) if which else w1[ex].rearrange("(k p) n -> p k n", p=P)
        to = raw[r].rearrange("p (h n) -> p h n", h=HC if which else KC)
        if which:
            cuts = [(slice(a, a + 1), slice(0, DIM)) for a in range(HC)]
        else:
            cuts = [(slice(k, k + 1), slice(a, a + DIM)) for k in range(KC) for a in range(0, HID, DIM)]
        for a, b in cuts:
            got[n] = q.do("sync", w_l[r], lambda e, a=a, b=b: e.dma_start(to[:, a, b], src_[:, a, b]),
                          [m_ids[CH - 1], done["dst"], stored.get(("low", n - RAW)), looked.get((1, n - RAW)), folds.get(n - RAW)])

    def w_small():
        for i, v in enumerate((ln_g, ln_b)):
            q.do("sync", w_ld, lambda e, i=i, v=v: e.dma_start(
                ln_r[i * EXPERTS * KC:(i + 1) * EXPERTS * KC, :], v.rearrange("e (k p) -> (e k) p", p=P)))
        m = q.do("sync", w_ld, lambda e: e.dma_start(b1_r, b1.rearrange("e (h p) -> (e h) p", p=P)))
        mz = wv(lambda e: e.memset(offset, 0.0))
        yield
        nl = 2 * EXPERTS * KC
        q.do("tensor", pe_w, lambda e: e.transpose(ps_kv[0][:, 0:nl], ln_r, ident[0:nl, 0:nl]), [m, m_const])
        m = q.do("tensor", pe_w, lambda e: e.transpose(ps_kv[0][:, P:P + EXPERTS * HC], b1_r,
                                                       ident[0:EXPERTS * HC, 0:EXPERTS * HC]))
        m = wv(lambda e: e.tensor_copy(ln_t.rearrange("p i e k -> p (i e k)"), ps_kv[0][:, 0:nl]), [m])
        wv(lambda e: e.tensor_copy(
            b1_t[:, :, 0:HC], ps_kv[0][:, P:P + EXPERTS * HC].rearrange("p (e h) -> p e h", h=HC)))
        wv(lambda e: e.tensor_scalar(gain_a.bitcast(I32).rearrange("p e k -> p (e k)"),
                                     ln_t[:, 0].rearrange("p e k -> p (e k)").bitcast(I32), 0x7fffffff, None,
                                     ALU.bitwise_and), [m])
        for k in range(KC):
            done["ln"] = wv(lambda e, k=k: e.tensor_copy(offset[:, k, 0:EXPERTS * EXPERTS:EXPERTS + 1], ln_t[:, 1, :, k]), [m, mz])
        yield

    def w_look(k):
        def look(n):
            which, ex, r = matrix(n)
            looked[k, n] = wv(lambda e: e.tensor_reduce(
                peak_k[:, n, k:k + 1], raw[r][:, k * HID:(k + 1) * HID], AX.X, ALU.max, apply_absolute_value=True), [got[n]])
            if not which:
                for c in range(2):
                    folds[n] = q.do("tensor", pe_w, lambda e, c=c: e.matmul(
                        ps_kv[c][0:EXPERTS, :], offset[:, k, ex * EXPERTS:(ex + 1) * EXPERTS],
                        raw[r][:, k * HID + c * INNER:k * HID + (c + 1) * INNER],
                        start=(ex == 0 and k == 0), stop=(ex == EXPERTS - 1 and k == KC - 1)), [got[n], done["ln"]])
        return look

    def w_peak(n):
        which, ex, r = matrix(n)
        m = looked[KC - 1, n]
        if not which:
            m = wv(lambda e: e.tensor_tensor(peak_k[:, n, :], peak_k[:, n, :], gain_a[:, ex, :], ALU.mult), [m])
        m = wv(lambda e: e.reduce_max(peaks[:, n:n + 1], peak_k[:, n, :], AX.X), [m])
        tall[n] = q.do("sync", pk_s[n % 2], lambda e: e.dma_start(
            peak_rows[n:n + 1, :].rearrange("o p -> p o"), peaks[:, n:n + 1]), [m])

    def w_spread(n):
        tall["all", n] = q.do("sync", pk_l[n % 2], lambda e: e.dma_start(
            peak_all[:, n % 2, :], peak_rows[n].partition_broadcast(P)), [tall[n], looked.get(("scale", n - 2))])

    def exponents(cols):
        m = wv(lambda e: e.tensor_scalar(expo[:, cols], tops[:, cols].bitcast(I32), 23, None, ALU.logical_shift_right),
               [Mark(v_w.sem, v_w.count)])
        return wv(lambda e: e.tensor_scalar(expo[:, cols], expo[:, cols], 30.0, 240.0, ALU.max, ALU.min), [m])

    def w_scale(n):
        which, ex, r = matrix(n)
        looked["scale", n] = wv(lambda e: e.reduce_max(tops[:, n:n + 1], peak_all[:, n % 2, :], AX.X), [tall["all", n]])
        m = exponents(slice(n, n + 1))
        m = wv(lambda e: e.tensor_scalar(sc_i[:, n:n + 1], expo[:, n:n + 1], -1.0, float(2 * BIAS + TOP), ALU.mult, ALU.add), [m])
        m = wv(lambda e: e.tensor_scalar(sc_i[:, n:n + 1], sc_i[:, n:n + 1], 23, None, ALU.logical_shift_left), [m])
        if not which:
            m = wv(lambda e: e.tensor_scalar(gain_s[:, ex, :], ln_t[:, 0, ex, :], scale_of[:, n:n + 1], None, ALU.mult), [m])
        looked["scaled", n] = m

    def scale_col(n, k):
        which, ex, r = matrix(n)
        return scale_of[:, n:n + 1] if which else gain_s[:, ex, k:k + 1]

    def w_store(n, i, l, part_, m):
        which, ex, r = matrix(n)
        for a in range(0, WN, WN // 2):
            stored[("high", "low")[i], n] = q.do("sync", l, lambda e, a=a: e.dma_start(
                w_parts[which][ex][:, i * WN + a:i * WN + a + WN // 2], part_[:, a:a + WN // 2]), [m])

    def w_high(n):
        which, ex, r = matrix(n)
        for k in range(KC):
            w = slice(k * HID, (k + 1) * HID)
            looked["high", n] = q.do("scalar", a_w, lambda e, w=w, k=k: e.activation(
                high[n % 2][:, w], raw[r][:, w], ACT.Copy, scale=scale_col(n, k)), [looked["scaled", n], stored.get(("high", n - 2)), looked.get(("low", n - 2))])
        w_store(n, 0, hi_s[n % 2], high[n % 2], looked["high", n])

    def w_low(k):
        def step(n):
            which, ex, r = matrix(n)
            w = slice(k * HID, (k + 1) * HID)
            looked["low", n] = wv(lambda e: e.scalar_tensor_tensor(
                low[r][:, w], raw[r][:, w], scale_col(n, k), high[n % 2][:, w], ALU.mult, ALU.subtract),
                [looked["high", n], looked.get(("low", n)), folds.get(n)])
            if k == KC - 1:
                w_store(n, 1, lo_s[r], low[r], looked["low", n])
        return step

    def b1_rows(n):
        for c in range(2):
            done["b1 rows"] = q.do("scalar", a_w, lambda e, c=c: e.copy(
                b1_fold[:, c * INNER:(c + 1) * INNER], ps_kv[c][0:EXPERTS, :]), [folds[n]])

    def b1_columns(n):
        for h in range(HC):
            m = q.do("tensor", pe_w, lambda e, h=h: e.transpose(
                ps_kv[0][:, h * EXPERTS:(h + 1) * EXPERTS], b1_fold[:, h * P:(h + 1) * P], ident[0:EXPERTS, 0:EXPERTS]),
                [done["b1 rows"]])
        done["b1"] = wv(lambda e: e.tensor_tensor(
            b1_t[:, :, 0:HC], b1_t[:, :, 0:HC], ps_kv[0][:, 0:EXPERTS * HC].rearrange("p (h e) -> p e h", e=EXPERTS), ALU.add),
            [m])
        m = wv(lambda e: e.tensor_reduce(peaks[:, 2 * EXPERTS:3 * EXPERTS], b1_t[:, :, 0:HC], AX.X, ALU.max,
                                         apply_absolute_value=True), [done["b1"]])
        done["b1 peaks"] = q.do("sync", bp_d, lambda e: e.dma_start(
            b1_peak_rows, peaks[:, 2 * EXPERTS:3 * EXPERTS]), [m])

    def b1_spread(n):
        done["b1 spread"] = q.do("sync", bp_d, lambda e: e.dma_start(
            b1_all, b1_peak_rows.rearrange("p e -> (p e)").partition_broadcast(P)), [done["b1 peaks"]])

    def b1_top(n):
        m = wv(lambda e: e.reduce_max(tops[:, 2 * EXPERTS:3 * EXPERTS], b1_all.rearrange("p (n e) -> p e n", e=EXPERTS), AX.X),
               [done["b1 spread"]])
        done["b1 all"] = [m]

    def once(fn):
        return lambda n: fn(n) if n == EXPERTS - 1 else None

    def meta_steps():
        e1, e2, eh = (expo[:, i * EXPERTS:(i + 1) * EXPERTS] for i in range(3))
        wv(lambda e: e.scalar_tensor_tensor(
            tops[:, 2 * EXPERTS:3 * EXPERTS], tops[:, 0:EXPERTS], float(DIM), tops[:, 2 * EXPERTS:3 * EXPERTS], ALU.mult, ALU.add),
            [Mark(v_w.sem, v_w.count)])
        m = exponents(slice(2 * EXPERTS, 3 * EXPERTS))
        bi = b1_t.bitcast(I32)
        x_exp = XSCALE.hex().split("p")[1]
        wv(lambda e: e.tensor_scalar(bi[:, :, HC], e1, float(-TOP - int(x_exp)), None, ALU.add), [m])
        wv(lambda e: e.tensor_scalar(bi[:, :, HC + 1], eh, -1.0, float(2 * BIAS + TOP), ALU.mult, ALU.add))
        m = wv(lambda e: e.tensor_tensor(bi[:, :, HC + 2], e2, eh, ALU.add))
        m = wv(lambda e: e.tensor_scalar(bi[:, :, HC + 2], bi[:, :, HC + 2], float(-BIAS - 2 * TOP), 1.0, ALU.add, ALU.max), [m])
        m = wv(lambda e: e.tensor_scalar(bi[:, :, HC + 2], bi[:, :, HC + 2], 254.0, None, ALU.min), [m])
        m = wv(lambda e: e.tensor_scalar(bi[:, :, HC:META], bi[:, :, HC:META], 23, None, ALU.logical_shift_left), [m])
        done["meta"] = q.do("sync", m_s, lambda e: e.dma_start(meta.rearrange("e p n -> p e n"), b1_t), [m])
        done["weights"] = [stored[i, n] for i in ("high", "low") for n in range(2 * EXPERTS - RAW, 2 * EXPERTS)] + [done["meta"]]
        yield

    zero_table(0, range(3))
    store_ids(0)
    zero_table(0, range(3, pieces))
    load_ids_rows(0)
    load_edges(0)
    load_edges(1)
    zero_table(1, range(1))
    for c in range(1, CH):
        store_ids(c)
    zero_table(1, range(1, pieces))
    load_edges(2)
    for i in range(2, TABLES):
        zero_table(i, range(pieces))
    m_dst = load_dst()
    m_pad = zero_pads()

    def load_step(g):
        if g * GROUP % LOAD == 0:
            load_edges(g * GROUP // LOAD + XRING - 1)
        if g * GROUP % IDLOAD == 0:
            load_ids_rows(g * GROUP // IDLOAD + 1)

    def chain(*gens):
        for g in gens:
            yield from g

    def idle(t):
        pass

    def pause(n):
        for _ in range(n):
            yield

    def beside(a, b):
        alive = [a, b]
        while alive:
            alive = [g for g in alive if next(g, alive) is not alive]
            yield

    edges = q.skewed(GROUPS, 1, [edge_match, edge_same, lambda g: (edge_sum(g), load_step(g)), edge_rows_of, idle, edge_add])
    degree = q.skewed(GROUPS, 1, [degree_hot, degree_sum])
    mix1 = q.skewed(TILES, 3, [mix_norm, mix_turn, mix_keep, mix_half(0), mix_out(0), (mix_squares(0), mix_half(1)), mix_out(1),
                               mix_squares(1), mix_sd, mix_keys, mix_dots])
    mix2 = q.skewed(TILES, 1, [rest_products, rest_sigmoid, rest_more, lambda t: (rest_add(t), rest_last(t))])
    weights = q.skewed(2 * EXPERTS, WEVERY, [
        w_load, idle, idle, idle, w_look(0), w_look(1), (w_peak, once(b1_rows)), (w_spread, once(b1_columns)), once(b1_spread),
        once(b1_top), w_scale, w_high, w_low(0), w_low(1)])
    side = chain(beside(chain(w_small(), weights, meta_steps()), chain(norm_steps(), pause(12), mix1)), fold_steps(), mix2)
    side_steps = 43 + (TILES * 3 + 8) + 3 + TILES + 3
    due, owed, ended = 0.0, 0.0, []
    for g, _ in enumerate(edges):
        if g < START:
            continue
        if g == START:
            done["dst"] = split_dst(m_dst)
        owed += DEGREES if g > START + WEVERY * 2 * EXPERTS + 10 else 0
        while owed >= 1:
            next(degree, None)
            owed -= 1
        due += side_steps / (GROUPS - 4 - START)
        while due >= 1:
            if next(side, ended) is ended:
                due = -1e9
            due -= 1
    for _ in side:
        pass
    for _ in degree:
        pass
    done["in_deg"] = q.do("vector", v_h, lambda e: e.tensor_scalar(
        in_deg, ps_deg[:, 0:TILES], float(DEG - 1), None, ALU.min), [done["deg", GROUPS - 1]])

    at[0] = 0
    PR, YR, HR = 8, 5, 3
    parts = part(PR * TABLES * RW).rearrange("p (r a w) -> p r a w", r=PR, a=TABLES)
    sumT = part(2 * P).rearrange("p (r n) -> p r n", r=2)
    diag = part(2 * P).rearrange("p (r n) -> p r n", r=2)
    y = part(YR * DIM).rearrange("p (r n) -> p r n", r=YR)
    yT = part(2 * DIM).rearrange("p (r n) -> p r n", r=2)
    xh = part(HR * DIM).bitcast(F16).rearrange("p (r i n) -> p r i n", r=HR, i=2)
    count = sb("count", [P, TILES])
    out_deg = sb("out_deg", [P, TILES], I32)
    mv2 = sb("mv2", [P, TILES, 2])
    r1 = sb("r1", [P, TILES])
    r2 = sb("r2", [P, TILES])
    p_l, zi_l, zo_l = lines("parts_load", PR // 2), lines("zin_add", 4), lines("zout_add", 4)
    xs_l, ys_l = lines("xn_store", HR), line("y_store", 16)
    v_n, a_n, pe_n = line("node_dve"), line("node_act"), line("node_pe")
    ps_t, ps_s, ps_y, ps_log = banks[0:2], banks[2:4], banks[5:7], banks[7]
    all_added = [added[c] for c in range(ETILES - TABLES, ETILES)]
    edges_done = [Mark(l.sem, l.count) for l in (v_m, pe_m, a_m, v_e, a_e, pe_e, v_h)]
    nd = {}

    def nv(fn, after=()):
        return q.do("vector", v_n, fn, after)

    def na(fn, after=()):
        return q.do("scalar", a_n, fn, after)

    def npe(fn, after=()):
        return q.do("tensor", pe_n, fn, after)

    def rows_of(t):
        return LAST if t == TILES - 1 else P

    def degree_row(t, lines_, z, deg, after):
        return q.do("gpsimd", lines_[t % 4], lambda e: e.indirect_dma_start(
            state[:, t, :], None, z, bass.IndirectOffsetOnAxis(ap=deg[:, t:t + 1], axis=0),
            compute_op=ALU.add, bounds_check=DEG - 1, oob_is_err=True), after)

    def node_load(t):
        if t % 2 == 0:
            n = min(2, TILES - t)
            for a in range(TABLES):
                nd["parts", t] = q.do("sync", p_l[t // 2 % (PR // 2)], lambda e, a=a: e.dma_start(
                    parts[:, t % PR:t % PR + n, a, :],
                    table[a][t * P:(t + n) * P, :].rearrange("(t p) w -> p t w", p=P)),
                    all_added + edges_done + [nd.get(("sum", t - PR + 1)), nd.get(("count", t - PR + 1))])
            nd["parts", t + 1] = nd["parts", t]
        nd["zin", t] = degree_row(t, zi_l, z_in, in_deg, [done["in_deg"], done["mix"], nd.get(("zin", t - 4))])

    def node_count(t):
        nd["counted", t] = nv(lambda e: e.reduce_sum(
            count[:, t:t + 1], parts[:, t % PR, :, EDIM:RW].rearrange("p a w -> p (a w)"), AX.X), [nd["parts", t]])

    def node_degree(t):
        nd["count", t] = nv(lambda e: e.tensor_scalar(
            out_deg[:, t:t + 1], count[:, t:t + 1], float(DEG - 1), None, ALU.min), [nd["counted", t]])

    def node_sum(t):
        nd["zout", t] = degree_row(t, zo_l, z_out, out_deg, [nd["count", t], nd["zin", t], nd.get(("zout", t - 4))])
        for a in range(TABLES):
            nd["sum", t] = npe(lambda e, a=a: e.matmul(
                ps_t[t % 2][:, 0:P], parts[:, t % PR, a, 0:EDIM], ident, start=(a == 0), stop=(a == TABLES - 1)),
                [nd["parts", t], nd.get(("sumT", t - 2))] + edges_done)

    def node_sumT(t):
        nd["sumT", t] = na(lambda e: e.copy(sumT[:, t % 2, :], ps_t[t % 2][:, 0:P]),
                           [nd["sum", t], nd.get(("proj", t - 2))] + edges_done)

    def node_diag(t):
        nd["diag", t] = na(lambda e: e.activation(diag[:, t % 2, :], ident, ACT.Copy, scale=count[:, t:t + 1]),
                           [nd["counted", t], nd.get(("proj", t - 2))] + edges_done)

    def node_project(t):
        npe(lambda e: e.matmul(ps_s[t % 2][:, 0:DIM], sumT[:, t % 2, :], wsum, start=True, stop=False),
            [nd["sumT", t], nd.get(("projected", t - 2))])
        nd["proj", t] = npe(lambda e: e.matmul(ps_s[t % 2][:, 0:DIM], diag[:, t % 2, :], vec["b_sum"], start=False, stop=True),
                            [nd["diag", t]])

    def node_state(t):
        st = state[:, t, :]
        nd["state", t] = nd["projected", t] = nv(lambda e: e.tensor_tensor(st, st, ps_s[t % 2][:, 0:DIM], ALU.add),
                                [nd["proj", t], nd["zout", t]])

    def node_stats(t):
        nd["bn", t] = nv(lambda e: e.bn_stats(stats[:, t % 2, :], state[:, t, :]), [nd["state", t], nd.get(("stat", t - 2))])

    def node_stat(t):
        nd["stat", t] = nv(lambda e: e.bn_aggr(mv2[:, t, :], stats[:, t % 2, :]), [nd["bn", t]])

    def node_sd(t):
        one = slice(t, t + 1)
        nd["sd", t] = na(lambda e: e.activation(r1[:, one], mv2[:, t, 1:2], ACT.Sqrt, bias=eps_t), [nd["stat", t]])

    def node_rstd(t):
        one = slice(t, t + 1)
        nd["rstd", t] = nv(lambda e: e.reciprocal(r1[:, one], r1[:, one]), [nd["sd", t]])

    def node_norm(t):
        one, r = slice(t, t + 1), t % YR
        nd["y", t] = nv(lambda e: e.tensor_scalar(y[:, r, :], state[:, t, :], mv2[:, t, 0:1], r1[:, one], ALU.subtract, ALU.mult),
                        [nd["rstd", t], nd.get(("lo", t - YR)), nd.get(("turn", t - YR))] + edges_done)
        nd["var", t] = nv(lambda e: e.tensor_scalar(r2[:, one], r1[:, one], r1[:, one], mv2[:, t, 1:2], ALU.mult, ALU.mult))

    def node_turn(t):
        one, r = slice(t, t + 1), t % YR
        nd["sd2", t] = na(lambda e: e.activation(r2[:, one], r2[:, one], ACT.Sqrt, bias=eps_s, scale=XSCALE ** -2), [nd["var", t]])
        for k in range(KC):
            nd["turn", t] = npe(lambda e, k=k: e.transpose(
                ps_y[t % 2][:, k * P:(k + 1) * P], y[:, r, k * P:(k + 1) * P], ident), [nd["y", t], nd.get(("yT", t - 2))])

    def node_second(t):
        one = slice(t, t + 1)
        nd["r2", t] = nv(lambda e: e.reciprocal(r2[:, one], r2[:, one]), [nd["sd2", t]])
        nd["yT", t] = na(lambda e: e.copy(yT[:, t % 2, :], ps_y[t % 2][:, 0:DIM]), [nd["turn", t], nd.get(("logit", t - 2))])

    def node_high(t):
        nd["hi", t] = na(lambda e: e.activation(xh[:, t % HR, 0, :], y[:, t % YR, :], ACT.Copy, scale=r2[:, t:t + 1]),
                         [nd["r2", t], nd.get(("stored", t - HR))])
        for k in range(KC):
            nd["logit", t] = npe(lambda e, k=k: e.matmul(
                ps_log[:, t * EXPERTS:(t + 1) * EXPERTS], yT[:, t % 2, k * P:(k + 1) * P],
                wr_t[:, k, :], start=(k == 0), stop=(k == KC - 1)), [nd["yT", t]])

    def node_low(t):
        nd["lo", t] = nv(lambda e: e.scalar_tensor_tensor(
            xh[:, t % HR, 1, :], y[:, t % YR, :], r2[:, t:t + 1], xh[:, t % HR, 0, :], ALU.mult, ALU.subtract), [nd["hi", t]])
        n = rows_of(t)
        nd["stored", t] = q.do("sync", xs_l[t % HR], lambda e: e.dma_start(
            xn_rows[t * P:t * P + n, :], xh[0:n, t % HR].rearrange("p i n -> p (i n)")), [nd["lo", t]])

    def both_of(f, g):
        return lambda t: (f(t), g(t))

    for _ in q.skewed(TILES, 1, [node_load, idle, idle, (node_count, node_degree), node_sum, both_of(node_sumT, node_diag),
                                 node_project, node_state, (node_stats, node_stat), node_sd, (node_rstd, node_norm),
                                 node_turn, node_second, node_high, node_low]):
        pass

    for t in range(0, TILES, 7):
        n = min(7, TILES - 1 - t)
        q.do("sync", ys_l, lambda e, t=t, n=n: e.dma_start(
            y_rows[t * P:(t + n) * P, :].rearrange("(t p) n -> p t n", p=P), state[:, t:t + n, :]), [nd["state", t + n - 1]])
    q.do("sync", ys_l, lambda e: e.dma_start(y_rows[(TILES - 1) * P:NODES, :], state[0:LAST, TILES - 1, :]), [nd["state", TILES - 1]])

    v_r, a_r, pe_r = line("route_dve"), line("route_act"), line("route_pe")
    at[0] = 0
    N8 = TILES * EXPERTS
    nodes_done = [Mark(l.sem, l.count) for l in (v_n, a_n, pe_n)]
    rows_stored = [nd["stored", t] for t in range(TILES - HR, TILES)]
    logit, hot1, hot2, tmp, cums, cums2 = (part(N8).rearrange("p (t e) -> p t e", e=EXPERTS) for _ in range(6))
    chosen = part(N8 // 2).bitcast(BF16).rearrange("p (t e) -> p t e", e=EXPERTS)
    rank = part(EXPERTS)
    share_, run1, run2 = (part(2 * EXPERTS).rearrange("p (a e) -> p a e", a=2) for _ in range(3))
    share_i = part(2 * EXPERTS).bitcast(I32).rearrange("p (a e) -> p a e", a=2)
    ends = part(2 * EXPERTS).rearrange("p (a e) -> p a e", a=2)
    singles = part(1)
    first, paired, jump = (part(EXPERTS) for _ in range(3))
    cnt_i = part(EXPERTS).bitcast(I32)
    top1, top2, wt1, wt2, num = (part(TILES) for _ in range(5))
    pos, p_hi, p_lo = (part(2 * TILES) for _ in range(3))
    pos_i, hi_i = (part(2 * TILES).bitcast(I32) for _ in range(2))
    valid = part(1)
    spare1 = part(1)
    MG, MR = 7, 8
    lo_flat = part(2 * MG * P)
    lo_hot = lo_flat.rearrange("p (r g n) -> p r g n", r=2, g=MG)
    lo_w = part(MR * P).rearrange("p (r n) -> p r n", r=MR)
    hi_hot = part(MR * STILES).rearrange("p (r n) -> p r n", r=MR)
    slot_tok = sb("slot_tok", [P, STILES], I32)
    slot_w = sb("slot_w", [P, STILES])
    slot_f = part(STILES)
    empty = part(STILES)
    block_tile = part(BLOCKS)
    passed = lo_flat[:, 0:BLOCKS * 2 * EXPERTS].rearrange("p (b e) -> p b e", b=BLOCKS)
    owner = part(BLOCKS)
    owner_i = sb("owner_i", [P, BLOCKS], I32)

    chainm = [None]

    def rv(fn, after=()):
        chainm[0] = q.do("vector", v_r, fn, [chainm[0], *after])
        return chainm[0]

    def b8(v):
        return v.unsqueeze(2).to_broadcast([P, TILES, EXPERTS])

    def over_tiles(v):
        return v.unsqueeze(1).to_broadcast([P, TILES, EXPERTS])

    rv(lambda e: e.tensor_tensor(logit, ps_log[:, 0:N8].rearrange("p (t e) -> p t e", e=EXPERTS), over_tiles(br_t), ALU.add),
       nodes_done)
    rv(lambda e: e.tensor_scalar(spare1, spare, 1.0, None, ALU.add))
    rv(lambda e: e.tensor_scalar(rank, iota[:, 0:EXPERTS], -1.0, float(EXPERTS), ALU.mult, ALU.add))
    rv(lambda e: e.tensor_scalar(valid, lane, float(LAST), None, ALU.is_lt))

    def pick(top, hot):
        rv(lambda e: e.reduce_max(top, logit, AX.X))
        rv(lambda e: e.tensor_tensor(tmp, logit, b8(top), ALU.is_equal))
        rv(lambda e: e.tensor_tensor(tmp, tmp, over_tiles(rank), ALU.mult))
        rv(lambda e: e.reduce_max(num, tmp, AX.X))
        rv(lambda e: e.tensor_tensor(hot, tmp, b8(num), ALU.is_equal))

    pick(top1, hot1)
    rv(lambda e: e.scalar_tensor_tensor(logit, hot1, -3.0e38, logit, ALU.mult, ALU.add))
    pick(top2, hot2)
    m = rv(lambda e: e.tensor_tensor(wt2, top2, top1, ALU.subtract))
    m_exp = q.do("scalar", a_r, lambda e: e.activation(wt2, wt2, ACT.Exp), [m])
    for h in (hot1, hot2):
        rv(lambda e, h=h: e.tensor_scalar(h[:, TILES - 1, :], h[:, TILES - 1, :], valid, None, ALU.mult))
    m = rv(lambda e: e.tensor_tensor(chosen, hot1, hot2, ALU.add))
    flat_t = chosen.rearrange("p t e -> p (t e)")
    q.do("tensor", pe_r, lambda e: e.matmul(banks[0][:, 0:N8], before, flat_t, start=True, stop=True), [m])
    m = q.do("tensor", pe_r, lambda e: e.matmul(banks[1][:, 0:N8], onesb, flat_t, start=True, stop=True), [m])
    rv(lambda e: e.tensor_scalar(wt1, wt2, 1.0, None, ALU.add), [m_exp])
    rv(lambda e: e.reciprocal(wt1, wt1))
    rv(lambda e: e.tensor_tensor(wt2, wt2, wt1, ALU.mult))
    for w in (wt1, wt2):
        rv(lambda e, w=w: e.tensor_scalar(w[:, TILES - 1:TILES], w[:, TILES - 1:TILES], valid, None, ALU.mult))
    rv(lambda e: e.tensor_scalar(num, iota[:, 0:TILES], float(P), 1.0, ALU.mult, ALU.add))
    rv(lambda e: e.tensor_scalar(num, num, lane, None, ALU.add))
    rv(lambda e: e.tensor_scalar(num[:, TILES - 1:TILES], num[:, TILES - 1:TILES], valid, None, ALU.mult))
    rv(lambda e: e.tensor_copy(cums.rearrange("p t e -> p (t e)"), banks[1][:, 0:N8]), [m])
    a, b, d = cums, cums2, 1
    while d < TILES:
        rv(lambda e, a=a, b=b, d=d: e.tensor_copy(b[:, 0:d, :], a[:, 0:d, :]))
        rv(lambda e, a=a, b=b, d=d: e.tensor_tensor(b[:, d:TILES, :], a[:, d:TILES, :], a[:, 0:TILES - d, :], ALU.add))
        a, b, d = b, a, 2 * d
    shift = P.bit_length() - 1
    rv(lambda e, a=a: e.tensor_scalar(cnt_i, a[:, TILES - 1, :], float(P - 1), None, ALU.add))
    rv(lambda e: e.tensor_scalar(share_i[:, 0, :], cnt_i, shift + 1, None, ALU.arith_shift_right))
    rv(lambda e: e.tensor_scalar(share_i[:, 1, :], cnt_i, shift, 1, ALU.arith_shift_right, ALU.bitwise_and))
    rv(lambda e: e.tensor_copy(share_, share_i))
    c, f, d = share_, run1, 1
    while d < EXPERTS:
        rv(lambda e, c=c, f=f, d=d: e.tensor_copy(f[:, :, 0:d], c[:, :, 0:d]))
        rv(lambda e, c=c, f=f, d=d: e.tensor_tensor(f[:, :, d:EXPERTS], c[:, :, d:EXPERTS], c[:, :, 0:EXPERTS - d], ALU.add))
        c, f, d = f, (run2 if f is run1 else run1), 2 * d
    rv(lambda e, c=c: e.tensor_scalar(ends[:, 0, :], c[:, 0, :], 2.0, None, ALU.mult))
    rv(lambda e: e.tensor_scalar(singles, ends[:, 0, EXPERTS - 1:EXPERTS], float(2 * FULL), None, ALU.max))
    rv(lambda e, c=c: e.tensor_scalar(ends[:, 1, :], c[:, 1, :], singles, None, ALU.add))
    rv(lambda e, c=c: e.tensor_tensor(first, c[:, 0, :], share_[:, 0, :], ALU.subtract))
    rv(lambda e: e.tensor_scalar(first, first, float(2 * P), None, ALU.mult))
    rv(lambda e: e.tensor_scalar(paired, share_[:, 0, :], float(2 * P), None, ALU.mult))
    rv(lambda e: e.tensor_tensor(jump, ends[:, 1, :], share_[:, 1, :], ALU.subtract))
    rv(lambda e: e.tensor_tensor(jump, jump, ends[:, 0, :], ALU.subtract))
    rv(lambda e: e.tensor_scalar(jump, jump, float(P), None, ALU.mult))
    rv(lambda e: e.tensor_scalar(block_tile[:, 0:FULL], iota[:, 0:FULL], 2.0, None, ALU.mult), rows_stored)
    rv(lambda e: e.tensor_scalar(block_tile[:, FULL:BLOCKS], iota[:, 0:BLOCKS - FULL], float(2 * FULL), None, ALU.add))
    rv(lambda e: e.tensor_tensor(
        passed, block_tile.unsqueeze(2).to_broadcast([P, BLOCKS, 2 * EXPERTS]),
        ends.rearrange("p a e -> p (a e)").unsqueeze(1).to_broadcast([P, BLOCKS, 2 * EXPERTS]), ALU.is_ge))
    rv(lambda e: e.reduce_sum(owner, passed, AX.X))
    rv(lambda e: e.tensor_copy(owner_i, owner))
    m_owner = rv(lambda e: e.tensor_scalar(owner_i, owner_i, EXPERTS - 1, None, ALU.bitwise_and))
    rv(lambda e, a=a, b=b: e.tensor_tensor(b, a, banks[1][:, 0:N8].rearrange("p (t e) -> p t e", e=EXPERTS), ALU.subtract))
    rv(lambda e, b=b: e.tensor_tensor(b, b, banks[0][:, 0:N8].rearrange("p (t e) -> p t e", e=EXPERTS), ALU.add))
    rv(lambda e, b=b: e.tensor_tensor(tmp, b, over_tiles(paired), ALU.is_ge))
    rv(lambda e: e.tensor_tensor(tmp, tmp, over_tiles(jump), ALU.mult))
    rv(lambda e, b=b: e.tensor_tensor(b, b, over_tiles(first), ALU.add))
    rv(lambda e, b=b: e.tensor_tensor(b, b, tmp, ALU.add))
    for k, h in enumerate((hot1, hot2)):
        rv(lambda e, h=h, b=b: e.tensor_tensor(tmp, h, b, ALU.mult))
        rv(lambda e, k=k: e.reduce_sum(pos[:, k * TILES:(k + 1) * TILES], tmp, AX.X))
    rv(lambda e: e.tensor_copy(pos_i, pos))
    rv(lambda e: e.tensor_scalar(hi_i, pos_i, 7, None, ALU.arith_shift_right))
    rv(lambda e: e.tensor_scalar(pos_i, pos_i, 127, None, ALU.bitwise_and))
    rv(lambda e: e.tensor_copy(p_lo, pos_i))
    m_pos = rv(lambda e: e.tensor_copy(p_hi, hi_i))

    mapped, weighed = {}, {}
    for g in range(0, 2 * TILES, MG):
        u = g // MG % 2
        m_lo = q.do("vector", v_r, lambda e, g=g, u=u: e.tensor_tensor(
            lo_hot[:, u], iota.unsqueeze(1).to_broadcast([P, MG, P]),
            p_lo[:, g:g + MG].unsqueeze(2).to_broadcast([P, MG, P]), ALU.is_equal),
            [m_pos, mapped.get(g - MG - 1), weighed.get(g - MG - 1)])
        for n in range(g, g + MG):
            k, t, r = n // TILES, n % TILES, n % MR
            w = (wt1, wt2)[k]
            weighed[n] = q.do("scalar", a_r, lambda e, n=n, g=g, u=u, r=r, t=t, w=w: e.activation(
                lo_w[:, r, :], lo_hot[:, u, n - g, :], ACT.Copy, scale=w[:, t:t + 1]), [m_lo, mapped.get(n - MR)])
            m = q.do("vector", v_r, lambda e, n=n, r=r, t=t: e.tensor_scalar(
                hi_hot[:, r, :], iota[:, 0:STILES], p_hi[:, n:n + 1], num[:, t:t + 1], ALU.is_equal, ALU.mult),
                [m_pos, mapped.get(n - MR)])
            q.do("tensor", pe_r, lambda e, n=n, g=g, u=u, r=r: e.matmul(
                banks[2][:, 0:STILES], lo_hot[:, u, n - g, :], hi_hot[:, r, :], start=(n == 0), stop=(n == 2 * TILES - 1)),
                [m_lo, m])
            mapped[n] = q.do("tensor", pe_r, lambda e, n=n, r=r: e.matmul(
                banks[3][:, 0:STILES], lo_w[:, r, :], hi_hot[:, r, :], start=(n == 0), stop=(n == 2 * TILES - 1)),
                [weighed[n]])
    chainm[0] = Mark(v_r.sem, v_r.count)
    rv(lambda e: e.tensor_scalar(empty, banks[2][:, 0:STILES], 0.5, None, ALU.is_lt), [mapped[2 * TILES - 1]])
    rv(lambda e: e.tensor_scalar(empty, empty, spare1, -1.0, ALU.mult, ALU.add))
    m_slots = rv(lambda e: e.tensor_tensor(slot_tok, empty, banks[2][:, 0:STILES], ALU.add))
    rv(lambda e: e.tensor_scalar(slot_f, banks[2][:, 0:STILES], 1.0, None, ALU.max))
    rv(lambda e: e.reciprocal(slot_f, slot_f))
    m_weights = rv(lambda e: e.tensor_tensor(slot_w, slot_f, banks[3][:, 0:STILES], ALU.mult))

    slab_at = [0]

    def slab(n):
        slab_at[0] += n
        return big[:, slab_at[0] - n:slab_at[0]]

    W1r = slab(2 * WN).bitcast(F16).rearrange("p (r i k n) -> p r i k n", r=2, i=2, k=KC)
    W2r = slab(2 * WN).bitcast(F16).rearrange("p (r i h n) -> p r i h n", r=2, i=2, h=HC)
    hT = slab(2 * HC * SLOT).bitcast(F16).rearrange("p (r i h n) -> p r i h n", r=2, i=2, h=HC)
    at[0] = 0
    routed = [m_slots, m_owner, Mark(pe_r.sem, pe_r.count)]
    XG = 4
    edge_mem = X.rearrange("p a b c -> p (a b c)")
    xg = edge_mem[:, 0:XG * 2 * DIM].bitcast(F16).rearrange("p (r s i k n) -> p r s i k n", r=XG, s=2, i=2, k=KC)
    xT = edge_mem[:, XG * 2 * DIM:(XG + 2) * 2 * DIM].bitcast(F16).rearrange("p (r i k n) -> p r i k n", r=2, i=2, k=KC)
    yo = part(2 * 2 * DIM).rearrange("p (r h n) -> p r h n", r=2, h=2)
    h32 = part(HC * SLOT).rearrange("p (h n) -> p h n", h=HC)
    NM = 3
    m_r = sb("m_r", [P, NM, META])
    b2r = sb("b2r", [P, NM, DIM])
    w1_l, w2_l, ml, gl, ad = lines("w1_load", 2), lines("w2_load", 2), lines("meta_load", NM), lines("gather", 2 * XG), line("row_add", 16)
    a_x, v_x2, pe_x = line("expert_act"), line("expert_dve"), line("expert_pe")
    ps_x, ps_h, ps_o = banks[0].bitcast(F16), banks[1:5], banks[5:7]
    ex = {}
    y_stored = [Mark(ys_l.sem, ys_l.count), m_pad]
    xn_stored = [nd["stored", t] for t in range(TILES - HR, TILES)] + [m_pad]
    blocks_ = []
    for c in range(FULL):
        blocks_.append((c, (2 * c, 2 * c + 1)))
        if (c + 1) % SPREAD == 0 and FULL + (c + 1) // SPREAD <= BLOCKS:
            i = (c + 1) // SPREAD - 1
            blocks_.append((FULL + i, (2 * FULL + i,)))
    assert len(blocks_) == BLOCKS
    THREE = ((0, 0), (0, 1), (1, 0))

    def slots_of(j):
        return slice(0, len(blocks_[j][1]) * P)

    def block_load(j):
        if j >= BLOCKS:
            return
        r, c = j % 2, blocks_[j][0]
        where = {}

        def first(e):
            where["v"] = e.value_load(owner_i[0:1, c:c + 1], min_val=0, max_val=EXPERTS - 1)
            return e.dma_start(W1r[:, r].rearrange("p i k n -> p (i k n)"),
                               w_parts[0][bass.ds(where["v"], 1)].rearrange("o p n -> p (o n)"))

        ex["w1", j] = q.do("sync", w1_l[r], first, [m_owner] + nodes_done + done["weights"] + [ex.get(("up", j - 2))])
        q.do("sync", ml[j % NM], lambda e: e.dma_start(
            m_r[:, j % NM, :], meta[bass.ds(where["v"], 1)].rearrange("o p n -> p (o n)")),
            [ex.get(("o", j - NM)), ex.get(("g", j - NM, HC - 1)), ex.get(("lo", j - NM, HC // 2 - 1))])
        ex["m", j] = q.do("sync", ml[j % NM], lambda e: e.dma_start(
            b2r[:, j % NM, :], b2[bass.ds(where["v"], 1)].rearrange("o n -> (o n)").partition_broadcast(P)))
        ex["w2", j] = q.do("sync", w2_l[r], lambda e: e.dma_start(
            W2r[:, r].rearrange("p i h n -> p (i h n)"), w_parts[1][bass.ds(where["v"], 1)].rearrange("o p n -> p (o n)")),
            [ex.get(("down", j - 2))])

    def block_gather(j):
        if j >= BLOCKS:
            return
        for h, s in enumerate(blocks_[j][1]):
            l = gl[(j % XG) * 2 + h]
            ex["g", j, "rows", h] = q.do("gpsimd", l, lambda e, h=h, s=s: e.indirect_dma_start(
                xg[:, j % XG, h].rearrange("p i k n -> p (i k n)"), None, xn_rows,
                bass.IndirectOffsetOnAxis(ap=slot_tok[:, s:s + 1], axis=0), bounds_check=ROWS - 1, oob_is_err=True),
                routed + xn_stored + [ex.get(("T", j - XG))])

    def block_turn(j):
        if j >= BLOCKS:
            return
        for i in range(2):
            for k in range(KC):
                for h in range(len(blocks_[j][1])):
                    c = (i * KC + k) * SLOT + h * P
                    m = q.do("tensor", pe_x, lambda e, i=i, k=k, h=h, c=c: e.transpose(
                        ps_x[:, c:c + P], xg[:, j % XG, h, i, k, :], identh),
                        [ex["g", j, "rows", 0], ex.get(("g", j, "rows", 1)), ex.get(("xT", j - 1))] + routed)
        ex["T", j] = m
        w = slots_of(j)
        ex["xT", j] = q.do("vector", v_x2, lambda e: e.tensor_copy(
            xT[:, j % 2].rearrange("p i k n -> p (i k) n")[:, :, w], ps_x.rearrange("p (a n) -> p a n", n=SLOT)[:, :, w]), [m, ex.get(("up", j - 2))])

    def block_up(j):
        if j >= BLOCKS:
            return
        r, n, w = j % 2, j % NM, slots_of(j)
        for h in range(HC):
            ps = ps_h[h % 4][:, w]
            steps = [(a, b, k) for k in range(KC) for a, b in THREE]
            for s, (a, b, k) in enumerate(steps):
                m = q.do("tensor", pe_x, lambda e, a=a, b=b, k=k, h=h, ps=ps, s=s: e.matmul(
                    ps, W1r[:, r, a, k, h * P:(h + 1) * P], xT[:, r, b, k, w], start=(s == 0), stop=(s == len(steps) - 1)),
                    [ex["w1", j], ex["xT", j], ex.get(("g", j, h - 4)) if h >= 4 else ex.get(("g", j - 1, h + 4))])
            ex["g", j, h] = q.do("scalar", a_x, lambda e, h=h, ps=ps: e.activation(
                h32[:, h, w], ps, ACT.Gelu, bias=m_r[:, n, h:h + 1], scale=m_r[:, n, HC:HC + 1]),
                [m, ex["m", j], ex.get(("lo", j - 1, h // 2))])
            if h % 2:
                pair = slice(h - 1, h + 1)
                hs = h32[:, pair, w]
                parts_ = [hT[:, r, i, pair, w] for i in range(2)]
                m = q.do("vector", v_x2, lambda e, hs=hs, o_=parts_[0]: e.tensor_scalar(
                    o_, hs, m_r[:, n, HC + 1:HC + 2], None, ALU.mult), [ex["g", j, h], ex["m", j], ex.get(("down", j - 2))])
                ex["lo", j, h // 2] = q.do("vector", v_x2, lambda e, hs=hs, p_=parts_: e.scalar_tensor_tensor(
                    p_[1], hs, m_r[:, n, HC + 1:HC + 2], p_[0], ALU.mult, ALU.subtract), [m])
        ex["up", j] = Mark(pe_x.sem, pe_x.count)

    def block_down(j):
        r, n = j % 2, j % NM
        for s, tile in enumerate(blocks_[j][1]):
            ps = ps_o[s][:, 0:DIM]
            steps = [(a, b, h) for h in range(HC) for a, b in THREE]
            for i, (a, b, h) in enumerate(steps):
                m = q.do("tensor", pe_x, lambda e, a=a, b=b, h=h, s=s, ps=ps, i=i: e.matmul(
                    ps, hT[:, r, a, h, s * P:(s + 1) * P], W2r[:, r, b, h, :], start=(i == 0), stop=(i == len(steps) - 1)),
                    [ex["lo", j, h // 2], ex["w2", j], ex.get(("o", j - 1))])
            ex["down", j] = m
            m = q.do("vector", v_x2, lambda e, s=s, ps=ps: e.scalar_tensor_tensor(
                yo[:, r, s, :], ps, m_r[:, n, HC + 2:HC + 3], b2r[:, n, :], ALU.mult, ALU.add),
                [m, ex["m", j], ex.get(("add", j - 2)), m_weights] + routed)
            m = q.do("vector", v_x2, lambda e, s=s, tile=tile: e.tensor_scalar(
                yo[:, r, s, :], yo[:, r, s, :], slot_w[:, tile:tile + 1], None, ALU.mult), [m])
            ex["o", j] = m
            ex["add", j] = q.do("gpsimd", ad, lambda e, s=s, tile=tile: e.indirect_dma_start(
                y_rows, bass.IndirectOffsetOnAxis(ap=slot_tok[:, tile:tile + 1], axis=0), yo[:, r, s, :], None,
                compute_op=ALU.add, bounds_check=ROWS - 1, oob_is_err=True),
                [m, Mark(ad.sem, ad.count) if ad.count else None] + y_stored)

    for j in range(2):
        block_load(j)
    for j in range(XG - 1):
        block_gather(j)
    block_turn(0)
    block_turn(1)
    block_up(0)
    for j in range(BLOCKS):
        block_gather(j + XG - 1)
        block_up(j + 1)
        block_turn(j + 2)
        block_down(j)
        block_load(j + 2)

    q.wait("gpsimd", [ex["add", BLOCKS - 1]])

    with ctx:
        block = ctx.enter_context(nc.Block())

        @block.tensor
        def _(e):
            q.play("tensor", e)

        @block.vector
        def _(e):
            q.play("vector", e)

        @block.scalar
        def _(e):
            q.play("scalar", e)

        @block.gpsimd
        def _(e):
            q.play("gpsimd", e)

        @block.sync
        def _(e):
            q.play("sync", e)


INPUTS = ["x", "src", "dst", "edge_attr_128", "node_vec1", "node_vec1_n2", "L0_gnn_z_in", "L0_gnn_z_out",
          "L0_gnn_W_cent", "L0_gnn_b_cent", "L0_gnn_W_vor", "L0_gnn_b_vor", "L0_gnn_W_sum", "L0_gnn_b_sum",
          "L0_mix_w_qkv", "L0_mix_w_out", "L0_mix_b_out", "L0_ffn_Wr", "L0_ffn_br", "L0_ffn_ln_g", "L0_ffn_ln_b",
          "L0_ffn_W1", "L0_ffn_b1", "L0_ffn_W2", "L0_ffn_b2"]


def kernel(**inputs):
    import concourse.bacc as bacc
    from concourse.bass_utils import run_bass_kernel_spmd

    nc = bacc.Bacc("TRN2", target_bir_lowering=False, num_devices=1)
    arrays, args = {}, []
    for name in INPUTS:
        a = np.ascontiguousarray(inputs[name])
        arrays[name] = a
        args.append(nc.dram_tensor(name, a.shape, mybir.dt.from_np(a.dtype), kind="ExternalInput").ap())
    result = nc.dram_tensor("result", (ROWS, DIM), F32, kind="ExternalOutput").ap()
    build_layer(nc, *args, result)
    r = run_bass_kernel_spmd(nc, [arrays], core_ids=[0])
    return r.results[0]["result"][0:NODES]
```
